# Optimizing a Trainium2 kernel written in Bass

```python
import numpy as np
import jax
import jax.numpy as jnp

def _softmax(x, axis=-1):
    return jax.nn.softmax(x, axis=axis)

def _gelu(x):
    return jax.nn.gelu(x, approximate=True)

def _silu(x):
    return jax.nn.silu(x)

def _sigmoid(x):
    return jax.nn.sigmoid(x)

def _layernorm(x, axis=-1, eps=1e-05):
    m = jnp.mean(x, axis=axis, keepdims=True)
    v = jnp.var(x, axis=axis, keepdims=True)
    return (x - m) / jnp.sqrt(v + eps)

def _scatter_add(tgt, idx, src, axis=0):
    return tgt.at[idx].add(src)

def _segment_sum(src, seg, n):
    return jax.ops.segment_sum(src, seg, n)
kernel_name = 'mk_lm_tower_d2_tok_ids2048_r4_cb4768'

def setup_inputs(seed: int=0):
    np.random.seed(seed)
    _w = jnp.asarray

    def _rec_inputs():
        import jax
        import jax.numpy as jnp
        _rk = jax.random.key(seed)
        x = jax.random.randint(jax.random.fold_in(_rk, 1), (16, 128), 0, 32000, jnp.int32)
        return x
    x = _rec_inputs()

    def _L0_tok_setup():
        import jax, jax.numpy as jnp
        import numpy as np
        VOCAB = 32000
        DIM = 512
        B, S = (8, 1024)
        TOKEN_IDS = np.arange(31996, 32000)
        key = jax.random.key(seed)
        k1, k2, k3 = jax.random.split(key, 3)
        weight = jax.random.normal(k1, (VOCAB, DIM), dtype=jnp.float32) * 0.02
        extra = jax.random.normal(k2, (len(TOKEN_IDS), DIM), dtype=jnp.float32) * 0.02
        input_ids = jax.random.randint(k3, (B, S), 0, VOCAB, dtype=jnp.int32)
        input_ids = input_ids.at[:, :len(TOKEN_IDS)].set(jnp.asarray(TOKEN_IDS, dtype=jnp.int32)[None, :])
        return {'input_ids': input_ids, 'weight': weight, 'extra': extra}
    _L0_tok_all = _L0_tok_setup()
    _L0_tok_in = {k: v for k, v in _L0_tok_all.items() if k in ('weight', 'extra')}
    del _L0_tok_all

    def _L0_attn_setup():
        import jax, jax.numpy as jnp
        import numpy as np
        HIDDEN = 512
        N_HEADS = 16
        HEAD_DIM = HIDDEN // N_HEADS
        KV_DIM = HEAD_DIM
        INTER = 4 * HIDDEN
        EPS = 1e-05

        def _ln(x, g, b):
            m = jnp.mean(x, -1, keepdims=True)
            v = jnp.var(x, -1, keepdims=True)
            return (x - m) * jax.lax.rsqrt(v + EPS) * g + b

        def _block(x, ln1_g, ln1_b, ln2_g, ln2_b, wq, bq, wkv, bkv, wo, bo, wfc, bfc, wproj, bproj):
            B, S, H = x.shape
            scale = HEAD_DIM ** (-0.5)
            res = x
            h = _ln(x, ln1_g, ln1_b)
            q = (h @ wq + bq).reshape(B, S, N_HEADS, HEAD_DIM)
            kv = h @ wkv + bkv
            k, v = (kv[..., :KV_DIM], kv[..., KV_DIM:])
            scores = jnp.einsum('bshd,btd->bhst', q, k) * scale
            causal = jnp.tril(jnp.ones((S, S), bool))
            scores = jnp.where(causal, scores, jnp.finfo(scores.dtype).min)
            probs = jax.nn.softmax(scores, axis=-1)
            attn = jnp.einsum('bhst,btd->bshd', probs, v).reshape(B, S, H)
            x = attn @ wo + bo + res
            res = x
            h = _ln(x, ln2_g, ln2_b)
            h = jax.nn.gelu(h @ wfc + bfc, approximate=True)
            return h @ wproj + bproj + res
        key = jax.random.key(seed)
        ks = jax.random.split(key, 16)
        s = 0.02
        d = dict(hidden_states=jax.random.normal(ks[0], (4, 512, HIDDEN), jnp.float32), ln1_g=jnp.ones((HIDDEN,), jnp.float32), ln1_b=jnp.zeros((HIDDEN,), jnp.float32), ln2_g=jnp.ones((HIDDEN,), jnp.float32), ln2_b=jnp.zeros((HIDDEN,), jnp.float32), wq=jax.random.normal(ks[1], (HIDDEN, HIDDEN), jnp.float32) * s, bq=jnp.zeros((HIDDEN,), jnp.float32), wkv=jax.random.normal(ks[2], (HIDDEN, 2 * KV_DIM), jnp.float32) * s, bkv=jnp.zeros((2 * KV_DIM,), jnp.float32), wo=jax.random.normal(ks[3], (HIDDEN, HIDDEN), jnp.float32) * s, bo=jnp.zeros((HIDDEN,), jnp.float32), wfc=jax.random.normal(ks[4], (HIDDEN, INTER), jnp.float32) * s, bfc=jnp.zeros((INTER,), jnp.float32), wproj=jax.random.normal(ks[5], (INTER, HIDDEN), jnp.float32) * s, bproj=jnp.zeros((HIDDEN,), jnp.float32))
        return d
    _L0_attn_all = _L0_attn_setup()
    _L0_attn_in = {k: v for k, v in _L0_attn_all.items() if k in ('ln1_g', 'ln1_b', 'ln2_g', 'ln2_b', 'wq', 'bq', 'wkv', 'bkv', 'wo', 'bo', 'wfc', 'bfc', 'wproj', 'bproj')}
    del _L0_attn_all

    def _L0_ffn_setup():
        import jax, jax.numpy as jnp
        import numpy as np
        DIM = 512
        INTER = 352
        E = 16
        TOPK = 4
        G = 4
        TOPK_G = 2
        N_SHARED = 2
        SHARED_INTER = N_SHARED * INTER
        ROUTE_SCALE = 1.0

        def _moe_forward(x, Wg, W1, W3, W2, Ws1, Ws3, Ws2):
            B, S, D = x.shape
            xt = x.reshape(-1, D)
            T = xt.shape[0]
            scores = jax.nn.softmax(xt @ Wg.T, axis=-1)
            sg = scores.reshape(T, G, E // G)
            group_scores = sg.max(axis=-1)
            gidx = jax.lax.top_k(group_scores, TOPK_G)[1]
            gmask = jax.nn.one_hot(gidx, G, dtype=jnp.float32).sum(axis=1) > 0
            masked = jnp.where(gmask[:, :, None], sg, -jnp.inf).reshape(T, E)
            topi = jax.lax.top_k(masked, TOPK)[1]
            weights = jnp.take_along_axis(scores, topi, axis=1) * ROUTE_SCALE
            combine = jnp.zeros((T, E), xt.dtype).at[jnp.arange(T)[:, None], topi].add(weights)
            h = jax.nn.silu(jnp.einsum('td,eid->eti', xt, W1)) * jnp.einsum('td,eid->eti', xt, W3)
            expert_out = jnp.einsum('eti,edi->etd', h, W2)
            y = jnp.einsum('etd,te->td', expert_out, combine)
            z = jax.nn.silu(xt @ Ws1.T) * (xt @ Ws3.T) @ Ws2.T
            return (y + z).reshape(B, S, D)
        key = jax.random.key(seed)
        ks = jax.random.split(key, 8)
        s = 0.02
        x = jax.random.normal(ks[0], (1, 512, DIM), dtype=jnp.float32)
        Wg = jax.random.normal(ks[1], (E, DIM), dtype=jnp.float32) * s
        W1 = jax.random.normal(ks[2], (E, INTER, DIM), dtype=jnp.float32) * s
        W3 = jax.random.normal(ks[3], (E, INTER, DIM), dtype=jnp.float32) * s
        W2 = jax.random.normal(ks[4], (E, DIM, INTER), dtype=jnp.float32) * s
        Ws1 = jax.random.normal(ks[5], (SHARED_INTER, DIM), dtype=jnp.float32) * s
        Ws3 = jax.random.normal(ks[6], (SHARED_INTER, DIM), dtype=jnp.float32) * s
        Ws2 = jax.random.normal(ks[7], (DIM, SHARED_INTER), dtype=jnp.float32) * s
        return {'x': x, 'Wg': Wg, 'W1': W1, 'W3': W3, 'W2': W2, 'Ws1': Ws1, 'Ws3': Ws3, 'Ws2': Ws2}
    _L0_ffn_all = _L0_ffn_setup()
    _L0_ffn_in = {k: v for k, v in _L0_ffn_all.items() if k in ('Wg', 'W1', 'W3', 'W2', 'Ws1', 'Ws3', 'Ws2')}
    del _L0_ffn_all

    def _L1_attn_setup():
        import jax, jax.numpy as jnp
        import numpy as np
        import math
        EMBED_DIM = 512
        HEAD_NUM = 2
        B, S = (2, 1024)
        key = jax.random.key(seed)
        ks = jax.random.split(key, 9)
        bf16 = jnp.bfloat16
        d = EMBED_DIM
        scale = 1.0 / math.sqrt(d)
        base = jax.random.normal(ks[0], (B, S, d), dtype=bf16)

        def lin(k):
            kw, kb = jax.random.split(k)
            W = jax.random.uniform(kw, (d, d), dtype=jnp.float32, minval=-scale, maxval=scale).astype(bf16)
            b = jax.random.uniform(kb, (d,), dtype=jnp.float32, minval=-scale, maxval=scale).astype(bf16)
            return (W, b)
        Wq, bq = lin(ks[1])
        Wk, bk = lin(ks[2])
        Wv, bv = lin(ks[3])
        Wo, bo = lin(ks[4])
        return {'base': base, 'Wq': Wq, 'bq': bq, 'Wk': Wk, 'bk': bk, 'Wv': Wv, 'bv': bv, 'Wo': Wo, 'bo': bo}
    _L1_attn_all = _L1_attn_setup()
    _L1_attn_in = {k: v for k, v in _L1_attn_all.items() if k in ('Wq', 'bq', 'Wk', 'bk', 'Wv', 'bv', 'Wo', 'bo')}
    del _L1_attn_all

    def _L1_ffn_setup():
        import jax, jax.numpy as jnp
        import numpy as np
        D = 512
        H_TOTAL = 2048
        E = 8
        K = 2
        HE = H_TOTAL // E
        B, S = (2, 512)
        key = jax.random.key(seed)
        ks = jax.random.split(key, 8)
        scale_up = 1.0 / np.sqrt(D)
        scale_dn = 1.0 / np.sqrt(HE)
        return {'x': jax.random.normal(ks[0], (B, S, D), dtype=jnp.float32), 'Wg1': jax.random.normal(ks[1], (E, D), dtype=jnp.float32) * 0.02, 'Wg2': jax.random.normal(ks[2], (E, E), dtype=jnp.float32) * 0.2, 'Wup': jax.random.uniform(ks[3], (E, HE, D), dtype=jnp.float32, minval=-scale_up, maxval=scale_up), 'bup': jax.random.uniform(ks[4], (E, HE), dtype=jnp.float32, minval=-scale_up, maxval=scale_up), 'Wdown': jax.random.uniform(ks[5], (E, D, HE), dtype=jnp.float32, minval=-scale_dn, maxval=scale_dn), 'bdown': jax.random.uniform(ks[6], (E, D), dtype=jnp.float32, minval=-scale_dn, maxval=scale_dn)}
    _L1_ffn_all = _L1_ffn_setup()
    _L1_ffn_in = {k: v for k, v in _L1_ffn_all.items() if k in ('Wg1', 'Wg2', 'Wup', 'bup', 'Wdown', 'bdown')}
    del _L1_ffn_all
    return {'x': x, 'L0_tok_weight': _L0_tok_in['weight'], 'L0_tok_extra': _L0_tok_in['extra'], 'L0_attn_ln1_g': _L0_attn_in['ln1_g'], 'L0_attn_ln1_b': _L0_attn_in['ln1_b'], 'L0_attn_ln2_g': _L0_attn_in['ln2_g'], 'L0_attn_ln2_b': _L0_attn_in['ln2_b'], 'L0_attn_wq': _L0_attn_in['wq'], 'L0_attn_bq': _L0_attn_in['bq'], 'L0_attn_wkv': _L0_attn_in['wkv'], 'L0_attn_bkv': _L0_attn_in['bkv'], 'L0_attn_wo': _L0_attn_in['wo'], 'L0_attn_bo': _L0_attn_in['bo'], 'L0_attn_wfc': _L0_attn_in['wfc'], 'L0_attn_bfc': _L0_attn_in['bfc'], 'L0_attn_wproj': _L0_attn_in['wproj'], 'L0_attn_bproj': _L0_attn_in['bproj'], 'L0_ffn_Wg': _L0_ffn_in['Wg'], 'L0_ffn_W1': _L0_ffn_in['W1'], 'L0_ffn_W3': _L0_ffn_in['W3'], 'L0_ffn_W2': _L0_ffn_in['W2'], 'L0_ffn_Ws1': _L0_ffn_in['Ws1'], 'L0_ffn_Ws3': _L0_ffn_in['Ws3'], 'L0_ffn_Ws2': _L0_ffn_in['Ws2'], 'L1_attn_Wq': _L1_attn_in['Wq'], 'L1_attn_bq': _L1_attn_in['bq'], 'L1_attn_Wk': _L1_attn_in['Wk'], 'L1_attn_bk': _L1_attn_in['bk'], 'L1_attn_Wv': _L1_attn_in['Wv'], 'L1_attn_bv': _L1_attn_in['bv'], 'L1_attn_Wo': _L1_attn_in['Wo'], 'L1_attn_bo': _L1_attn_in['bo'], 'L1_ffn_Wg1': _L1_ffn_in['Wg1'], 'L1_ffn_Wg2': _L1_ffn_in['Wg2'], 'L1_ffn_Wup': _L1_ffn_in['Wup'], 'L1_ffn_bup': _L1_ffn_in['bup'], 'L1_ffn_Wdown': _L1_ffn_in['Wdown'], 'L1_ffn_bdown': _L1_ffn_in['bdown']}

def reference(x, L0_tok_weight, L0_tok_extra, L0_attn_ln1_g, L0_attn_ln1_b, L0_attn_ln2_g, L0_attn_ln2_b, L0_attn_wq, L0_attn_bq, L0_attn_wkv, L0_attn_bkv, L0_attn_wo, L0_attn_bo, L0_attn_wfc, L0_attn_bfc, L0_attn_wproj, L0_attn_bproj, L0_ffn_Wg, L0_ffn_W1, L0_ffn_W3, L0_ffn_W2, L0_ffn_Ws1, L0_ffn_Ws3, L0_ffn_Ws2, L1_attn_Wq, L1_attn_bq, L1_attn_Wk, L1_attn_bk, L1_attn_Wv, L1_attn_bv, L1_attn_Wo, L1_attn_bo, L1_ffn_Wg1, L1_ffn_Wg2, L1_ffn_Wup, L1_ffn_bup, L1_ffn_Wdown, L1_ffn_bdown):
    import jax
    import jax.numpy as jnp

    def _L0_tok_ref(input_ids, weight, extra):
        import jax, jax.numpy as jnp
        import numpy as np
        VOCAB = 32000
        DIM = 512
        B, S = (8, 1024)
        TOKEN_IDS = np.arange(31996, 32000)
        n_over = extra.shape[0]
        over_idx = jnp.full((VOCAB,), -1, dtype=jnp.int32).at[jnp.asarray(TOKEN_IDS, dtype=jnp.int32)].set(jnp.arange(n_over, dtype=jnp.int32))
        oi = over_idx[input_ids]
        base = weight[input_ids]
        repl = extra[jnp.clip(oi, 0, n_over - 1)]
        return jnp.where((oi >= 0)[..., None], repl, base)

    def _L0_attn_ref(hidden_states, ln1_g, ln1_b, ln2_g, ln2_b, wq, bq, wkv, bkv, wo, bo, wfc, bfc, wproj, bproj):
        import jax, jax.numpy as jnp
        import numpy as np
        HIDDEN = 512
        N_HEADS = 16
        HEAD_DIM = HIDDEN // N_HEADS
        KV_DIM = HEAD_DIM
        INTER = 4 * HIDDEN
        EPS = 1e-05

        def _ln(x, g, b):
            m = jnp.mean(x, -1, keepdims=True)
            v = jnp.var(x, -1, keepdims=True)
            return (x - m) * jax.lax.rsqrt(v + EPS) * g + b

        def _block(x, ln1_g, ln1_b, ln2_g, ln2_b, wq, bq, wkv, bkv, wo, bo, wfc, bfc, wproj, bproj):
            B, S, H = x.shape
            scale = HEAD_DIM ** (-0.5)
            res = x
            h = _ln(x, ln1_g, ln1_b)
            q = (h @ wq + bq).reshape(B, S, N_HEADS, HEAD_DIM)
            kv = h @ wkv + bkv
            k, v = (kv[..., :KV_DIM], kv[..., KV_DIM:])
            scores = jnp.einsum('bshd,btd->bhst', q, k) * scale
            causal = jnp.tril(jnp.ones((S, S), bool))
            scores = jnp.where(causal, scores, jnp.finfo(scores.dtype).min)
            probs = jax.nn.softmax(scores, axis=-1)
            attn = jnp.einsum('bhst,btd->bshd', probs, v).reshape(B, S, H)
            x = attn @ wo + bo + res
            res = x
            h = _ln(x, ln2_g, ln2_b)
            h = jax.nn.gelu(h @ wfc + bfc, approximate=True)
            return h @ wproj + bproj + res
        return _block(hidden_states, ln1_g, ln1_b, ln2_g, ln2_b, wq, bq, wkv, bkv, wo, bo, wfc, bfc, wproj, bproj)

    def _L0_ffn_ref(x, Wg, W1, W3, W2, Ws1, Ws3, Ws2):
        import jax, jax.numpy as jnp
        import numpy as np
        DIM = 512
        INTER = 352
        E = 16
        TOPK = 4
        G = 4
        TOPK_G = 2
        N_SHARED = 2
        SHARED_INTER = N_SHARED * INTER
        ROUTE_SCALE = 1.0

        def _moe_forward(x, Wg, W1, W3, W2, Ws1, Ws3, Ws2):
            B, S, D = x.shape
            xt = x.reshape(-1, D)
            T = xt.shape[0]
            scores = jax.nn.softmax(xt @ Wg.T, axis=-1)
            sg = scores.reshape(T, G, E // G)
            group_scores = sg.max(axis=-1)
            gidx = jax.lax.top_k(group_scores, TOPK_G)[1]
            gmask = jax.nn.one_hot(gidx, G, dtype=jnp.float32).sum(axis=1) > 0
            masked = jnp.where(gmask[:, :, None], sg, -jnp.inf).reshape(T, E)
            topi = jax.lax.top_k(masked, TOPK)[1]
            weights = jnp.take_along_axis(scores, topi, axis=1) * ROUTE_SCALE
            combine = jnp.zeros((T, E), xt.dtype).at[jnp.arange(T)[:, None], topi].add(weights)
            h = jax.nn.silu(jnp.einsum('td,eid->eti', xt, W1)) * jnp.einsum('td,eid->eti', xt, W3)
            expert_out = jnp.einsum('eti,edi->etd', h, W2)
            y = jnp.einsum('etd,te->td', expert_out, combine)
            z = jax.nn.silu(xt @ Ws1.T) * (xt @ Ws3.T) @ Ws2.T
            return (y + z).reshape(B, S, D)
        return _moe_forward(x, Wg, W1, W3, W2, Ws1, Ws3, Ws2)

    def _L1_attn_ref(base, Wq, bq, Wk, bk, Wv, bv, Wo, bo):
        import jax, jax.numpy as jnp
        import numpy as np
        import math
        EMBED_DIM = 512
        HEAD_NUM = 2
        B, S = (2, 1024)
        H = HEAD_NUM
        b, s, d = base.shape
        hd = d // H
        relu = jax.nn.relu
        q = relu(base @ Wq.T + bq)
        k = relu(base @ Wk.T + bk)
        v = relu(base @ Wv.T + bv)

        def split_heads(x):
            return x.reshape(b, s, H, hd).transpose(0, 2, 1, 3)
        q, k, v = (split_heads(q), split_heads(k), split_heads(v))
        scale = 1.0 / math.sqrt(hd)
        scores = jnp.einsum('bhqd,bhkd->bhqk', q, k) * jnp.asarray(scale, q.dtype)
        attn = jax.nn.softmax(scores, axis=-1)
        y = jnp.einsum('bhqk,bhkd->bhqd', attn, v)
        y = y.transpose(0, 2, 1, 3).reshape(b, s, d)
        y = relu(y @ Wo.T + bo)
        return y.astype(base.dtype)

    def _L1_ffn_ref(x, Wg1, Wg2, Wup, bup, Wdown, bdown):
        import jax, jax.numpy as jnp
        import numpy as np
        D = 512
        H_TOTAL = 2048
        E = 8
        K = 2
        HE = H_TOTAL // E
        B, S = (2, 512)
        Bd, Sd, Dd = x.shape
        T = Bd * Sd
        xt = x.reshape(T, Dd)
        logits = jnp.tanh(xt @ Wg1.T) @ Wg2.T
        _, top_idx = jax.lax.top_k(logits, K)
        top_logits = jnp.take_along_axis(logits, top_idx, axis=1)
        top_scores = jax.nn.softmax(top_logits.astype(jnp.float32), axis=1).astype(logits.dtype)
        rows = jnp.arange(T)[:, None]
        scores = jnp.zeros_like(logits).at[rows, top_idx].set(top_scores)
        up = jnp.einsum('td,ehd->teh', xt, Wup) + bup
        h = jax.nn.silu(up)
        down = jnp.einsum('teh,eoh->teo', h, Wdown) + bdown
        out = jnp.einsum('te,teo->to', scores, down)
        return out.reshape(Bd, Sd, Dd)
    h = _L0_tok_ref(x, L0_tok_weight, L0_tok_extra)
    h = h + _L0_attn_ref(_layernorm(h, axis=-1), L0_attn_ln1_g, L0_attn_ln1_b, L0_attn_ln2_g, L0_attn_ln2_b, L0_attn_wq, L0_attn_bq, L0_attn_wkv, L0_attn_bkv, L0_attn_wo, L0_attn_bo, L0_attn_wfc, L0_attn_bfc, L0_attn_wproj, L0_attn_bproj)
    h = h + _L0_ffn_ref(_layernorm(h, axis=-1), L0_ffn_Wg, L0_ffn_W1, L0_ffn_W3, L0_ffn_W2, L0_ffn_Ws1, L0_ffn_Ws3, L0_ffn_Ws2)
    h = h + _L1_attn_ref(_layernorm(h, axis=-1), L1_attn_Wq, L1_attn_bq, L1_attn_Wk, L1_attn_bk, L1_attn_Wv, L1_attn_bv, L1_attn_Wo, L1_attn_bo)
    h = h + _L1_ffn_ref(_layernorm(h, axis=-1), L1_ffn_Wg1, L1_ffn_Wg2, L1_ffn_Wup, L1_ffn_bup, L1_ffn_Wdown, L1_ffn_bdown)
    return h

_drawn_inputs = setup_inputs


def setup_inputs(seed=0):
    import zlib

    import numpy as np

    out = dict(_drawn_inputs(seed))
    spreads = {'L0_attn_ln1_g': (1.0, 0.6),
     'L0_attn_ln1_b': (0.0, 0.1),
     'L0_attn_ln2_g': (1.0, 0.2),
     'L0_attn_ln2_b': (0.0, 0.1),
     'L0_attn_bq': (0.0, 0.8),
     'L0_attn_bkv': (0.0, 0.1),
     'L0_attn_bo': (0.0, 0.1),
     'L0_attn_bfc': (0.0, 0.1),
     'L0_attn_bproj': (0.0, 0.1)}
    factors = {'L0_attn_wq': 4.242,
     'L0_ffn_Wg': 4.692,
     'L0_ffn_W1': 4.156,
     'L0_ffn_W3': 4.589,
     'L0_ffn_W2': 4.242,
     'L1_attn_Wq': 8.0,
     'L1_attn_bq': 64.0,
     'L1_attn_Wk': 8.0,
     'L1_attn_bk': 64.0,
     'L1_attn_bv': 19.77,
     'L1_ffn_bup': 25.498,
     'L1_attn_bo': 6.923,
     'L1_ffn_bdown': 5.704}
    for name, (base, spread) in spreads.items():
        noise = np.random.default_rng([zlib.crc32(name.encode()), seed]).standard_normal(out[name].shape)
        drawn = base * np.exp(spread * noise) if base else spread * noise
        out[name] = jnp.asarray(drawn.astype(out[name].dtype))
    for name, factor in factors.items():
        out[name] = (out[name] * factor).astype(out[name].dtype)
    return out
```

```python
from contextlib import ExitStack, contextmanager

import concourse.bass as bass
from concourse import mybir
from concourse.alu_op_type import AluOpType as ALU

ACT = mybir.ActivationFunctionType
AX = mybir.AxisListType
F32 = mybir.dt.float32
F32R = mybir.dt.float32r
BF16 = mybir.dt.bfloat16
I32 = mybir.dt.int32
U32 = mybir.dt.uint32

P = 128
D = 512
KC = D // P
TILES = 16
GT = 4
GROUPS = TILES // GT
GN = GT * P
TOKENS = TILES * P
EPS = 1e-5

OVER_FIRST = 31996
HEADS, HD = 16, 32
QUADS = 4
UH = 8
UNITS = 2 * GT
ATT0_SCALE = HD ** -0.5
MASKED = -1e30
INTER = 2048
IC = INTER // P


FIRST = 1


class Steps:

    def __init__(self, engine, semaphore):
        self.engine, self.semaphore = engine, semaphore
        self.before, self.inside, self.turns = 0, 0, 0

    def note(self, instruction):
        instruction.then_inc(self.semaphore, 1)
        self.inside += 1

    def value(self):
        return self.turns + (self.before + self.inside)

    def settle(self, passed=None):
        self.engine.wait_ge(self.semaphore, self.value())
        if passed is not None:
            self.engine.sem_inc(passed, 1)

    @contextmanager
    def loop(self, count, each):
        self.before, self.inside = self.before + self.inside, 0
        with self.engine.Fori(0, count) as i:
            self.turns = i * each
            yield i
        assert self.inside == each, (self.inside, each)
        self.before, self.inside, self.turns = self.before + count * each, 0, 0


def wait_alone(engine, semaphore, value, passed):
    engine.wait_ge(semaphore, value)
    engine.sem_inc(passed, 1)


class Norm:

    def __init__(self, k, name):
        self.stats = k.sb(f"{name}_stats", [P, GT, 6])
        self.mv = k.sb(f"{name}_mean_var", [P, GT, 2])
        self.veps = k.sb(f"{name}_var_eps", [P, GT])
        self.rstd = k.sb(f"{name}_rstd", [P, GT])
        self.veps_ready = k.sem(f"{name}_veps_ready")
        self.rstd_ready = k.sem(f"{name}_rstd_ready")
        self.passed = k.sem(f"{name}_passed")


def norm_vector(v, steps, norm, turn, source, target):
    for j in range(GT):
        steps.note(v.bn_stats(norm.stats[:, j, :], source(j)))
    steps.settle(norm.passed)
    for j in range(GT):
        steps.note(v.bn_aggr(norm.mv[:, j, :], norm.stats[:, j, :]))
    steps.settle()
    v.tensor_scalar(norm.veps[:, :], norm.mv[:, :, 1], EPS, None, ALU.add).then_inc(norm.veps_ready, 1)
    v.wait_ge(norm.rstd_ready, turn + 1)
    for j in range(GT):
        last = v.tensor_scalar(target(j), source(j), norm.mv[:, j, 0:1], norm.rstd[:, j:j + 1],
                               ALU.subtract, ALU.mult)
    return last


def norm_gpsimd(pool, k, norm, turn):
    pool.wait_ge(norm.veps_ready, turn + 1)
    pool.tensor_tensor(norm.rstd[:, :], norm.veps[:, :], k.minus_half[:, :], ALU.pow)\
        .then_inc(norm.rstd_ready, 1)


class Core:

    def __init__(self, nc, ctx):
        self.nc, self.whole, self.scope = nc, ctx, ctx
        self.semaphores = []

    def sb(self, name, shape, dt=F32):
        return self.scope.enter_context(self.nc.sbuf_tensor(name, shape, dt))

    def ps(self, name, shape, dt=F32):
        return self.scope.enter_context(self.nc.psum_tensor(name, shape, dt))

    def sem(self, name):
        semaphore = self.nc.alloc_semaphore(name=name)
        self.semaphores.append(semaphore)
        return semaphore

    @contextmanager
    def stage(self):
        self.semaphores = []
        with ExitStack() as scope:
            self.scope = scope
            yield
        self.scope = self.whole
        self.nc.clear_and_free_semaphores(self.semaphores)
        self.nc.all_engine_barrier()


def row_chunks(w):
    return w.rearrange("(c p) n -> p c n", p=P)


def constants(k):
    k.ident = k.sb("ident", [P, P])
    k.ident16 = k.sb("ident16", [P, P], BF16)
    k.minus_half = k.sb("minus_half", [P, GT])
    made = k.sem("constants_made")
    with k.nc.Block() as block:
        @block.gpsimd
        def _(pool):
            pool.memset(k.ident[:, :], 0.0).then_inc(made, 1)
            pool.memset(k.ident16[:, :], 0.0).then_inc(made, 1)
            pool.memset(k.minus_half[:, :], -0.5).then_inc(made, 1)
            pool.wait_ge(made, 3)
            for m in (k.ident, k.ident16):
                pool.affine_select(out=m[:, :], in_=m[:, :], compare_op=ALU.not_equal, fill=1.0, base=0,
                                   pattern=[[-1, P]], channel_multiplier=1).then_inc(made, 1)
            pool.wait_ge(made, 5)


def attention_first(k, d):
    h, x = k.h, k.x
    wq = k.sb("wq", [P, KC, D])
    wk4 = k.sb("wk4", [P, KC, QUADS * HD])
    wv = k.sb("wv", [P, KC, HD])
    wo = k.sb("wo", [P, KC, D])
    ln_g = k.sb("ln1_g", [P, KC])
    ln_b = k.sb("ln1_b", [P, KC])
    bq = k.sb("bq", [P, KC])
    bk4 = k.sb("bk4", [P, 1])
    bv_rows = k.sb("bv_rows", [P, HD])
    bo_rows = k.sb("bo_rows", [P, D])
    ids = k.sb("ids", [P, TILES], I32)
    over = k.sb("over", [P, TILES], I32)
    is_over = k.sb("is_over", [P, TILES], I32)
    mask = k.sb("mask", [P, GN], BF16)
    norm0, norm1 = Norm(k, "norm0"), Norm(k, "norm1")
    a = k.sb("a", [P, GT, D])
    aT = k.sb("aT", [P, KC, GN])
    qT = k.sb("qT", [P, KC, GN])
    kT = k.sb("kT", [P, GN])
    vals = k.sb("vals", [P, GT, HD + 1])
    top = k.sb("top", [P, 2, UH, 1])
    prob = k.sb("prob", [P, 2, UH, P])
    probT = k.sb("probT", [P, 2, UH, P])
    rsum = k.sb("rsum", [P, 2, UH, 1])
    o = k.sb("o", [P, 2, D])
    oT = k.sb("oT", [P, KC, P])

    ps_s = k.ps("ps_s", [P, 2, UH, P])
    ps_t = k.ps("ps_t", [P, UH, P])
    ps_m = [k.ps(f"ps_m{i}", [P, GN]) for i in range(2)]
    ps_a = ps_s[:, :, :, :].rearrange("p a b c -> p (a b c)")

    ids_in = k.sem("ids_in")
    weights_in = k.sem("att0_weights_in")
    over_ready, pool_passed = k.sem("over_ready"), k.sem("att0_pool_passed")
    gathered = [k.sem(f"gathered{g}") for g in range(GROUPS)]
    mask_made = k.sem("mask_made")
    dve = k.sem("att0_dve")
    x0_ready, a_ready = k.sem("x0_ready"), k.sem("a_ready")
    residual_ready = k.sem("residual_ready")
    t_ready, aT_ready = k.sem("att0_t_ready"), k.sem("aT_ready")
    qk_mm, qk_done, v_mm, v_done = k.sem("qk_mm"), k.sem("qk_done"), k.sem("v_mm"), k.sem("v_done")
    s_ready, shifted, exp_done = k.sem("s_ready"), k.sem("shifted"), k.sem("exp_done")
    pt_ready, pt_done = k.sem("pt_ready"), k.sem("pt_done")
    pv_ready, o_done = k.sem("pv_ready"), k.sem("o_done")
    ot_ready, ot_done = k.sem("ot_ready"), k.sem("ot_done")
    wo_ready, x1_done = k.sem("wo_ready"), k.sem("x1_done")

    with k.nc.Block() as block:
        @block.sync
        def _(sp):
            sp.dma_start(ids[:, :], d["ids"]).then_inc(ids_in, 16)
            for dst, src in ((wq, row_chunks(d["wq"])), (wk4, row_chunks(d["wk4"])), (wv, row_chunks(d["wv"])),
                             (wo, row_chunks(d["wo"]))):
                sp.dma_start(dst[:, :, :], src).then_inc(weights_in, 16)
            for dst, src in ((ln_g, d["ln1_g"]), (ln_b, d["ln1_b"]), (bq, d["bq"]), (bk4, d["bk4"]),
                             (bv_rows, d["bv"].to_broadcast([P, HD])), (bo_rows, d["bo"].to_broadcast([P, D]))):
                sp.dma_start(dst[:, :], src).then_inc(weights_in, 16)

        WEIGHTS = 16 * 10

        @block.gpsimd
        def _(pool):
            pool.memset(vals[:, :, :], 1.0).then_inc(mask_made, 1)
            pool.memset(mask[:, :], 0.0).then_inc(mask_made, 1)
            pool.wait_ge(mask_made, 2)
            pool.affine_select(out=mask[:, :], in_=mask[:, :], compare_op=ALU.is_ge, fill=MASKED, base=0,
                               pattern=[[0, GN // P], [-1, P]], channel_multiplier=1).then_inc(mask_made, 1)
            pool.wait_ge(over_ready, 2)
            for t in range(TILES):
                pool.indirect_dma_start(h[:, t, :], None, d["tok"], bass.IndirectOffsetOnAxis(
                    ap=ids[:, t:t + 1].bitcast(U32), axis=0)).then_inc(gathered[t // GT], 16)
                pool.indirect_dma_start(x[:, t, :], None, d["extra"], bass.IndirectOffsetOnAxis(
                    ap=over[:, t:t + 1].bitcast(U32), axis=0)).then_inc(gathered[t // GT], 16)

            def group(g):
                norm_gpsimd(pool, k, norm0, g)
                norm_gpsimd(pool, k, norm1, g)
                wait_alone(pool, a_ready, g + 1, pool_passed)
                for j in range(GT):
                    t = x[:, bass.ds(g * GT + j, 1), :].rearrange("p a n -> p (a n)")
                    last = pool.tensor_tensor(t, t, bo_rows[:, :], ALU.add)
                last.then_inc(residual_ready, 1)

            pool.wait_ge(weights_in, WEIGHTS)
            with pool.Fori(0, GROUPS) as g:
                group(g)

        @block.vector
        def _(v):
            v.sem_inc(x1_done, FIRST)
            v.sem_inc(shifted, FIRST)
            steps = Steps(v, dve)
            v.wait_ge(ids_in, 16)
            v.tensor_scalar(over[:, :], ids[:, :], OVER_FIRST, 0, ALU.subtract, ALU.max).then_inc(over_ready, 1)
            v.tensor_scalar(is_over[:, :], ids[:, :], OVER_FIRST, None, ALU.is_ge).then_inc(over_ready, 1)
            v.wait_ge(over_ready, 2)

            for t in range(TILES):
                if t % GT == 0:
                    v.wait_ge(gathered[t // GT], 32 * GT)
                steps.note(v.copy_predicated(h[:, t, :], is_over[:, t:t + 1].to_broadcast([P, D]), x[:, t, :]))
            steps.settle()

            def tile(buf, g, j):
                return buf[:, bass.ds(g * GT + j, 1), :].rearrange("p a n -> p (a n)")

            def normalise(g, first):
                steps.note(norm_vector(v, steps, norm0, g, lambda j: tile(h, g, j), lambda j: tile(x, g, j)))
                steps.settle(norm0.passed)
                if not first:
                    wait_alone(v, t_ready, g * KC, norm1.passed)
                norm_vector(v, steps, norm1, g, lambda j: tile(x, g, j), lambda j: a[:, j, :])\
                    .then_inc(a_ready, 1)

            def shift(g, u):
                s = ps_s[:, u % 2, :, :]
                v.wait_ge(s_ready, g * UNITS + (u + 1))
                steps.note(v.tensor_reduce(top[:, u % 2, :, 0], s, AX.X, ALU.max))
                steps.settle()
                v.tensor_tensor(prob[:, u % 2, :, :], s, top[:, u % 2, :, :].to_broadcast([P, UH, P]),
                                ALU.subtract).then_inc(shifted, 1)

            def divide(g, u):
                m = ps_m[u % 2][:, 0:UH * (HD + 1)].rearrange("p (h n) -> p h n", h=UH)
                v.wait_ge(pv_ready, g * UNITS + (u + 1))
                steps.note(v.reciprocal(rsum[:, u % 2, :, :], m[:, :, HD:HD + 1]))
                steps.settle()
                out = o[:, (u // 2) % 2, :].rearrange("p (m r n) -> p r m n", r=QUADS, n=HD)
                half = u % 2
                for r in range(2):
                    last = v.tensor_tensor(out[:, 2 * half + r, :, :], m[:, 4 * r:4 * r + 4, 0:HD],
                                           rsum[:, u % 2, 4 * r:4 * r + 4, :].to_broadcast([P, 4, HD]), ALU.mult)
                last.then_inc(o_done, 1)

            def residual(g, b):
                v.wait_ge(wo_ready, g * GT + (b + 1))
                v.tensor_tensor(tile(x, g, b), ps_m[1][:, :], tile(x, g, b), ALU.add).then_inc(x1_done, 1)

            def group(g, last):
                if not last:
                    normalise(g + 1, False)
                v.wait_ge(v_mm, g + 1)
                v.tensor_tensor(vals[:, :, 0:HD], ps_m[1][:, 0:GT * HD].rearrange("p (t n) -> p t n", t=GT),
                                bv_rows[:, :].rearrange("p (t n) -> p t n", t=1).to_broadcast([P, GT, HD]),
                                ALU.add).then_inc(v_done, 1)
                v.wait_ge(residual_ready, g + 1)
                shift(g, 0)
                shift(g, 1)
                for u in range(UNITS):
                    if u + 2 < UNITS:
                        shift(g, u + 2)
                    if u % 2 == 0 and u >= 2:
                        residual(g, u // 2 - 1)
                    divide(g, u)
                residual(g, GT - 1)

            v.wait_ge(weights_in, WEIGHTS)
            v.wait_ge(mask_made, 1)
            normalise(0, True)
            with steps.loop(GROUPS - 1, 4 * GT + 1 + 2 * UNITS) as g:
                group(g, False)
            group(GROUPS - 1, True)

        @block.scalar
        def _(act):
            act.sem_inc(ot_done, FIRST)
            act.wait_ge(weights_in, WEIGHTS)

            def turn(g):
                for c in range(KC):
                    act.wait_ge(t_ready, g * KC + (c + 1))
                    act.activation(aT[:, c, :], ps_a[:, c * GN:(c + 1) * GN], ACT.Identity,
                                   bias=ln_b[:, c:c + 1], scale=ln_g[:, c:c + 1]).then_inc(aT_ready, 1)

            def group(g, last):
                for c in range(KC + 1):
                    act.wait_ge(qk_mm, g * (KC + 1) + (c + 1))
                    out, bias = (qT[:, c, :], bq[:, c:c + 1]) if c < KC else (kT[:, :], bk4[:, :])
                    act.activation(out, ps_m[c % 2][:, :], ACT.Identity, bias=bias).then_inc(qk_done, 1)
                if not last:
                    turn(g + 1)

                def exponent(u):
                    act.wait_ge(shifted, FIRST + g * UNITS + (u + 1))
                    act.activation(prob[:, u % 2, :, :], prob[:, u % 2, :, :], ACT.Exp, scale=ATT0_SCALE)\
                        .then_inc(exp_done, 1)

                def turned_heads(b):
                    act.wait_ge(ot_ready, g * GT + (b + 1))
                    act.copy(oT[:, :, :], ps_m[0][:, :].rearrange("p (c n) -> p c n", c=KC)).then_inc(ot_done, 1)

                exponent(0)
                exponent(1)
                for u in range(UNITS):
                    act.wait_ge(pt_ready, g * UNITS + (u + 1))
                    act.copy(probT[:, u % 2, :, :], ps_t[:, :, :]).then_inc(pt_done, 1)
                    if u % 2 == 0 and u >= 2:
                        turned_heads(u // 2 - 1)
                    if u + 2 < UNITS:
                        exponent(u + 2)
                turned_heads(GT - 1)

            turn(0)
            with act.Fori(0, GROUPS - 1) as g:
                group(g, False)
            group(GROUPS - 1, True)

        @block.tensor
        def _(pe):
            def turn(g, first):
                pe.wait_ge(a_ready, g + 1)
                if not first:
                    pe.wait_ge(shifted, FIRST + (g - 1) * UNITS)
                for c in range(KC):
                    for j in range(GT):
                        last = pe.transpose(ps_a[:, c * GN + j * P:c * GN + (j + 1) * P],
                                            a[:, j, c * P:(c + 1) * P], k.ident[:, :])
                    last.then_inc(t_ready, 1)

            def project(g):
                pe.wait_ge(aT_ready, (g + 1) * KC)
                pe.wait_ge(ot_done, FIRST + g * GT)
                pe.wait_ge(x1_done, FIRST + g * GT)
                for c in range(KC + 1):
                    if c >= 2:
                        pe.wait_ge(qk_done, g * (KC + 1) + (c - 1))
                    for i in range(KC):
                        w = wq[:, i, c * P:(c + 1) * P] if c < KC else wk4[:, i, :]
                        last = pe.matmul(ps_m[c % 2][:, :], w, aT[:, i, :], start=(i == 0), stop=(i == KC - 1))
                    last.then_inc(qk_mm, 1)
                pe.wait_ge(qk_done, g * (KC + 1) + 4)
                for j in range(GT):
                    for i in range(KC):
                        last = pe.matmul(ps_m[1][:, j * HD:(j + 1) * HD], aT[:, i, j * P:(j + 1) * P], wv[:, i, :],
                                         start=(i == 0), stop=(i == KC - 1))
                last.then_inc(v_mm, 1)

            def scores(g, u):
                b = u // 2
                if u >= 2:
                    pe.wait_ge(shifted, FIRST + g * UNITS + (u - 1))
                for r in range(2):
                    q = 2 * (u % 2) + r
                    bank = ps_s[:, u % 2, 4 * r:4 * r + 4, :]
                    pe.matmul(bank, k.ident16[:, :], mask[:, :].rearrange("p (h n) -> p h n", h=4),
                              start=True, stop=False)
                    for m in range(KC):
                        last = pe.matmul(bank[:, m, :], qT[HD * q:HD * (q + 1), m, b * P:(b + 1) * P],
                                         kT[HD * q:HD * (q + 1), b * P:(b + 1) * P], start=False, stop=(m == KC - 1))
                last.then_inc(s_ready, 1)

            def turn_probs(g, u):
                pe.wait_ge(exp_done, g * UNITS + (u + 1))
                if u >= 1:
                    pe.wait_ge(pt_done, g * UNITS + u)
                for i in range(UH):
                    last = pe.transpose(ps_t[:, i, :], prob[:, u % 2, i, :], k.ident[:, :])
                last.then_inc(pt_ready, 1)

            def weigh(g, u):
                pe.wait_ge(pt_done, g * UNITS + (u + 1))
                if u == 0:
                    pe.wait_ge(qk_done, (g + 1) * (KC + 1))
                    pe.wait_ge(v_done, g + 1)
                elif u % 2 == 0:
                    pe.wait_ge(ot_done, FIRST + g * GT + u // 2)
                elif u >= 3:
                    pe.wait_ge(x1_done, FIRST + g * GT + u // 2)
                for i in range(UH):
                    last = pe.matmul(ps_m[u % 2][:, i * (HD + 1):(i + 1) * (HD + 1)], probT[:, u % 2, i, :],
                                     vals[:, u // 2, :], start=True, stop=True)
                last.then_inc(pv_ready, 1)

            def turn_heads(g, b):
                pe.wait_ge(o_done, g * UNITS + 2 * (b + 1))
                for c in range(KC):
                    last = pe.transpose(ps_m[0][:, c * P:(c + 1) * P], o[:, b % 2, c * P:(c + 1) * P], k.ident[:, :])
                last.then_inc(ot_ready, 1)

            def output(g, b):
                pe.wait_ge(ot_done, FIRST + g * GT + (b + 1))
                for c in range(KC):
                    last = pe.matmul(ps_m[1][:, :], oT[:, c, :], wo[:, c, :], start=(c == 0), stop=(c == KC - 1))
                last.then_inc(wo_ready, 1)

            def group(g, last):
                project(g)
                if not last:
                    turn(g + 1, False)
                    pe.wait_ge(aT_ready, (g + 2) * KC)
                pe.wait_ge(qk_done, (g + 1) * (KC + 1))
                scores(g, 0)
                scores(g, 1)
                for u in range(UNITS):
                    turn_probs(g, u)
                    even = u % 2 == 0 and u >= 2
                    if even:
                        turn_heads(g, u // 2 - 1)
                    if u + 2 < UNITS:
                        scores(g, u + 2)
                    if even:
                        output(g, u // 2 - 1)
                    weigh(g, u)
                turn_heads(g, GT - 1)
                output(g, GT - 1)

            pe.wait_ge(mask_made, 3)
            pe.wait_ge(weights_in, WEIGHTS)
            turn(0, True)
            with pe.Fori(0, GROUPS - 1) as g:
                group(g, False)
            group(GROUPS - 1, True)


def feed_forward(k, d):
    h, x = k.h, k.x
    wfc = k.sb("wfc", [P, KC, INTER])
    wproj = k.sb("wproj", [P, IC, D])
    ln_g = k.sb("ln2_g", [P, KC])
    ln_b = k.sb("ln2_b", [P, KC])
    bfc = k.sb("bfc", [P, IC])
    bproj_rows = k.sb("bproj_rows", [P, D])
    norm = Norm(k, "norm2")
    a = k.sb("ff_a", [P, GT, D])
    aT = k.sb("ff_aT", [P, KC, GN])
    gT = k.sb("gT", [P, IC, GN])
    ps_a = [k.ps(f"ff_ps_a{c}", [P, GN]) for c in range(KC)]
    ps_f = [k.ps(f"ps_f{i}", [P, GN]) for i in range(2)]
    ps_p = [k.ps(f"ps_p{i}", [P, D]) for i in range(2)]

    weights_in, proj_in = k.sem("ff_weights_in"), k.sem("proj_in")
    dve = k.sem("ff_dve")
    a_ready, t_ready, aT_ready = k.sem("ff_a_ready"), k.sem("ff_t_ready"), k.sem("ff_aT_ready")
    fc_mm, gelu_done = k.sem("fc_mm"), k.sem("gelu_done")
    proj_mm, h_done = k.sem("proj_mm"), k.sem("ff_h_done")
    pool_own, summed = k.sem("ff_pool"), k.sem("ff_summed")

    with k.nc.Block() as block:
        @block.sync
        def _(sp):
            for dst, src in ((ln_g, d["ln2_g"]), (ln_b, d["ln2_b"]), (bfc, d["bfc"]),
                             (bproj_rows, d["bproj"].to_broadcast([P, D]))):
                sp.dma_start(dst[:, :], src).then_inc(weights_in, 16)
            sp.dma_start(wfc[:, :, :], row_chunks(d["wfc"])).then_inc(weights_in, 16)
            sp.dma_start(wproj[:, :, :], row_chunks(d["wproj"])).then_inc(proj_in, 16)

        WEIGHTS = 16 * 5

        def tile(buf, g, j):
            return buf[:, bass.ds(g * GT + j, 1), :].rearrange("p a n -> p (a n)")

        @block.gpsimd
        def _(pool):
            steps = Steps(pool, pool_own)
            pool.wait_ge(weights_in, WEIGHTS)
            with steps.loop(GROUPS, 2 * GT) as g:
                norm_gpsimd(pool, k, norm, g)
                for j in range(GT):
                    steps.note(pool.tensor_tensor(tile(h, g, j), tile(h, g, j), tile(x, g, j), ALU.add))
                steps.settle(norm.passed)
                for j in range(GT):
                    steps.note(pool.tensor_tensor(tile(h, g, j), tile(h, g, j), bproj_rows[:, :], ALU.add))
                steps.settle()
                pool.sem_inc(summed, 1)

        @block.vector
        def _(v):
            v.sem_inc(h_done, FIRST)
            steps = Steps(v, dve)

            def normalise(g, first):
                if not first:
                    wait_alone(v, t_ready, g * KC, norm.passed)
                norm_vector(v, steps, norm, g, lambda j: tile(x, g, j), lambda j: a[:, j, :]).then_inc(a_ready, 1)

            def group(g, last):
                if not last:
                    normalise(g + 1, False)
                v.wait_ge(summed, g + 1)
                for j in range(GT):
                    v.wait_ge(proj_mm, g * GT + (j + 1))
                    v.tensor_tensor(tile(h, g, j), ps_p[j % 2][:, :], tile(h, g, j), ALU.add).then_inc(h_done, 1)

            normalise(0, True)
            with steps.loop(GROUPS - 1, 2 * GT) as g:
                group(g, False)
            group(GROUPS - 1, True)

        @block.scalar
        def _(act):
            def turn(g):
                for c in range(KC):
                    act.wait_ge(t_ready, g * KC + (c + 1))
                    act.activation(aT[:, c, :], ps_a[c][:, :], ACT.Identity, bias=ln_b[:, c:c + 1],
                                   scale=ln_g[:, c:c + 1]).then_inc(aT_ready, 1)

            def group(g, last):
                for c in range(IC):
                    act.wait_ge(fc_mm, g * IC + (c + 1))
                    act.activation(gT[:, c, :], ps_f[c % 2][:, :], ACT.Gelu_apprx_tanh, bias=bfc[:, c:c + 1])\
                        .then_inc(gelu_done, 1)
                if not last:
                    turn(g + 1)

            act.wait_ge(weights_in, WEIGHTS)
            turn(0)
            with act.Fori(0, GROUPS - 1) as g:
                group(g, False)
            group(GROUPS - 1, True)

        @block.tensor
        def _(pe):
            def turn(g):
                pe.wait_ge(a_ready, g + 1)
                pe.wait_ge(aT_ready, g * KC)
                for c in range(KC):
                    for j in range(GT):
                        last = pe.transpose(ps_a[c][:, j * P:(j + 1) * P], a[:, j, c * P:(c + 1) * P], k.ident[:, :])
                    last.then_inc(t_ready, 1)

            def group(g, last):
                pe.wait_ge(aT_ready, (g + 1) * KC)
                for c in range(IC):
                    if c >= 2:
                        pe.wait_ge(gelu_done, g * IC + (c - 1))
                    for i in range(KC):
                        mm = pe.matmul(ps_f[c % 2][:, :], wfc[:, i, c * P:(c + 1) * P], aT[:, i, :],
                                       start=(i == 0), stop=(i == KC - 1))
                    mm.then_inc(fc_mm, 1)
                if not last:
                    turn(g + 1)
                for j in range(GT):
                    pe.wait_ge(h_done, FIRST + g * GT + max(j - 1, 0))
                    for c in range(IC):
                        if j == 0:
                            pe.wait_ge(gelu_done, g * IC + (c + 1))
                        mm = pe.matmul(ps_p[j % 2][:, :], gT[:, c, j * P:(j + 1) * P], wproj[:, c, :],
                                       start=(c == 0), stop=(c == IC - 1))
                    mm.then_inc(proj_mm, 1)

            pe.wait_ge(weights_in, WEIGHTS)
            turn(0)
            pe.wait_ge(proj_in, 16)
            with pe.Fori(0, GROUPS - 1) as g:
                group(g, False)
            group(GROUPS - 1, True)


def write_output(k, d):
    out_sent = k.sem("out_sent")
    with k.nc.Block() as block:
        @block.sync
        def _(sp):
            sp.dma_start(d["out"].rearrange("t p n -> p t n"), k.h[:, :, :]).then_inc(out_sent, 16)
            sp.wait_ge(out_sent, 16)


BLOCK = 2 * P
E0, TOP0, SETS0, SET_TOP0 = 16, 4, 4, 2
MID0, SHARED = 352, 704
E1, TOP1, MID1 = 8, 2, 256


def chunks(n):
    return [(c, min(P, n - c)) for c in range(0, n, P)]


class Routing:

    def __init__(self, k, name, experts, top):
        self.name, self.experts, self.top = name, experts, top
        self.blocks = (TOKENS * top + experts * (BLOCK - 1)) // BLOCK
        self.slots = self.blocks * BLOCK
        self.best = k.sb(f"{name}_best", [P, TILES, 8])
        self.slot = k.sb(f"{name}_slot", [P, TILES, top], I32)
        self.token = k.sb(f"{name}_token", [P, 2 * self.blocks], I32)
        self.expert = k.sb(f"{name}_expert", [P, self.blocks], I32)
        self.weight = self.best
        nc = k.nc
        self.rows = nc.dram_tensor(f"{name}_rows", (TOKENS, D), F32).ap()
        self.map = nc.dram_tensor(f"{name}_map", (self.slots, 1), I32).ap()
        self.result = nc.dram_tensor(f"{name}_result", (self.slots, D), F32).ap()


class RoutingWork:

    def __init__(self, k, r):
        n, e = r.name, r.experts
        self.scores = k.sb(f"{n}_scores", [P, TILES, e])
        self.index = k.sb(f"{n}_index", [P, TILES, 8], U32)
        self.chosen = k.sb(f"{n}_chosen", [P, r.top, TILES, e])
        self.indexf = k.sb(f"{n}_indexf", [P, TILES, 8])
        self.any = k.sb(f"{n}_any", [P, TILES, e])
        self.before = k.sb(f"{n}_before", [P, TILES, e])
        self.count = k.sb(f"{n}_count", [P, e])
        self.counti = k.sb(f"{n}_counti", [P, e], I32)
        self.blocks = k.sb(f"{n}_nblocks", [P, e])
        self.end = k.sb(f"{n}_end", [P, e])
        self.first = k.sb(f"{n}_first", [P, 1, e])
        self.place = k.sb(f"{n}_place", [P, TILES, e])
        self.product = k.sb(f"{n}_product", [P, TILES, e])
        self.slotf = k.sb(f"{n}_slotf", [P, TILES, r.top])
        self.past = k.sb(f"{n}_past", [P, r.blocks, e])
        self.expertf = k.sb(f"{n}_expertf", [P, r.blocks])
        self.iota_e = k.sb(f"{n}_iota_e", [P, 1, e])
        self.iota_b = k.sb(f"{n}_iota_b", [P, r.blocks, 1])
        self.token_id = k.sb(f"{n}_token_id", [P, TILES], I32)
        self.zeros = k.sb(f"{n}_zeros", [2 * r.blocks, P], I32)
        self.map = k.sb(f"{n}_map_sb", [2 * r.blocks, P], I32)
        self.mapf = k.sb(f"{n}_mapf", [2 * r.blocks, P])
        self.before_p = k.sb(f"{n}_before_p", [P, P])
        self.ones = k.sb(f"{n}_ones", [P, P])
        self.made, self.any_ready, self.ranked = k.sem(f"{n}_made"), k.sem(f"{n}_any_ready"), k.sem(f"{n}_ranked")
        self.slot_ready, self.scattered = k.sem(f"{n}_slot_ready"), k.sem(f"{n}_scattered")
        self.map_zeroed, self.map_in = k.sem(f"{n}_map_zeroed"), k.sem(f"{n}_map_in")
        self.map_ready, self.map_turned = k.sem(f"{n}_map_ready"), k.sem(f"{n}_map_turned")
        self.token_ready = k.sem(f"{n}_token_ready")


def routing_constants(pool, r, w):
    pool.memset(w.before_p[:, :], 0.0).then_inc(w.made, 1)
    pool.memset(w.ones[:, :], 1.0).then_inc(w.made, 1)
    pool.memset(w.zeros[:, :], 0).then_inc(w.made, 1)
    pool.iota(w.iota_e[:, :, :], [[1, r.experts]], base=0, channel_multiplier=0,
              allow_small_or_imprecise_dtypes=True).then_inc(w.made, 1)
    pool.iota(w.iota_b[:, :, :], [[1, r.blocks]], base=0, channel_multiplier=0,
              allow_small_or_imprecise_dtypes=True).then_inc(w.made, 1)
    pool.iota(w.token_id[:, :], [[P, TILES]], base=0, channel_multiplier=1).then_inc(w.made, 1)
    pool.wait_ge(w.made, 6)
    pool.affine_select(out=w.before_p[:, :], in_=w.before_p[:, :], compare_op=ALU.is_ge, fill=1.0, base=0,
                       pattern=[[-1, P]], channel_multiplier=1).then_inc(w.made, 1)
    pool.dma_start(r.map.rearrange("(a b) n -> a (b n)", b=P), w.zeros[:, :]).then_inc(w.map_zeroed, 16)


ROUTING_MADE = 7


def routing_vector(v, steps, r, w, iota=True):
    e = r.experts
    steps.note(v.tensor_copy(w.indexf[:, :, :], w.index[:, :, :]))
    steps.settle()
    for c in range(r.top):
        steps.note(v.tensor_tensor(w.chosen[:, c, :, :], w.indexf[:, :, c:c + 1].to_broadcast([P, TILES, e]),
                                   w.iota_e[:, :, :].to_broadcast([P, TILES, e]), ALU.is_equal))
    steps.settle()
    steps.note(v.tensor_tensor(w.any[:, :, :], w.chosen[:, 0, :, :], w.chosen[:, 1, :, :], ALU.add))
    for c in range(2, r.top):
        steps.settle()
        steps.note(v.tensor_tensor(w.any[:, :, :], w.any[:, :, :], w.chosen[:, c, :, :], ALU.add))
    steps.settle()
    v.sem_inc(w.any_ready, 1)


def routing_tensor(pe, r, w, ps_rank, ps_sum):
    pe.wait_ge(w.any_ready, 1)
    pe.wait_ge(w.made, ROUTING_MADE)
    pe.matmul(ps_rank, w.before_p[:, :], w.any[:, :, :].rearrange("p t e -> p (t e)"), start=True, stop=True)
    pe.matmul(ps_sum, w.ones[:, :], w.any[:, :, :].rearrange("p t e -> p (t e)"), start=True, stop=True)\
        .then_inc(w.ranked, 1)


def routing_slots(v, steps, r, w, ps_rank, ps_sum):
    e = r.experts
    rank = ps_rank.rearrange("p (t e) -> p t e", e=e)
    rows = ps_sum.rearrange("p (t e) -> p t e", e=e)
    steps.note(v.memset(w.before[:, 0, :], 0.0))
    steps.settle()
    v.wait_ge(w.ranked, 1)
    for t in range(TILES):
        out = w.before[:, t + 1, :] if t + 1 < TILES else w.count[:, :]
        steps.note(v.tensor_tensor(out, rows[:, t, :], w.before[:, t, :], ALU.add))
        steps.settle()
    steps.note(v.tensor_scalar(w.counti[:, :], w.count[:, :], float(BLOCK - 1), None, ALU.add))
    steps.settle()
    steps.note(v.tensor_scalar(w.counti[:, :], w.counti[:, :], BLOCK.bit_length() - 1, None,
                               ALU.logical_shift_right))
    steps.settle()
    steps.note(v.tensor_copy(w.blocks[:, :], w.counti[:, :]))
    steps.settle()
    steps.note(v.tensor_copy(w.end[:, 0:1], w.blocks[:, 0:1]))
    for i in range(1, e):
        steps.settle()
        steps.note(v.tensor_tensor(w.end[:, i:i + 1], w.end[:, i - 1:i], w.blocks[:, i:i + 1], ALU.add))
    steps.settle()
    steps.note(v.tensor_tensor(w.first[:, 0, :], w.end[:, :], w.blocks[:, :], ALU.subtract))
    steps.note(v.tensor_tensor(w.past[:, :, :], w.iota_b[:, :, :].to_broadcast([P, r.blocks, e]),
                               w.end[:, :].rearrange("p (a e) -> p a e", a=1).to_broadcast([P, r.blocks, e]),
                               ALU.is_ge))
    steps.note(v.tensor_tensor(w.place[:, :, :], rank, w.before[:, :, :], ALU.add))
    steps.settle()
    steps.note(v.tensor_scalar(w.first[:, 0, :], w.first[:, 0, :], float(BLOCK), None, ALU.mult))
    steps.note(v.tensor_reduce(w.expertf[:, :], w.past[:, :, :], AX.X, ALU.add))
    steps.settle()
    steps.note(v.tensor_tensor(w.place[:, :, :], w.place[:, :, :], w.first[:, :, :].to_broadcast([P, TILES, e]),
                               ALU.add))
    steps.note(v.tensor_scalar(r.expert[:, :], w.expertf[:, :], float(e - 1), None, ALU.min))
    for c in range(r.top):
        steps.settle()
        steps.note(v.tensor_tensor(w.product[:, :, :], w.place[:, :, :], w.chosen[:, c, :, :], ALU.mult))
        steps.settle()
        steps.note(v.tensor_reduce(w.slotf[:, :, c], w.product[:, :, :], AX.X, ALU.add))
    steps.settle()
    v.tensor_copy(r.slot[:, :, :], w.slotf[:, :, :]).then_inc(w.slot_ready, 1)


def routing_scatter(pool, r, w):
    pool.wait_ge(w.map_zeroed, 16)
    pool.wait_ge(w.slot_ready, 1)
    for t in range(TILES):
        for c in range(r.top):
            pool.indirect_dma_start(r.map, bass.IndirectOffsetOnAxis(ap=r.slot[:, t, c:c + 1].bitcast(U32), axis=0),
                                    w.token_id[:, t:t + 1], None).then_inc(w.scattered, 16)
    pool.wait_ge(w.scattered, 16 * TILES * r.top)
    pool.dma_start(w.map[:, :], r.map.rearrange("(a b) n -> a (b n)", b=P)).then_inc(w.map_in, 16)


PASSES = ((0, 0), (0, 1), (1, 0))


def experts(k, d, r, mid, gated):
    n, nb, mids = r.name + "e", r.blocks, chunks(mid)
    nm = len(mids)
    width = 2 * mid if gated else mid
    parts = KC + nm
    turns = (nb - 1) // 2
    spare = k.x[:, :, :].rearrange("p t n -> p (t n)")
    up = [spare[:, i * KC * width:(i + 1) * KC * width].rearrange("p (c n) -> p c n", c=KC) for i in range(2)]
    down = [k.sb(f"{n}_down{i}", [P, nm, D]) for i in range(2)]
    two = lambda name, shape: [k.sb(f"{n}_{name}{part}", shape, F32R) for part in ("", "_rest")]
    up_parts = [two(f"up_part{i}", [P, KC, width]) for i in range(2)]
    down_parts = [two(f"down_part{i}", [P, nm, D]) for i in range(2)]
    if not gated:
        up_bias = [k.sb(f"{n}_up_bias{i}", [P, nm]) for i in range(2)]
        down_bias = [k.sb(f"{n}_down_bias{i}", [P, D]) for i in range(2)]
    pick = [k.sb(f"{n}_pick{i}", [P, 2], I32) for i in range(2)]
    rows = [k.sb(f"{n}_xrows{i}", [P, 2, D]) for i in range(2)]
    rowsT = two("rowsT", [P, KC, BLOCK])
    act_up = k.sb(f"{n}_act_up", [P, nm, BLOCK])
    hid = k.sb(f"{n}_hid", [P, nm, BLOCK])
    hidT = two("hidT", [P, nm, BLOCK])
    y = [k.sb(f"{n}_y{i}", [P, 2, D]) for i in range(2)]
    ps_t = [k.ps(f"{n}_ps_t{i}", [P, 2, BLOCK]) for i in range(2)]
    ps_u = [k.ps(f"{n}_ps_u{i}", [P, 2, BLOCK]) for i in range(3)]
    ps_d = [k.ps(f"{n}_ps_d{i}", [P, D]) for i in range(2)]
    pair = lambda s: [k.sem(f"{n}_{s}{i}") for i in range(2)]
    up_in, rows_in, y_out = pair("up_in"), pair("rows_in"), pair("y_out")
    pick_ready, cut, cut_rest = pair("pick_ready"), pair("cut"), pair("cut_rest")
    turned, down_mm, y_ready, y1_ready = pair("turned"), pair("down_mm"), pair("y_ready"), pair("y1_ready")
    rows_cut, rows_rest = k.sem(f"{n}_rows_cut"), k.sem(f"{n}_rows_rest")
    up_mm, act_done, hid_made = k.sem(f"{n}_up_mm"), k.sem(f"{n}_act_done"), k.sem(f"{n}_hid_made")
    hid_cut, hid_rest = k.sem(f"{n}_hid_cut"), k.sem(f"{n}_hid_rest")
    LOADS = 16 * (2 if gated else 4)

    def piece(q, s):
        if s < KC:
            return up[q][:, s, :], up_parts[q][0][:, s, :], up_parts[q][1][:, s, :]
        return (down[q][:, s - KC, :], down_parts[q][0][:, s - KC, :], down_parts[q][1][:, s - KC, :])

    def following(i, q):
        return (i, 1) if q == 0 else (i + 1, 0)

    def blocks(engine, block):
        with engine.Fori(0, turns) as i:
            block(i, 0, False)
            block(i, 1, False)
        for t in range(2 * turns, nb):
            block(turns, t % 2, t == nb - 1)

    with k.nc.Block() as block:
        @block.sync
        def _(sp):
            def load(i, q, last):
                e = sp.value_load(r.expert[0:1, bass.ds(2 * i + q, 1)], min_val=0, max_val=r.experts - 1)
                sp.wait_ge(cut_rest[q], FIRST + i * parts)
                sp.dma_start(up[q].rearrange("p c n -> p (c n)"),
                             d[f"{r.name}_up"][bass.ds(e, 1), :, :].rearrange("a p n -> (a p) n"))\
                    .then_inc(up_in[q], 16)
                if not gated:
                    sp.wait_ge(y_ready[q], FIRST + i)
                    sp.wait_ge(y1_ready[q], FIRST + i)
                    sp.dma_start(up_bias[q][:, :], d[f"{r.name}_up_bias"][bass.ds(e, 1), :, :]
                                 .rearrange("a p n -> (a p) n")).then_inc(up_in[q], 16)
                    sp.dma_start(down_bias[q][:, :], d[f"{r.name}_down_bias"][bass.ds(e, 1), :]
                                 .to_broadcast([P, D])).then_inc(up_in[q], 16)
                sp.dma_start(down[q][:, :, :].rearrange("p c n -> p (c n)"),
                             d[f"{r.name}_down"][bass.ds(e, 1), :, :].rearrange("a p n -> (a p) n"))\
                    .then_inc(up_in[q], 16)

            blocks(sp, load)
            sp.wait_ge(y_out[0], FIRST + 16 * ((nb + 1) // 2))
            sp.wait_ge(y_out[1], FIRST + 16 * (nb // 2))

        @block.gpsimd
        def _(pool):
            def gather(i, q, last):
                wait_alone(pool, turned[q], FIRST + i, k.passed_pool)
                pool.tensor_copy(pick[q][:, :], r.token[:, bass.ds(4 * i + 2 * q, 2)]).then_inc(pick_ready[q], 1)
                wait_alone(pool, pick_ready[q], i + 1, k.passed_pool)
                for j in range(2):
                    pool.indirect_dma_start(rows[q][:, j, :], None, r.rows, bass.IndirectOffsetOnAxis(
                        ap=pick[q][:, j:j + 1].bitcast(U32), axis=0)).then_inc(rows_in[q], 16)

            blocks(pool, gather)

        @block.scalar
        def _(act):
            for s in (y_ready if gated else [hid_made]) + y_out:
                act.sem_inc(s, FIRST)

            def cut_weights(i, q, some):
                for s in some:
                    if s == 0:
                        act.wait_ge(up_in[q], LOADS * (i + 1))
                        act.wait_ge(down_mm[q], FIRST + i)
                    came, part, rest = piece(q, s)
                    act.copy(part, came).then_inc(cut[q], 1)

            def cut_rows(i, q):
                act.wait_ge(turned[q], FIRST + i + 1)
                for half in range(2):
                    act.copy(rowsT[0][:, 2 * half:2 * half + 2, :], ps_t[half][:, :, :]).then_inc(rows_cut, 1)

            def hidden(i, q, m):
                size = mids[m][1]
                act.wait_ge(up_mm, (2 * i + q) * nm + (m + 1))
                if gated:
                    act.activation(act_up[0:size, m, :], ps_u[m][0:size, 0, :], ACT.Silu).then_inc(act_done, 1)
                else:
                    act.activation(hid[0:size, m, :], ps_u[m][0:size, 0, :], ACT.Silu,
                                   bias=up_bias[q][0:size, m:m + 1]).then_inc(hid_made, 1)

            def cut_hidden(i, q, m):
                size = mids[m][1]
                act.wait_ge(hid_made, FIRST + (2 * i + q) * nm + (m + 1))
                act.copy(hidT[0][0:size, m, :], hid[0:size, m, :]).then_inc(hid_cut, 1)

            def step(i, q, last):
                then = following(i, q)
                if not last:
                    cut_weights(*then, (0,))
                for m in range(nm):
                    hidden(i, q, m)
                    if not last and m < nm - 1:
                        cut_weights(*then, (m + 1,))
                    cut_hidden(i, q, m)
                if not last:
                    cut_rows(*then)
                    cut_weights(*then, range(nm, parts))
                act.wait_ge(y_out[q], FIRST + 16 * i)
                act.wait_ge(down_mm[q], FIRST + i + 1)
                if gated:
                    act.copy(y[q][:, 0, :], ps_d[0][:, :]).then_inc(y_ready[q], 1)
                act.wait_ge(y_ready[q], FIRST + i + 1)
                act.wait_ge(y1_ready[q], FIRST + i + 1)
                act.dma_start(r.result[bass.ds((2 * i + q) * BLOCK, BLOCK), :]
                              .rearrange("(j p) n -> p j n", p=P), y[q][:, :, :]).then_inc(y_out[q], 16)

            cut_weights(0, 0, range(parts))
            cut_rows(0, 0)
            blocks(act, step)

        @block.vector
        def _(v):
            for s in ([hid_made] if gated else y_ready) + y1_ready + cut_rest:
                v.sem_inc(s, FIRST)

            def rest_of_weights(i, q, some):
                for s in some:
                    came, part, rest = piece(q, s)
                    v.wait_ge(cut[q], i * parts + (s + 1))
                    v.tensor_tensor(rest, came, part, ALU.subtract).then_inc(cut_rest[q], 1)

            def rest_of_rows(i, q):
                for half in range(2):
                    two_chunks = slice(2 * half, 2 * half + 2)
                    v.wait_ge(rows_cut, 2 * (2 * i + q) + (half + 1))
                    v.tensor_tensor(rowsT[1][:, two_chunks, :], ps_t[half][:, :, :], rowsT[0][:, two_chunks, :],
                                    ALU.subtract).then_inc(rows_rest, 1)

            def gate(i, q, m):
                size = mids[m][1]
                v.wait_ge(act_done, (2 * i + q) * nm + (m + 1))
                v.tensor_tensor(hid[0:size, m, :], act_up[0:size, m, :], ps_u[m][0:size, 1, :], ALU.mult)\
                    .then_inc(hid_made, 1)

            def rest_of_hidden(i, q, m):
                size = mids[m][1]
                v.wait_ge(hid_cut, (2 * i + q) * nm + (m + 1))
                v.tensor_tensor(hidT[1][0:size, m, :], hid[0:size, m, :], hidT[0][0:size, m, :], ALU.subtract)\
                    .then_inc(hid_rest, 1)

            def step(i, q, last):
                then = following(i, q)
                if not last:
                    rest_of_weights(*then, (0,))
                for m in range(nm):
                    if gated:
                        gate(i, q, m)
                    if not last and m < nm - 1:
                        rest_of_weights(*then, (m + 1,))
                    rest_of_hidden(i, q, m)
                if not last:
                    rest_of_rows(*then)
                    rest_of_weights(*then, range(nm, parts))
                v.wait_ge(y_out[q], FIRST + 16 * i)
                v.wait_ge(down_mm[q], FIRST + i + 1)
                if gated:
                    v.tensor_copy(y[q][:, 1, :], ps_d[1][:, :]).then_inc(y1_ready[q], 1)
                else:
                    v.tensor_tensor(y[q][:, 0, :], ps_d[0][:, :], down_bias[q][:, :], ALU.add)\
                        .then_inc(y_ready[q], 1)
                    v.tensor_tensor(y[q][:, 1, :], ps_d[1][:, :], down_bias[q][:, :], ALU.add)\
                        .then_inc(y1_ready[q], 1)

            rest_of_weights(0, 0, range(parts))
            rest_of_rows(0, 0)
            blocks(v, step)

        @block.tensor
        def _(pe):
            for s in down_mm + turned:
                pe.sem_inc(s, FIRST)

            def turn(i, q):
                pe.wait_ge(rows_in[q], 32 * (i + 1))
                for c in range(KC):
                    for j in range(2):
                        last = pe.transpose(ps_t[c // 2][:, c % 2, j * P:(j + 1) * P],
                                            rows[q][:, j, c * P:(c + 1) * P], k.ident[:, :])
                last.then_inc(turned[q], 1)

            def step(i, q, last):
                pe.wait_ge(rows_rest, 2 * (2 * i + q) + 2)
                pe.wait_ge(cut_rest[q], FIRST + i * parts + KC)
                pe.wait_ge(hid_made, FIRST + (2 * i + q) * nm)
                for m, (c, size) in enumerate(mids):
                    for side in range(2 if gated else 1):
                        first = side * mid + c
                        for a in range(KC):
                            for p, (w, x) in enumerate(PASSES):
                                mm = pe.matmul(ps_u[m][0:size, side, :], up_parts[q][w][:, a, first:first + size],
                                               rowsT[x][:, a, :], start=(a == 0 and p == 0),
                                               stop=(a == KC - 1 and p == len(PASSES) - 1))
                    mm.then_inc(up_mm, 1)
                if not last:
                    turn(*following(i, q))
                pe.wait_ge(cut_rest[q], FIRST + (i + 1) * parts)
                if q == 0:
                    pe.wait_ge(y_ready[1], FIRST + i)
                    pe.wait_ge(y1_ready[1], FIRST + i)
                else:
                    pe.wait_ge(y_ready[0], FIRST + i + 1)
                    pe.wait_ge(y1_ready[0], FIRST + i + 1)
                for j in range(2):
                    for m, (c, size) in enumerate(mids):
                        if j == 0:
                            pe.wait_ge(hid_rest, (2 * i + q) * nm + (m + 1))
                        for p, (w, x) in enumerate(PASSES):
                            mm = pe.matmul(ps_d[j][:, :], hidT[x][0:size, m, j * P:(j + 1) * P],
                                           down_parts[q][w][0:size, m, :], start=(m == 0 and p == 0),
                                           stop=(m == nm - 1 and p == len(PASSES) - 1))
                mm.then_inc(down_mm[q], 1)

            turn(0, 0)
            blocks(pe, step)


def combine(k, r):
    h, top = k.h, r.top
    depth = 4
    y = k.sb(f"{r.name}_back", [P, depth, top, D])
    back = [k.sem(f"{r.name}_back{i}") for i in range(depth)]
    added, own = k.sem(f"{r.name}_combined"), k.sem(f"{r.name}_combine_dve")
    with k.nc.Block() as block:
        @block.gpsimd
        def _(pool):
            for t in range(TILES):
                if t >= depth:
                    pool.wait_ge(added, t - depth + 1)
                for c in range(top):
                    pool.indirect_dma_start(y[:, t % depth, c, :], None, r.result, bass.IndirectOffsetOnAxis(
                        ap=r.slot[:, t, c:c + 1].bitcast(U32), axis=0)).then_inc(back[t % depth], 16)

        @block.vector
        def _(v):
            steps = Steps(v, own)
            for t in range(TILES):
                v.wait_ge(back[t % depth], 16 * top * (t // depth + 1))
                for c in range(top):
                    ins = v.scalar_tensor_tensor(out=h[:, t, :], in0=y[:, t % depth, c, :],
                                                 scalar=r.weight[:, t, c:c + 1], in1=h[:, t, :],
                                                 op0=ALU.mult, op1=ALU.add)
                    if c < top - 1:
                        steps.note(ins)
                        steps.settle()
                ins.then_inc(added, 1)


def tile_of(buf, g, j):
    return buf[:, bass.ds(g * GT + j, 1), :].rearrange("p a n -> p (a n)")


def mixture_first_route(k, d):
    h, r = k.h, k.route0
    mids = chunks(SHARED)
    nm = len(mids)
    wg = k.sb("wg", [P, KC, E0])
    ws1 = k.sb("ws1", [P, KC, SHARED])
    ws3 = k.sb("ws3", [P, KC, SHARED])
    ws2 = k.sb("ws2", [P, nm, D])
    norm = Norm(k, "norm3")
    a = k.sb("m0_a", [P, GT, D])
    aT = k.x[:, :, :].rearrange("p (c g) n -> p c (g n)", c=KC)
    scoresT = k.sb("m0_scoresT", [E0, GN])
    act_up = k.sb("m0_act_up", [P, 2, GN])
    hidT = k.sb("m0_hidT", [P, nm, GN])
    w = RoutingWork(k, r)
    smax = k.sb("m0_smax", [P, TILES, 1])
    ssum = k.sb("m0_ssum", [P, TILES, 1])
    sets = k.sb("m0_sets", [P, TILES, 8])
    set_best = k.sb("m0_set_best", [P, TILES, 8])
    set_index = k.sb("m0_set_index", [P, TILES, 8], U32)
    set_indexf = k.sb("m0_set_indexf", [P, TILES, 8])
    open0 = k.sb("m0_open0", [P, TILES, SETS0])
    open1 = k.sb("m0_open1", [P, TILES, SETS0])
    allowed = k.sb("m0_allowed", [P, TILES, E0])
    ps_a = [k.ps(f"m0_ps_a{i}", [P, 2, GN]) for i in range(2)]
    ps_r = k.ps("m0_ps_r", [P, GN])
    ps_q = k.ps("m0_ps_q", [P, GN])
    ps_d = [k.ps(f"m0_ps_d{i}", [P, D]) for i in range(2)]

    weights_in, dve = k.sem("m0_weights_in"), k.sem("m0_dve")
    a_ready, rows_out = k.sem("m0_a_ready"), k.sem("m0_rows_out")
    t_ready, aT_ready = k.sem("m0_t_ready"), k.sem("m0_aT_ready")
    rt_mm, rt_out, r_mm, r_out = k.sem("m0_rt_mm"), k.sem("m0_rt_out"), k.sem("m0_r_mm"), k.sem("m0_r_out")
    top_ready, exp_ready = k.sem("m0_top_ready"), k.sem("m0_exp_ready")
    up_mm, act_done, hid_ready = k.sem("m0_up_mm"), k.sem("m0_act_done"), k.sem("m0_hid_ready")
    down_mm, added = k.sem("m0_down_mm"), k.sem("m0_added")
    WEIGHTS = 16 * 4

    with k.nc.Block() as block:
        @block.sync
        def _(sp):
            sp.sem_inc(rows_out, FIRST)
            sp.dma_start(wg[:, :, :], row_chunks(d["wg"])).then_inc(weights_in, 16)
            sp.dma_start(ws1[:, :, :], row_chunks(d["ws1"])).then_inc(weights_in, 16)
            sp.dma_start(ws3[:, :, :], row_chunks(d["ws3"])).then_inc(weights_in, 16)
            full = SHARED // P
            sp.dma_start(ws2[:, 0:full, :], row_chunks(d["ws2"][0:full * P, :])).then_inc(weights_in, 16)
            sp.dma_start(ws2[0:SHARED - full * P, full, :], d["ws2"][full * P:, :]).then_inc(weights_in, 16)
            with sp.Fori(0, GROUPS) as g:
                sp.wait_ge(a_ready, g + 1)
                sp.dma_start(r.rows[bass.ds(g * GN, GN), :].rearrange("(j p) n -> p j n", p=P), a[:, :, :])\
                    .then_inc(rows_out, 16)
            sp.wait_ge(rows_out, FIRST + 16 * GROUPS)

        @block.gpsimd
        def _(pool):
            with pool.Fori(0, GROUPS) as g:
                norm_gpsimd(pool, k, norm, g)
            routing_constants(pool, r, w)
            routing_scatter(pool, r, w)

        @block.vector
        def _(v):
            v.sem_inc(hid_ready, FIRST)
            v.sem_inc(added, FIRST)
            steps = Steps(v, dve)
            with steps.loop(GROUPS, 2 * GT) as g:
                wait_alone(v, t_ready, FIRST + g * KC, norm.passed)
                wait_alone(v, rows_out, FIRST + 16 * g, norm.passed)
                norm_vector(v, steps, norm, g, lambda j: tile_of(h, g, j), lambda j: a[:, j, :])\
                    .then_inc(a_ready, 1)
            v.wait_ge(r_out, FIRST + GROUPS)
            steps.note(v.tensor_reduce(smax[:, :, 0], w.scores[:, :, :], AX.X, ALU.max))
            steps.settle()
            v.tensor_tensor(w.scores[:, :, :], w.scores[:, :, :], smax[:, :, :].to_broadcast([P, TILES, E0]),
                            ALU.subtract).then_inc(top_ready, 1)
            v.wait_ge(exp_ready, 1)
            steps.note(v.tensor_reduce(ssum[:, :, 0], w.scores[:, :, :], AX.X, ALU.add))
            steps.settle()
            steps.note(v.reciprocal(ssum[:, :, :], ssum[:, :, :]))
            steps.settle()
            steps.note(v.tensor_tensor(w.scores[:, :, :], w.scores[:, :, :],
                                       ssum[:, :, :].to_broadcast([P, TILES, E0]), ALU.mult))
            steps.note(v.memset(sets[:, :, SETS0:8], -1.0))
            steps.settle()
            steps.note(v.tensor_reduce(sets[:, :, 0:SETS0], w.scores[:, :, :].rearrange("p t (s e) -> p t s e", s=SETS0),
                                       AX.X, ALU.max))
            steps.settle()
            for t in range(TILES):
                steps.note(v.max(set_best[:, t, :], sets[:, t, :]))
            steps.settle()
            for t in range(TILES):
                steps.note(v.max_index(set_index[:, t, :], set_best[:, t, :], sets[:, t, :]))
            v.wait_ge(w.made, ROUTING_MADE)
            steps.settle()
            steps.note(v.tensor_copy(set_indexf[:, :, :], set_index[:, :, :]))
            steps.settle()
            for c, o in ((0, open0), (1, open1)):
                steps.note(v.tensor_tensor(o[:, :, :], set_indexf[:, :, c:c + 1].to_broadcast([P, TILES, SETS0]),
                                           w.iota_e[:, :, 0:SETS0].to_broadcast([P, TILES, SETS0]), ALU.is_equal))
            steps.settle()
            steps.note(v.tensor_tensor(open0[:, :, :], open0[:, :, :], open1[:, :, :], ALU.add))
            steps.settle()
            steps.note(v.tensor_scalar(open0[:, :, :], open0[:, :, :], 2.0, -2.0, ALU.mult, ALU.add))
            steps.settle()
            each = E0 // SETS0
            steps.note(v.tensor_tensor(
                allowed[:, :, :].rearrange("p t (s e) -> p (t s) e", s=SETS0),
                w.scores[:, :, :].rearrange("p t (s e) -> p (t s) e", s=SETS0),
                open0[:, :, :].rearrange("p t (s e) -> p (t s) e", e=1).to_broadcast([P, TILES * SETS0, each]),
                ALU.add))
            steps.settle()
            for t in range(TILES):
                steps.note(v.max(r.best[:, t, :], allowed[:, t, :]))
            steps.settle()
            for t in range(TILES):
                steps.note(v.max_index(w.index[:, t, :], r.best[:, t, :], allowed[:, t, :]))
            steps.settle()
            routing_vector(v, steps, r, w)
            routing_slots(v, steps, r, w, ps_r[:, 0:TILES * E0], ps_q[:, 0:TILES * E0])

            def shared_vector(i):
                for m, (c, size) in enumerate(mids):
                    v.wait_ge(act_done, i * nm + (m + 1))
                    v.tensor_tensor(hidT[0:size, m, :], act_up[0:size, m % 2, :], ps_a[m % 2][0:size, 1, :],
                                    ALU.mult).then_inc(hid_ready, 1)
                for j in range(GT):
                    v.wait_ge(down_mm, i * GT + (j + 1))
                    t = tile_of(h, i, j)
                    v.tensor_tensor(t, ps_d[j % 2][:, :], t, ALU.add).then_inc(added, 1)

            with v.Fori(0, GROUPS) as i:
                shared_vector(i)
            v.wait_ge(w.map_in, 16)
            v.tensor_copy(w.mapf[:, :], w.map[:, :]).then_inc(w.map_ready, 1)
            v.wait_ge(w.map_turned, 1)
            v.tensor_copy(r.token[:, :], ps_r[:, 0:2 * r.blocks]).then_inc(w.token_ready, 1)

        @block.scalar
        def _(act):
            act.sem_inc(aT_ready, FIRST)
            act.sem_inc(r_out, FIRST)
            with act.Fori(0, GROUPS) as g:
                for half in range(2):
                    act.wait_ge(t_ready, FIRST + g * KC + (2 * half + 2))
                    act.copy(aT[:, 2 * half:2 * half + 2, bass.ds(g * GN, GN)], ps_a[half][:, :, :])\
                        .then_inc(aT_ready, 1)
                act.wait_ge(rt_mm, g + 1)
                act.copy(scoresT[:, :], ps_r[0:E0, :]).then_inc(rt_out, 1)
                act.wait_ge(r_mm, g + 1)
                act.copy(w.scores[:, bass.ds(g * GT, GT), :],
                         ps_q[:, 0:GT * E0].rearrange("p (t e) -> p t e", t=GT)).then_inc(r_out, 1)
            act.wait_ge(top_ready, 1)
            act.activation(w.scores[:, :, :], w.scores[:, :, :], ACT.Exp).then_inc(exp_ready, 1)
            with act.Fori(0, GROUPS) as g:
                for m, (c, size) in enumerate(mids):
                    act.wait_ge(up_mm, g * nm + (m + 1))
                    if m < 2:
                        act.wait_ge(hid_ready, FIRST + g * nm)
                    act.activation(act_up[0:size, m % 2, :], ps_a[m % 2][0:size, 0, :], ACT.Silu)\
                        .then_inc(act_done, 1)

        @block.tensor
        def _(pe):
            pe.sem_inc(t_ready, FIRST)
            pe.wait_ge(weights_in, WEIGHTS + 16)
            with pe.Fori(0, GROUPS) as g:
                pe.wait_ge(a_ready, g + 1)
                pe.wait_ge(aT_ready, FIRST + 2 * g)
                for c in range(KC):
                    for j in range(GT):
                        last = pe.transpose(ps_a[c // 2][:, c % 2, j * P:(j + 1) * P], a[:, j, c * P:(c + 1) * P],
                                            k.ident[:, :])
                    last.then_inc(t_ready, 1)
                pe.wait_ge(aT_ready, FIRST + 2 * g + 2)
                for c in range(KC):
                    mm = pe.matmul(ps_r[0:E0, :], wg[:, c, :], aT[:, c, bass.ds(g * GN, GN)],
                                   start=(c == 0), stop=(c == KC - 1))
                mm.then_inc(rt_mm, 1)
                wait_alone(pe, rt_out, g + 1, k.passed_pe)
                wait_alone(pe, r_out, FIRST + g, k.passed_pe)
                for j in range(GT):
                    last = pe.transpose(ps_q[:, j * E0:(j + 1) * E0], scoresT[:, j * P:(j + 1) * P],
                                        k.ident[0:E0, 0:E0])
                last.then_inc(r_mm, 1)

            def shared(g):
                for m, (c, size) in enumerate(mids):
                    wait_alone(pe, hid_ready, FIRST + g * nm + max(m - 1, 0), k.passed_pe)
                    for side, ws in enumerate((ws1, ws3)):
                        for a_ in range(KC):
                            mm = pe.matmul(ps_a[m % 2][0:size, side, :], ws[:, a_, c:c + size],
                                           aT[:, a_, bass.ds(g * GN, GN)], start=(a_ == 0), stop=(a_ == KC - 1))
                    mm.then_inc(up_mm, 1)
                for j in range(GT):
                    pe.wait_ge(added, FIRST + g * GT + max(j - 1, 0))
                    for m, (c, size) in enumerate(mids):
                        if j == 0:
                            pe.wait_ge(hid_ready, FIRST + g * nm + (m + 1))
                        mm = pe.matmul(ps_d[j % 2][:, :], hidT[0:size, m, j * P:(j + 1) * P], ws2[0:size, m, :],
                                       start=(m == 0), stop=(m == nm - 1))
                    mm.then_inc(down_mm, 1)

            pe.wait_ge(aT_ready, FIRST + 2 * GROUPS)
            pe.wait_ge(r_out, FIRST + GROUPS)
            routing_tensor(pe, r, w, ps_r[:, 0:TILES * E0], ps_q[:, 0:TILES * E0])
            with pe.Fori(0, GROUPS) as g:
                shared(g)
            pe.wait_ge(w.map_ready, 1)
            pe.transpose(ps_r[:, 0:2 * r.blocks], w.mapf[:, :], k.ident[0:2 * r.blocks, 0:2 * r.blocks])\
                .then_inc(w.map_turned, 1)


def mixture_first_experts(k, d):
    experts(k, d, k.route0, MID0, True)


def mixture_first_combine(k, d):
    combine(k, k.route0)


HEADS2, HC2 = 2, 2
ATT1_SCALE = (HC2 * P) ** -0.5


def attention_second(k, d):
    h = k.h
    raw = {n: k.sb(f"raw_{n}", [P, KC, D], BF16) for n in "qkvo"}
    wt = {n: k.sb(f"w2_{n}", [P, KC, D], F32R) for n in "qkvo"}
    bq16, bk16 = k.sb("bq16", [P, KC], BF16), k.sb("bk16", [P, KC], BF16)
    bv16, bo16 = k.sb("bv16", [P, D], BF16), k.sb("bo16", [P, D], BF16)
    bias_q, bias_k = k.sb("bias_q", [P, KC]), k.sb("bias_k", [P, KC])
    norm = Norm(k, "norm4")
    a = k.sb("a2_a", [P, GT, D])
    aT, aT_rest = k.sb("a2_aT", [P, KC, GN], F32R), k.sb("a2_aT_rest", [P, KC, GN], F32R)
    qT = k.sb("a2_qT", [P, KC, GN])
    kT = k.sb("a2_kT", [P, KC, GN])
    vals = k.sb("a2_vals", [P, GT, D])
    top = k.sb("a2_top", [P, 2, HEADS2, 1])
    prob = k.sb("a2_prob", [P, 2, HEADS2, P])
    probT = k.sb("a2_probT", [P, 2, HEADS2, P])
    rsum = k.sb("a2_rsum", [P, 2, HEADS2, 1])
    o = k.sb("a2_o", [P, 2, D])
    oT, oT_rest = k.sb("a2_oT", [P, KC, P], F32R), k.sb("a2_oT_rest", [P, KC, P], F32R)
    res = k.sb("a2_res", [P, 2, D])
    ps_a = [k.ps(f"a2_ps_a{i}", [P, GN]) for i in range(4)]
    ps_m = [k.ps(f"a2_ps_m{i}", [P, GN]) for i in range(4)]

    weights_in, cast = k.sem("a2_weights_in"), k.sem("a2_cast")
    dve = k.sem("a2_dve")
    a_ready, t_ready, aT_ready = k.sem("a2_a_ready"), k.sem("a2_t_ready"), k.sem("a2_aT_ready")
    qk_mm, qk_done = k.sem("a2_qk_mm"), k.sem("a2_qk_done")
    v_mm, v_added, v_done = k.sem("a2_v_mm"), k.sem("a2_v_added"), k.sem("a2_v_done")
    s_ready, shifted, exp_done = k.sem("a2_s_ready"), k.sem("a2_shifted"), k.sem("a2_exp_done")
    pt_ready, pt_done = k.sem("a2_pt_ready"), k.sem("a2_pt_done")
    pv_ready, o_done = k.sem("a2_pv_ready"), k.sem("a2_o_done")
    ot_ready, ot_done, ot_rest = k.sem("a2_ot_ready"), k.sem("a2_ot_done"), k.sem("a2_ot_rest")
    aT_rest_ready = k.sem("a2_aT_rest_ready")
    wo_ready, wo_read = k.sem("a2_wo_ready"), k.sem("a2_wo_read")
    QK = 2 * KC

    with k.nc.Block() as block:
        @block.sync
        def _(sp):
            for n in "qkvo":
                sp.dma_start(raw[n][:, :, :], row_chunks(d["w2" + n])).then_inc(weights_in, 16)
            for dst, src in ((bq16, d["b2q"]), (bk16, d["b2k"]), (bv16, d["b2v"].to_broadcast([P, D])),
                             (bo16, d["b2o"].to_broadcast([P, D]))):
                sp.dma_start(dst[:, :], src).then_inc(weights_in, 16)

        WEIGHTS = 16 * 8

        @block.gpsimd
        def _(pool):
            with pool.Fori(0, GROUPS) as g:
                norm_gpsimd(pool, k, norm, g)

        @block.vector
        def _(v):
            v.sem_inc(o_done, FIRST)
            v.sem_inc(wo_read, FIRST)
            v.sem_inc(v_added, FIRST)
            v.sem_inc(shifted, FIRST)
            v.sem_inc(ot_rest, FIRST)
            steps = Steps(v, dve)

            def normalise(g, first):
                if not first:
                    wait_alone(v, t_ready, g * KC, norm.passed)
                norm_vector(v, steps, norm, g, lambda j: tile_of(h, g, j), lambda j: a[:, j, :]).then_inc(a_ready, 1)

            def turn_rest(g):
                for c in range(KC):
                    v.wait_ge(aT_ready, g * KC + (c + 1))
                    v.tensor_tensor(aT_rest[:, c, :], ps_a[c][:, :], aT[:, c, :], ALU.subtract)\
                        .then_inc(aT_rest_ready, 1)

            def heads_rest(g, b):
                v.wait_ge(ot_done, FIRST + g * GT + (b + 1))
                v.tensor_tensor(oT_rest[:, :, :], ps_m[1][:, :].rearrange("p (c n) -> p c n", c=KC), oT[:, :, :],
                                ALU.subtract).then_inc(ot_rest, 1)

            def shift(g, b):
                s = ps_a[b % 2][:, 0:HEADS2 * P].rearrange("p (h n) -> p h n", h=HEADS2)
                v.wait_ge(s_ready, g * GT + (b + 1))
                steps.note(v.tensor_reduce(top[:, b % 2, :, 0], s, AX.X, ALU.max))
                steps.settle()
                v.tensor_tensor(prob[:, b % 2, :, :], s, top[:, b % 2, :, :].to_broadcast([P, HEADS2, P]),
                                ALU.subtract).then_inc(shifted, 1)

            def divide(g, b):
                v.wait_ge(exp_done, g * GT + (b + 1))
                steps.note(v.tensor_reduce(rsum[:, b % 2, :, 0], prob[:, b % 2, :, :], AX.X, ALU.add))
                steps.settle()
                steps.note(v.reciprocal(rsum[:, b % 2, :, :], rsum[:, b % 2, :, :]))
                steps.settle()
                v.wait_ge(pv_ready, g * GT + (b + 1))
                v.tensor_tensor(o[:, b % 2, :].rearrange("p (h n) -> p h n", h=HEADS2),
                                ps_m[0][:, :].rearrange("p (h n) -> p h n", h=HEADS2),
                                rsum[:, b % 2, :, :].to_broadcast([P, HEADS2, HC2 * P]), ALU.mult).then_inc(o_done, 1)

            def residual(g, b):
                v.wait_ge(wo_ready, g * GT + (b + 1))
                v.tensor_tensor(res[:, b % 2, :], ps_m[2][:, :], bo16[:, :], ALU.add).then_inc(wo_read, 1)
                v.wait_ge(wo_read, FIRST + g * GT + (b + 1))
                t = tile_of(h, g, b)
                steps.note(v.scalar_tensor_tensor(out=t, in0=res[:, b % 2, :], scalar=0.0, in1=t,
                                                  op0=ALU.max, op1=ALU.add))

            def group(g, last):
                if not last:
                    normalise(g + 1, False)
                for j in range(GT):
                    v.wait_ge(v_mm, g * GT + (j + 1))
                    v.tensor_tensor(vals[:, j, :], ps_m[j][:, :], bv16[:, :], ALU.add).then_inc(v_added, 1)
                if not last:
                    turn_rest(g + 1)
                shift(g, 0)
                shift(g, 1)
                for b in range(GT):
                    if b >= 1:
                        heads_rest(g, b - 1)
                    divide(g, b)
                    if b + 2 < GT:
                        shift(g, b + 2)
                    if b >= 1:
                        residual(g, b - 1)
                heads_rest(g, GT - 1)
                residual(g, GT - 1)

            v.wait_ge(weights_in, WEIGHTS)
            normalise(0, True)
            turn_rest(0)
            with steps.loop(GROUPS - 1, 6 * GT) as g:
                group(g, False)
            group(GROUPS - 1, True)

        @block.scalar
        def _(act):
            act.sem_inc(ot_done, FIRST)
            act.sem_inc(pt_done, FIRST)
            act.wait_ge(weights_in, WEIGHTS)
            for n in "qkvo":
                act.copy(wt[n][:, :, :], raw[n][:, :, :]).then_inc(cast, 1)
            act.copy(bias_q[:, :], bq16[:, :]).then_inc(cast, 1)
            act.copy(bias_k[:, :], bk16[:, :]).then_inc(cast, 1)
            act.wait_ge(cast, 6)

            def turn(g):
                for c in range(KC):
                    act.wait_ge(t_ready, g * KC + (c + 1))
                    act.copy(aT[:, c, :], ps_a[c][:, :]).then_inc(aT_ready, 1)

            def group(g, last):
                for c in range(QK):
                    act.wait_ge(qk_mm, g * QK + (c + 1))
                    out, bias = (qT, bias_q) if c < KC else (kT, bias_k)
                    act.activation(out[:, c % KC, :], ps_m[c % 4][:, :], ACT.Relu, bias=bias[:, c % KC:c % KC + 1])\
                        .then_inc(qk_done, 1)
                for j in range(GT):
                    act.wait_ge(v_added, FIRST + g * GT + (j + 1))
                    act.activation(vals[:, j, :], vals[:, j, :], ACT.Relu).then_inc(v_done, 1)
                if not last:
                    turn(g + 1)

                def exponent(b):
                    act.wait_ge(shifted, FIRST + g * GT + (b + 1))
                    act.activation(prob[:, b % 2, :, :], prob[:, b % 2, :, :], ACT.Exp, scale=ATT1_SCALE)\
                        .then_inc(exp_done, 1)

                def turned_heads(b):
                    act.wait_ge(ot_ready, g * GT + (b + 1))
                    act.copy(oT[:, :, :], ps_m[1][:, :].rearrange("p (c n) -> p c n", c=KC)).then_inc(ot_done, 1)

                exponent(0)
                exponent(1)
                for b in range(GT):
                    act.wait_ge(pt_ready, g * GT + (b + 1))
                    act.copy(probT[:, b % 2, :, :], ps_a[2 + b % 2][:, 0:HEADS2 * P]
                             .rearrange("p (h n) -> p h n", h=HEADS2)).then_inc(pt_done, 1)
                    if b >= 1:
                        turned_heads(b - 1)
                    if b + 2 < GT:
                        act.wait_ge(o_done, FIRST + g * GT + (b + 1))
                        exponent(b + 2)
                turned_heads(GT - 1)

            turn(0)
            with act.Fori(0, GROUPS - 1) as g:
                group(g, False)
            group(GROUPS - 1, True)

        @block.tensor
        def _(pe):
            def turn(g, first):
                pe.wait_ge(a_ready, g + 1)
                if not first:
                    pe.wait_ge(shifted, FIRST + (g - 1) * GT)
                    pe.wait_ge(pt_done, FIRST + (g - 1) * GT)
                for c in range(KC):
                    for j in range(GT):
                        last = pe.transpose(ps_a[c][:, j * P:(j + 1) * P], a[:, j, c * P:(c + 1) * P], k.ident[:, :])
                    last.then_inc(t_ready, 1)

            def project(g):
                pe.wait_ge(aT_rest_ready, (g + 1) * KC)
                pe.wait_ge(ot_rest, FIRST + g * GT)
                pe.wait_ge(o_done, FIRST + g * GT)
                pe.wait_ge(ot_done, FIRST + g * GT)
                pe.wait_ge(wo_read, FIRST + g * GT)
                pe.wait_ge(v_added, FIRST + g * GT)
                for c in range(QK):
                    if c >= 4:
                        pe.wait_ge(qk_done, g * QK + (c - 3))
                    w = wt["q"] if c < KC else wt["k"]
                    for i in range(KC):
                        for part in (aT, aT_rest):
                            mm = pe.matmul(ps_m[c % 4][:, :], w[:, i, (c % KC) * P:(c % KC + 1) * P], part[:, i, :],
                                           start=(i == 0 and part is aT), stop=(i == KC - 1 and part is aT_rest))
                    mm.then_inc(qk_mm, 1)
                for j in range(GT):
                    pe.wait_ge(qk_done, g * QK + (KC + 1 + j))
                    for i in range(KC):
                        for part in (aT, aT_rest):
                            mm = pe.matmul(ps_m[j][:, :], part[:, i, j * P:(j + 1) * P], wt["v"][:, i, :],
                                           start=(i == 0 and part is aT), stop=(i == KC - 1 and part is aT_rest))
                    mm.then_inc(v_mm, 1)

            def scores(g, b):
                if b >= 2:
                    pe.wait_ge(shifted, FIRST + g * GT + (b - 1))
                for hh in range(HEADS2):
                    for c in range(HC2):
                        mm = pe.matmul(ps_a[b % 2][:, hh * P:(hh + 1) * P], qT[:, HC2 * hh + c, b * P:(b + 1) * P],
                                       kT[:, HC2 * hh + c, b * P:(b + 1) * P], start=(c == 0), stop=(c == HC2 - 1))
                mm.then_inc(s_ready, 1)

            def turn_probs(g, b):
                pe.wait_ge(exp_done, g * GT + (b + 1))
                for hh in range(HEADS2):
                    last = pe.transpose(ps_a[2 + b % 2][:, hh * P:(hh + 1) * P], prob[:, b % 2, hh, :], k.ident[:, :])
                last.then_inc(pt_ready, 1)

            def turn_heads(g, b):
                pe.wait_ge(o_done, FIRST + g * GT + (b + 1))
                for c in range(KC):
                    last = pe.transpose(ps_m[1][:, c * P:(c + 1) * P], o[:, b % 2, c * P:(c + 1) * P], k.ident[:, :])
                last.then_inc(ot_ready, 1)

            def weigh(g, b):
                pe.wait_ge(pt_done, FIRST + g * GT + (b + 1))
                if b == 0:
                    pe.wait_ge(v_done, (g + 1) * GT)
                for hh in range(HEADS2):
                    mm = pe.matmul(ps_m[0][:, hh * HC2 * P:(hh + 1) * HC2 * P], probT[:, b % 2, hh, :],
                                   vals[:, b, hh * HC2 * P:(hh + 1) * HC2 * P], start=True, stop=True)
                mm.then_inc(pv_ready, 1)

            def output(g, b):
                pe.wait_ge(ot_rest, FIRST + g * GT + (b + 1))
                if b >= 1:
                    pe.wait_ge(wo_read, FIRST + g * GT + b)
                for part in (oT, oT_rest):
                    for c in range(KC):
                        mm = pe.matmul(ps_m[2][:, :], part[:, c, :], wt["o"][:, c, :],
                                       start=(c == 0 and part is oT), stop=(c == KC - 1 and part is oT_rest))
                mm.then_inc(wo_ready, 1)

            def group(g, last):
                project(g)
                if not last:
                    turn(g + 1, False)
                    pe.wait_ge(aT_rest_ready, (g + 2) * KC)
                pe.wait_ge(qk_done, (g + 1) * QK)
                scores(g, 0)
                scores(g, 1)
                for b in range(GT + 1):
                    if b < GT:
                        turn_probs(g, b)
                    if b + 2 < GT:
                        scores(g, b + 2)
                    if b >= 1:
                        turn_heads(g, b - 1)
                    if b < GT:
                        weigh(g, b)
                    if b >= 1:
                        output(g, b - 1)

            pe.wait_ge(cast, 6)
            turn(0, True)
            with pe.Fori(0, GROUPS - 1) as g:
                group(g, False)
            group(GROUPS - 1, True)


def mixture_second_route(k, d):
    h, r = k.h, k.route1
    r.weight = k.route1_weight
    wg1 = k.sb("wg1", [P, KC, E1])
    wg2 = k.sb("wg2", [E1, E1])
    norm = Norm(k, "norm5")
    a = k.sb("m1_a", [P, GT, D])
    aT = k.sb("m1_aT", [P, KC, GN])
    tanhT = k.sb("m1_tanhT", [E1, GN])
    w = RoutingWork(k, r)
    gap = k.sb("m1_gap", [P, TILES, 1])
    ps_a = [k.ps(f"m1_ps_a{i}", [P, GN]) for i in range(4)]
    ps_r = k.ps("m1_ps_r", [P, GN])
    ps_q = k.ps("m1_ps_q", [P, GN])
    weights_in, dve = k.sem("m1_weights_in"), k.sem("m1_dve")
    a_ready, rows_out = k.sem("m1_a_ready"), k.sem("m1_rows_out")
    t_ready, aT_ready = k.sem("m1_t_ready"), k.sem("m1_aT_ready")
    rt_mm, rt_out, r_mm, r_out = k.sem("m1_rt_mm"), k.sem("m1_rt_out"), k.sem("m1_r_mm"), k.sem("m1_r_out")
    gap_ready, exp_ready = k.sem("m1_gap_ready"), k.sem("m1_exp_ready")

    with k.nc.Block() as block:
        @block.sync
        def _(sp):
            sp.sem_inc(rows_out, FIRST)
            sp.dma_start(wg1[:, :, :], row_chunks(d["wg1"])).then_inc(weights_in, 16)
            sp.dma_start(wg2[:, :], d["wg2"]).then_inc(weights_in, 16)
            with sp.Fori(0, GROUPS) as g:
                sp.wait_ge(a_ready, g + 1)
                sp.dma_start(r.rows[bass.ds(g * GN, GN), :].rearrange("(j p) n -> p j n", p=P), a[:, :, :])\
                    .then_inc(rows_out, 16)
            sp.wait_ge(rows_out, FIRST + 16 * GROUPS)

        @block.gpsimd
        def _(pool):
            with pool.Fori(0, GROUPS) as g:
                norm_gpsimd(pool, k, norm, g)
            routing_constants(pool, r, w)
            routing_scatter(pool, r, w)

        @block.vector
        def _(v):
            steps = Steps(v, dve)
            with steps.loop(GROUPS, 2 * GT) as g:
                wait_alone(v, t_ready, FIRST + g * KC, norm.passed)
                wait_alone(v, rows_out, FIRST + 16 * g, norm.passed)
                norm_vector(v, steps, norm, g, lambda j: tile_of(h, g, j), lambda j: a[:, j, :])\
                    .then_inc(a_ready, 1)
            v.wait_ge(r_out, FIRST + GROUPS)
            for t in range(TILES):
                steps.note(v.max(r.best[:, t, :], w.scores[:, t, :]))
            steps.settle()
            for t in range(TILES):
                steps.note(v.max_index(w.index[:, t, :], r.best[:, t, :], w.scores[:, t, :]))
            v.tensor_tensor(gap[:, :, :], r.best[:, :, 1:2], r.best[:, :, 0:1], ALU.subtract).then_inc(gap_ready, 1)
            v.wait_ge(w.made, ROUTING_MADE)
            steps.settle()
            routing_vector(v, steps, r, w)
            v.wait_ge(exp_ready, 1)
            steps.note(v.tensor_scalar(r.weight[:, :, 1:2], gap[:, :, :], 1.0, None, ALU.add))
            steps.settle()
            steps.note(v.reciprocal(r.weight[:, :, 0:1], r.weight[:, :, 1:2]))
            steps.settle()
            steps.note(v.tensor_tensor(r.weight[:, :, 1:2], gap[:, :, :], r.weight[:, :, 0:1], ALU.mult))
            routing_slots(v, steps, r, w, ps_r[:, 0:TILES * E1], ps_q[:, 0:TILES * E1])
            v.wait_ge(w.map_in, 16)
            v.tensor_copy(w.mapf[:, :], w.map[:, :]).then_inc(w.map_ready, 1)
            v.wait_ge(w.map_turned, 1)
            v.tensor_copy(r.token[:, :], ps_r[:, 0:2 * r.blocks]).then_inc(w.token_ready, 1)

        @block.scalar
        def _(act):
            act.sem_inc(aT_ready, FIRST)
            act.sem_inc(r_out, FIRST)
            with act.Fori(0, GROUPS) as g:
                for c in range(KC):
                    act.wait_ge(t_ready, FIRST + g * KC + (c + 1))
                    act.copy(aT[:, c, :], ps_a[c][:, :]).then_inc(aT_ready, 1)
                act.wait_ge(rt_mm, g + 1)
                act.activation(tanhT[:, :], ps_r[0:E1, :], ACT.Tanh).then_inc(rt_out, 1)
                act.wait_ge(r_mm, g + 1)
                act.copy(w.scores[:, bass.ds(g * GT, GT), :],
                         ps_q[:, 0:GT * E1].rearrange("p (t e) -> p t e", t=GT)).then_inc(r_out, 1)
            act.wait_ge(gap_ready, 1)
            act.activation(gap[:, :, :], gap[:, :, :], ACT.Exp).then_inc(exp_ready, 1)

        @block.tensor
        def _(pe):
            pe.sem_inc(t_ready, FIRST)
            pe.wait_ge(weights_in, 32)
            with pe.Fori(0, GROUPS) as g:
                pe.wait_ge(a_ready, g + 1)
                pe.wait_ge(aT_ready, FIRST + g * KC)
                for c in range(KC):
                    for j in range(GT):
                        last = pe.transpose(ps_a[c][:, j * P:(j + 1) * P], a[:, j, c * P:(c + 1) * P], k.ident[:, :])
                    last.then_inc(t_ready, 1)
                wait_alone(pe, aT_ready, FIRST + (g + 1) * KC, k.passed_pe)
                for c in range(KC):
                    mm = pe.matmul(ps_r[0:E1, :], wg1[:, c, :], aT[:, c, :], start=(c == 0), stop=(c == KC - 1))
                mm.then_inc(rt_mm, 1)
                wait_alone(pe, rt_out, g + 1, k.passed_pe)
                wait_alone(pe, r_out, FIRST + g, k.passed_pe)
                for j in range(GT):
                    mm = pe.matmul(ps_q[:, j * E1:(j + 1) * E1], tanhT[:, j * P:(j + 1) * P], wg2[:, :],
                                   start=True, stop=True)
                mm.then_inc(r_mm, 1)
            pe.wait_ge(r_out, FIRST + GROUPS)
            routing_tensor(pe, r, w, ps_r[:, 0:TILES * E1], ps_q[:, 0:TILES * E1])
            pe.wait_ge(w.map_ready, 1)
            pe.transpose(ps_r[:, 0:2 * r.blocks], w.mapf[:, :], k.ident[0:2 * r.blocks, 0:2 * r.blocks])\
                .then_inc(w.map_turned, 1)


def mixture_second_experts(k, d):
    experts(k, d, k.route1, MID1, False)


def mixture_second_combine(k, d):
    combine(k, k.route1)


def program(nc, d, stages=9):
    with ExitStack() as whole:
        k = Core(nc, whole)
        k.h = k.sb("h", [P, TILES, D])
        k.x = k.sb("x", [P, TILES, D])
        k.passed_pool, k.passed_pe = k.sem("passed_pool"), k.sem("passed_pe")
        constants(k)
        k.route0 = Routing(k, "m0", E0, TOP0)
        k.route1 = Routing(k, "m1", E1, TOP1)
        k.route1_weight = k.sb("m1_weight", [P, TILES, TOP1])
        for n, stage in enumerate(STAGES):
            if n < stages:
                with k.stage():
                    stage(k, d)
        write_output(k, d)


STAGES = [attention_first, feed_forward, mixture_first_route, mixture_first_experts, mixture_first_combine,
          attention_second, mixture_second_route, mixture_second_experts, mixture_second_combine]


def columns(a):
    import numpy as np
    return np.ascontiguousarray(np.reshape(a, (-1, P)).T)


def layouts(inputs):
    import numpy as np
    i = {n: np.asarray(a) for n, a in inputs.items()}
    wkv, bkv = i["L0_attn_wkv"], i["L0_attn_bkv"]
    a = {
        "ids": columns(i["x"].reshape(-1)), "tok": i["L0_tok_weight"], "extra": i["L0_tok_extra"],
        "wq": i["L0_attn_wq"], "wk4": np.tile(wkv[:, :HD], (1, QUADS)), "wv": wkv[:, HD:], "wo": i["L0_attn_wo"],
        "ln1_g": columns(i["L0_attn_ln1_g"]), "ln1_b": columns(i["L0_attn_ln1_b"]),
        "ln2_g": columns(i["L0_attn_ln2_g"]), "ln2_b": columns(i["L0_attn_ln2_b"]),
        "bq": columns(i["L0_attn_bq"]), "bk4": np.tile(bkv[:HD], QUADS).reshape(P, 1),
        "bv": bkv[HD:].reshape(1, HD), "bo": i["L0_attn_bo"].reshape(1, D),
        "wfc": i["L0_attn_wfc"], "bfc": columns(i["L0_attn_bfc"]), "wproj": i["L0_attn_wproj"],
        "bproj": i["L0_attn_bproj"].reshape(1, D),
    }
    def ups(w):
        e, m, _ = w.shape
        return w.transpose(0, 2, 1).reshape(e, KC, P, m).transpose(0, 2, 1, 3)

    def downs(w):
        e, o, m = w.shape
        pad = -m % P
        w = np.concatenate([w.transpose(0, 2, 1), np.zeros((e, pad, o), w.dtype)], 1)
        return w.reshape(e, -1, P, o).transpose(0, 2, 1, 3).reshape(e, P, -1)

    a |= {
        "wg": i["L0_ffn_Wg"].T, "ws1": i["L0_ffn_Ws1"].T, "ws3": i["L0_ffn_Ws3"].T, "ws2": i["L0_ffn_Ws2"].T,
        "m0_up": np.concatenate([ups(i["L0_ffn_W1"]), ups(i["L0_ffn_W3"])], 3).reshape(E0, P, -1),
        "m0_down": downs(i["L0_ffn_W2"]),
    }
    for n in "qkvo":
        a["w2" + n] = i["L1_attn_W" + n].T
    a |= {
        "b2q": columns(i["L1_attn_bq"]), "b2k": columns(i["L1_attn_bk"]),
        "b2v": i["L1_attn_bv"].reshape(1, D), "b2o": i["L1_attn_bo"].reshape(1, D),
        "wg1": i["L1_ffn_Wg1"].T, "wg2": i["L1_ffn_Wg2"].T,
        "m1_up": ups(i["L1_ffn_Wup"]).reshape(E1, P, -1), "m1_down": downs(i["L1_ffn_Wdown"]),
        "m1_up_bias": i["L1_ffn_bup"].reshape(E1, -1, P).transpose(0, 2, 1), "m1_down_bias": i["L1_ffn_bdown"],
    }
    return {n: np.ascontiguousarray(b) for n, b in a.items()}


def kernel(**inputs):
    import concourse.bacc as bacc
    from concourse.bass_utils import run_bass_kernel_spmd

    nc = bacc.Bacc("TRN2", target_bir_lowering=False, num_devices=1)
    arrays = layouts(inputs)
    d = {n: nc.dram_tensor("in_" + n, a.shape, mybir.dt.from_np(a.dtype), kind="ExternalInput").ap()
         for n, a in arrays.items()}
    d["out"] = nc.dram_tensor("out", (TILES, P, D), F32, kind="ExternalOutput").ap()
    program(nc, d)
    result = run_bass_kernel_spmd(nc, [{"in_" + n: a for n, a in arrays.items()}], core_ids=[0])
    return result.results[0]["out"]
```

```python
import math
from contextlib import ExitStack, contextmanager

import concourse.bass as bass
from concourse import mybir
from concourse.alu_op_type import AluOpType as ALU

ACT = mybir.ActivationFunctionType
AX = mybir.AxisListType
F32 = mybir.dt.float32
F32R = mybir.dt.float32r
BF16 = mybir.dt.bfloat16
I32 = mybir.dt.int32
U32 = mybir.dt.uint32

P = 128
D = 512
KC = D // P
TILES = 16
GT = 4
GROUPS = TILES // GT
GN = GT * P
TOKENS = TILES * P
EPS = 1e-5

OVER_FIRST = 31996
HEADS, HD = 16, 32
QUADS = 4
UH = 8
UNITS = 2 * GT
AHEAD = 3
ATT0_SCALE = HD ** -0.5
MASKED = -1e30
INTER = 2048
IC = INTER // P
SC = 2
SLICES = IC // SC


FIRST = 1


class Steps:

    def __init__(self, engine, semaphore):
        self.engine, self.semaphore = engine, semaphore
        self.before, self.inside, self.turns = 0, 0, 0

    def note(self, instruction):
        instruction.then_inc(self.semaphore, 1)
        self.inside += 1

    def value(self):
        return self.turns + (self.before + self.inside)

    def settle(self, passed=None):
        self.engine.wait_ge(self.semaphore, self.value())
        if passed is not None:
            self.engine.sem_inc(passed, 1)

    @contextmanager
    def loop(self, count, each):
        self.before, self.inside = self.before + self.inside, 0
        with self.engine.Fori(0, count) as i:
            self.turns = i * each
            yield i
        assert self.inside == each, (self.inside, each)
        self.before, self.inside, self.turns = self.before + count * each, 0, 0


def wait_alone(engine, semaphore, value, passed):
    engine.wait_ge(semaphore, value)
    engine.sem_inc(passed, 1)


class Norm:

    def __init__(self, k, name):
        self.stats = k.sb(f"{name}_stats", [P, GT, 6])
        self.mv = k.sb(f"{name}_mean_var", [P, GT, 2])
        self.veps = k.sb(f"{name}_var_eps", [P, GT])
        self.rstd = k.sb(f"{name}_rstd", [P, GT])
        self.veps_ready = k.sem(f"{name}_veps_ready")
        self.rstd_ready = k.sem(f"{name}_rstd_ready")
        self.passed = k.sem(f"{name}_passed")


def norm_vector(v, steps, norm, turn, source, target):
    for j in range(GT):
        steps.note(v.bn_stats(norm.stats[:, j, :], source(j)))
    steps.settle(norm.passed)
    for j in range(GT):
        steps.note(v.bn_aggr(norm.mv[:, j, :], norm.stats[:, j, :]))
    steps.settle()
    v.tensor_scalar(norm.veps[:, :], norm.mv[:, :, 1], EPS, None, ALU.add).then_inc(norm.veps_ready, 1)
    v.wait_ge(norm.rstd_ready, turn + 1)
    for j in range(GT):
        last = v.tensor_scalar(target(j), source(j), norm.mv[:, j, 0:1], norm.rstd[:, j:j + 1],
                               ALU.subtract, ALU.mult)
    return last


def normalise_ahead(v, steps, norm, k, source):
    norm_vector(v, steps, norm, 0, lambda j: source[:, j, :], lambda j: k.a[:, j, :])


def norm_gpsimd(pool, k, norm, turn):
    pool.wait_ge(norm.veps_ready, turn + 1)
    pool.tensor_tensor(norm.rstd[:, :], norm.veps[:, :], k.minus_half[:, :], ALU.pow)\
        .then_inc(norm.rstd_ready, 1)


class Core:

    def __init__(self, nc, ctx):
        self.nc, self.whole, self.scope = nc, ctx, ctx
        self.semaphores = []

    def sb(self, name, shape, dt=F32):
        return self.scope.enter_context(self.nc.sbuf_tensor(name, shape, dt))

    def ps(self, name, shape, dt=F32):
        return self.scope.enter_context(self.nc.psum_tensor(name, shape, dt))

    def sem(self, name):
        semaphore = self.nc.alloc_semaphore(name=name)
        self.semaphores.append(semaphore)
        return semaphore

    @contextmanager
    def stage(self):
        self.semaphores = []
        with ExitStack() as scope:
            self.scope = scope
            yield
        self.scope = self.whole
        self.nc.clear_and_free_semaphores(self.semaphores)
        self.nc.all_engine_barrier()


def row_chunks(w):
    return w.rearrange("(c p) n -> p c n", p=P)


def constants(k):
    k.ident = k.sb("ident", [P, P])
    k.ident16 = k.sb("ident16", [P, P], BF16)
    k.minus_half = k.sb("minus_half", [P, GT])
    made = k.sem("constants_made")
    with k.nc.Block() as block:
        @block.gpsimd
        def _(pool):
            pool.memset(k.ident[:, :], 0.0).then_inc(made, 1)
            pool.memset(k.ident16[:, :], 0.0).then_inc(made, 1)
            pool.memset(k.minus_half[:, :], -0.5).then_inc(made, 1)
            pool.wait_ge(made, 3)
            for m in (k.ident, k.ident16):
                pool.affine_select(out=m[:, :], in_=m[:, :], compare_op=ALU.not_equal, fill=1.0, base=0,
                                   pattern=[[-1, P]], channel_multiplier=1).then_inc(made, 1)
            pool.wait_ge(made, 5)


PASSES = ((0, 0), (0, 1), (1, 0))


def attention_first(k, d):
    h, x = k.h, k.x
    wq = k.sb("wq", [P, KC, D])
    wk4 = k.sb("wk4", [P, KC, QUADS * HD])
    wv4 = k.sb("wv4", [P, KC, QUADS * HD])
    wo = k.sb("wo", [P, KC, D])
    ln_g = k.sb("ln1_g", [P, KC])
    ln_b = k.sb("ln1_b", [P, KC])
    bq = k.sb("bq", [P, KC])
    bk4 = k.sb("bk4", [P, 1])
    bv_rows = k.sb("bv_rows", [P, QUADS * HD])
    bo_rows = k.sb("bo_rows", [P, D])
    ids = k.sb("ids", [P, TILES], I32)
    over = k.sb("over", [P, TILES], I32)
    is_over = k.sb("is_over", [P, TILES], I32)
    mask = k.sb("mask", [P, GN], BF16)
    norm0, norm1, ahead = Norm(k, "norm0"), Norm(k, "norm1"), Norm(k, "ahead_ff")
    a = k.a
    aT = k.sb("aT", [P, KC, GN])
    two = lambda name, shape: [k.sb(f"{name}{part}", shape, F32R) for part in ("_part", "_rest")]
    aT_parts, oT = two("aT", [P, KC, GN]), two("oT", [P, KC, P])
    cut_weights = [(wq, two("wq", [P, KC, D])), (wk4, two("wk4", [P, KC, QUADS * HD])), (wo, two("wo", [P, KC, D]))]
    wq_parts, wk4_parts, wo_parts = (parts for _, parts in cut_weights)
    qT = k.sb("qT", [P, KC, GN])
    kT = k.sb("kT", [P, GN])
    vals = k.sb("vals", [P, GT, QUADS * HD])
    top = k.sb("top", [P, AHEAD, UH, 1])
    prob = k.sb("prob", [P, AHEAD, UH, P])
    probT = k.sb("probT", [P, 2, UH, P])
    rsum = k.sb("rsum", [P, AHEAD, UH, 1])

    ps_s = k.ps("ps_s", [P, 2, UH, P])
    ps_t = k.ps("ps_t", [P, UH, P])
    ps_m = [k.ps(f"ps_m{i}", [P, GN]) for i in range(2)]
    ps_a = ps_t[:, :, :].rearrange("p b c -> p (b c)")

    ids_in = k.sem("ids_in")
    weights_in = k.sem("att0_weights_in")
    over_ready = k.sem("over_ready")
    gathered = [k.sem(f"gathered{g}") for g in range(GROUPS)]
    mask_made = k.sem("mask_made")
    dve = k.sem("att0_dve")
    x0_ready, a_ready = k.sem("x0_ready"), k.sem("a_ready")
    residual_ready = k.sem("residual_ready")
    t_ready, aT_ready = k.sem("att0_t_ready"), k.sem("aT_ready")
    qk_mm, qk_done, v_mm, v_done = k.sem("qk_mm"), k.sem("qk_done"), k.sem("v_mm"), k.sem("v_done")
    s_ready, shifted, exp_done, prob_ready = (k.sem(n) for n in ("s_ready", "shifted", "exp_done", "prob_ready"))
    pt_ready, pt_done = k.sem("pt_ready"), k.sem("pt_done")
    pv_ready, o_done, o_rest = k.sem("pv_ready"), k.sem("o_done"), k.sem("o_rest")
    cut, cut_rest = k.sem("att0_cut"), k.sem("att0_cut_rest")
    aT_cut, aT_rest = k.sem("aT_cut"), k.sem("aT_rest")
    wo_ready, x1_done = k.sem("wo_ready"), k.sem("x1_done")

    with k.nc.Block() as block:
        @block.sync
        def _(sp):
            sp.dma_start(ids[:, :], d["ids"]).then_inc(ids_in, 16)
            for dst, src in ((ln_g, d["ln1_g"]), (ln_b, d["ln1_b"]), (bq, d["bq"]), (bk4, d["bk4"]),
                             (bv_rows, d["bv"].to_broadcast([P, QUADS * HD])), (bo_rows, d["bo"].to_broadcast([P, D]))):
                sp.dma_start(dst[:, :], src).then_inc(weights_in, 16)
            sp.wait_ge(gathered[0], 32 * GT)
            for dst, src in ((wq, row_chunks(d["wq"])), (wk4, row_chunks(d["wk4"])), (wv4, row_chunks(d["wv4"])),
                             (wo, row_chunks(d["wo"]))):
                sp.dma_start(dst[:, :, :], src).then_inc(weights_in, 16)

        WEIGHTS = 16 * 10

        @block.gpsimd
        def _(pool):
            pool.memset(mask[:, :], 0.0).then_inc(mask_made, 1)
            pool.wait_ge(mask_made, 1)
            pool.affine_select(out=mask[:, :], in_=mask[:, :], compare_op=ALU.is_ge, fill=MASKED, base=0,
                               pattern=[[0, GN // P], [-1, P]], channel_multiplier=1).then_inc(mask_made, 1)
            pool.wait_ge(over_ready, 2)

            def gather(g):
                for t in range(g * GT, (g + 1) * GT):
                    pool.indirect_dma_start(h[:, t, :], None, d["tok"], bass.IndirectOffsetOnAxis(
                        ap=ids[:, t:t + 1].bitcast(U32), axis=0)).then_inc(gathered[g], 16)
                    pool.indirect_dma_start(x[:, t, :], None, d["extra"], bass.IndirectOffsetOnAxis(
                        ap=over[:, t:t + 1].bitcast(U32), axis=0)).then_inc(gathered[g], 16)

            asked = {0: (1,), 1: range(2, GROUPS)}
            gather(0)
            for g in range(GROUPS):
                norm_gpsimd(pool, k, norm0, g)
                norm_gpsimd(pool, k, norm1, g)
                for n in asked.get(g, ()):
                    gather(n)
                if g == 0:
                    pool.wait_ge(weights_in, WEIGHTS)
                pool.wait_ge(a_ready, g + 1)
                for t in range(g * GT, (g + 1) * GT):
                    last = pool.tensor_tensor(x[:, t, :], x[:, t, :], bo_rows[:, :], ALU.add)
                last.then_inc(residual_ready, 1)
            norm_gpsimd(pool, k, ahead, 0)

        @block.vector
        def _(v):
            v.sem_inc(x1_done, FIRST)
            v.sem_inc(o_rest, FIRST)
            steps = Steps(v, dve)
            v.wait_ge(ids_in, 16)
            v.tensor_scalar(over[:, :], ids[:, :], OVER_FIRST, 0, ALU.subtract, ALU.max).then_inc(over_ready, 1)
            v.tensor_scalar(is_over[:, :], ids[:, :], OVER_FIRST, None, ALU.is_ge).then_inc(over_ready, 1)
            v.wait_ge(over_ready, 2)

            def replace(g):
                v.wait_ge(gathered[g], 32 * GT)
                for t in range(g * GT, (g + 1) * GT):
                    steps.note(v.copy_predicated(h[:, t, :], is_over[:, t:t + 1].to_broadcast([P, D]), x[:, t, :]))
                steps.settle()

            def tile(buf, g, j):
                return buf[:, bass.ds(g * GT + j, 1), :].rearrange("p a n -> p (a n)")

            def normalise(g, first):
                steps.note(norm_vector(v, steps, norm0, g, lambda j: tile(h, g, j), lambda j: tile(x, g, j)))
                steps.settle(norm0.passed)
                if not first:
                    wait_alone(v, t_ready, g * KC, norm1.passed)
                norm_vector(v, steps, norm1, g, lambda j: tile(x, g, j), lambda j: a[:, j, :])\
                    .then_inc(a_ready, 1)

            def rest_of_weights(n):
                came, parts = cut_weights[n]
                v.wait_ge(cut, n + 1)
                v.tensor_tensor(parts[1][:, :, :], came[:, :, :], parts[0][:, :, :], ALU.subtract)\
                    .then_inc(cut_rest, 1)

            def rest_of_turned(g):
                for c in range(KC):
                    v.wait_ge(aT_cut, g * KC + (c + 1))
                    v.tensor_tensor(aT_parts[1][:, c, :], aT[:, c, :], aT_parts[0][:, c, :], ALU.subtract)\
                        .then_inc(aT_rest, 1)

            def rest_of_heads(g, u):
                for r in range(2):
                    q = slice(HD * (2 * (u % 2) + r), HD * (2 * (u % 2) + r + 1))
                    v.wait_ge(o_done, 2 * (g * UNITS + u) + (r + 1))
                    v.tensor_tensor(oT[1][q, :, :], ps_m[r][q, :].rearrange("p (c n) -> p c n", c=KC), oT[0][q, :, :],
                                    ALU.subtract).then_inc(o_rest, 1)

            def shift(g, u):
                v.wait_ge(s_ready, g * UNITS + (u + 1))
                steps.note(v.tensor_reduce(top[:, u % AHEAD, :, 0], ps_s[:, u % 2, :, :], AX.X, ALU.max))
                steps.settle()
                v.tensor_scalar(top[:, u % AHEAD, :, :], top[:, u % AHEAD, :, :], -ATT0_SCALE, None, ALU.mult)\
                    .then_inc(shifted, 1)

            def divide(g, u):
                v.wait_ge(exp_done, g * UNITS + (u + 1))
                steps.note(v.tensor_reduce(rsum[:, u % AHEAD, :, 0], prob[:, u % AHEAD, :, :], AX.X, ALU.add))
                steps.settle()
                steps.note(v.reciprocal(rsum[:, u % AHEAD, :, :], rsum[:, u % AHEAD, :, :]))
                steps.settle()
                v.tensor_tensor(prob[:, u % AHEAD, :, :], prob[:, u % AHEAD, :, :],
                                rsum[:, u % AHEAD, :, :].to_broadcast([P, UH, P]), ALU.mult).then_inc(prob_ready, 1)

            def residual(g, b):
                v.wait_ge(wo_ready, g * GT + (b + 1))
                v.tensor_tensor(tile(x, g, b), ps_m[1][:, :], tile(x, g, b), ALU.add).then_inc(x1_done, 1)

            def group(g, last):
                if not last:
                    normalise(g + 1, False)
                else:
                    v.wait_ge(t_ready, GROUPS * KC)
                    v.wait_ge(x1_done, FIRST + GT)
                    normalise_ahead(v, steps, ahead, k, x)
                v.wait_ge(v_mm, g + 1)
                v.tensor_tensor(vals[:, :, :], ps_m[1][:, :].rearrange("p (t n) -> p t n", t=GT),
                                bv_rows[:, :].rearrange("p (t n) -> p t n", t=1).to_broadcast([P, GT, QUADS * HD]),
                                ALU.add).then_inc(v_done, 1)
                v.wait_ge(residual_ready, g + 1)
                shift(g, 0)
                shift(g, 1)
                divide(g, 0)
                shift(g, 2)
                for u in range(UNITS):
                    if u + 1 < UNITS:
                        divide(g, u + 1)
                    if u + AHEAD < UNITS:
                        shift(g, u + AHEAD)
                    if u % 2 == 0 and u >= 2:
                        residual(g, u // 2 - 1)
                    rest_of_heads(g, u)
                    if u == 1 and not last:
                        rest_of_turned(g + 1)
                residual(g, GT - 1)

            replace(0)
            normalise(0, True)
            v.wait_ge(weights_in, WEIGHTS)
            rest_of_weights(0)
            rest_of_weights(1)
            rest_of_turned(0)
            rest_of_weights(2)
            replace(1)
            group(0, False)
            for g in range(2, GROUPS):
                replace(g)
            with steps.loop(GROUPS - 2, 4 * GT + 1 + 3 * UNITS) as i:
                group(i + 1, False)
            group(GROUPS - 1, True)

        @block.scalar
        def _(act):
            act.wait_ge(weights_in, WEIGHTS)
            for came, parts in cut_weights:
                act.copy(parts[0][:, :, :], came[:, :, :]).then_inc(cut, 1)

            def turn(g, some):
                for c in some:
                    act.wait_ge(t_ready, g * KC + (c + 1))
                    act.activation(aT[:, c, :], ps_a[:, c % 2 * GN:(c % 2 + 1) * GN], ACT.Identity,
                                   bias=ln_b[:, c:c + 1], scale=ln_g[:, c:c + 1]).then_inc(aT_ready, 1)
                    act.wait_ge(aT_ready, g * KC + (c + 1))
                    act.copy(aT_parts[0][:, c, :], aT[:, c, :]).then_inc(aT_cut, 1)

            def group(g, last):
                for c in range(KC + 1):
                    act.wait_ge(qk_mm, g * (KC + 1) + (c + 1))
                    out, bias = (qT[:, c, :], bq[:, c:c + 1]) if c < KC else (kT[:, :], bk4[:, :])
                    act.activation(out, ps_m[c % 2][:, :], ACT.Identity, bias=bias).then_inc(qk_done, 1)

                def exponent(u):
                    act.wait_ge(shifted, g * UNITS + (u + 1))
                    for i in range(UH):
                        last = act.activation(prob[:, u % AHEAD, i, :], ps_s[:, u % 2, i, :], ACT.Exp,
                                              bias=top[:, u % AHEAD, i, :], scale=ATT0_SCALE)
                    last.then_inc(exp_done, 1)

                def heads(u):
                    for r in range(2):
                        q = slice(HD * (2 * (u % 2) + r), HD * (2 * (u % 2) + r + 1))
                        act.wait_ge(pv_ready, 2 * (g * UNITS + u) + (r + 1))
                        act.copy(oT[0][q, :, :], ps_m[r][q, :].rearrange("p (c n) -> p c n", c=KC)).then_inc(o_done, 1)

                exponent(0)
                if not last:
                    turn(g + 1, (0, 1))
                exponent(1)
                if not last:
                    turn(g + 1, (2, 3))
                for u in range(UNITS):
                    act.wait_ge(pt_ready, g * UNITS + (u + 1))
                    act.copy(probT[:, u % 2, :, :], ps_t[:, :, :]).then_inc(pt_done, 1)
                    if u + 2 < UNITS:
                        exponent(u + 2)
                    heads(u)

            turn(0, range(KC))
            with act.Fori(0, GROUPS - 1) as g:
                group(g, False)
            group(GROUPS - 1, True)

        @block.tensor
        def _(pe):
            def turn(g):
                pe.wait_ge(a_ready, g + 1)
                for c in range(KC):
                    if c >= 2:
                        pe.wait_ge(aT_ready, g * KC + (c - 1))
                    for j in range(GT):
                        last = pe.transpose(ps_a[:, c % 2 * GN + j * P:c % 2 * GN + (j + 1) * P],
                                            a[:, j, c * P:(c + 1) * P], k.ident[:, :])
                    last.then_inc(t_ready, 1)

            def project(g):
                pe.wait_ge(aT_rest, (g + 1) * KC)
                pe.wait_ge(o_rest, FIRST + g * 2 * UNITS)
                for c in range(KC + 1):
                    if c == 1:
                        pe.wait_ge(x1_done, FIRST + g * GT)
                    if c >= 2:
                        pe.wait_ge(qk_done, g * (KC + 1) + (c - 1))
                    for i in range(KC):
                        for n, (w, x_) in enumerate(PASSES):
                            ws = wq_parts[w][:, i, c * P:(c + 1) * P] if c < KC else wk4_parts[w][:, i, :]
                            last = pe.matmul(ps_m[c % 2][:, :], ws, aT_parts[x_][:, i, :], start=(i == 0 and n == 0),
                                             stop=(i == KC - 1 and n == len(PASSES) - 1))
                    last.then_inc(qk_mm, 1)
                pe.wait_ge(qk_done, g * (KC + 1) + 4)
                for j in range(GT):
                    for i in range(KC):
                        last = pe.matmul(ps_m[1][:, j * P:(j + 1) * P], aT[:, i, j * P:(j + 1) * P], wv4[:, i, :],
                                         start=(i == 0), stop=(i == KC - 1))
                last.then_inc(v_mm, 1)

            def scores(g, u):
                b = u // 2
                if u >= 2:
                    pe.wait_ge(exp_done, g * UNITS + (u - 1))
                for r in range(2):
                    q = 2 * (u % 2) + r
                    bank = ps_s[:, u % 2, 4 * r:4 * r + 4, :]
                    pe.matmul(bank, k.ident16[:, :], mask[:, :].rearrange("p (h n) -> p h n", h=4),
                              start=True, stop=False)
                    for m in range(KC):
                        last = pe.matmul(bank[:, m, :], qT[HD * q:HD * (q + 1), m, b * P:(b + 1) * P],
                                         kT[HD * q:HD * (q + 1), b * P:(b + 1) * P], start=False, stop=(m == KC - 1))
                last.then_inc(s_ready, 1)

            def turn_probs(g, u):
                pe.wait_ge(prob_ready, g * UNITS + (u + 1))
                if u >= 1:
                    pe.wait_ge(pt_done, g * UNITS + u)
                for i in range(UH):
                    last = pe.transpose(ps_t[:, i, :], prob[:, u % AHEAD, i, :], k.ident[:, :])
                last.then_inc(pt_ready, 1)

            def weigh(g, u):
                pe.wait_ge(pt_done, g * UNITS + (u + 1))
                if u == 0:
                    pe.wait_ge(qk_done, (g + 1) * (KC + 1))
                    pe.wait_ge(v_done, g + 1)
                else:
                    pe.wait_ge(o_rest, FIRST + 2 * (g * UNITS + u))
                for r in range(2):
                    if r == 1 and u % 2 == 0 and u >= 2:
                        pe.wait_ge(x1_done, FIRST + g * GT + u // 2)
                    pe.matmul(ps_m[r][:, :].rearrange("p (h n) -> p h n", h=4), vals[:, u // 2, :],
                              probT[:, u % 2, 4 * r:4 * r + 4, :], start=True, stop=True).then_inc(pv_ready, 1)

            def output(g, b):
                pe.wait_ge(o_rest, FIRST + 2 * (g * UNITS + 2 * (b + 1)))
                for c in range(KC):
                    for n, (t, w) in enumerate(PASSES):
                        last = pe.matmul(ps_m[1][:, :], oT[t][:, c, :], wo_parts[w][:, c, :],
                                         start=(c == 0 and n == 0), stop=(c == KC - 1 and n == len(PASSES) - 1))
                last.then_inc(wo_ready, 1)

            def group(g, last):
                project(g)
                pe.wait_ge(qk_done, (g + 1) * (KC + 1))
                scores(g, 0)
                scores(g, 1)
                if not last:
                    turn(g + 1)
                    pe.wait_ge(aT_ready, (g + 2) * KC)
                scores(g, 2)
                for u in range(UNITS):
                    turn_probs(g, u)
                    if u + AHEAD < UNITS:
                        scores(g, u + AHEAD)
                    if u % 2 == 0 and u >= 2:
                        output(g, u // 2 - 1)
                    weigh(g, u)
                output(g, GT - 1)

            pe.wait_ge(mask_made, 2)
            pe.wait_ge(weights_in, WEIGHTS)
            turn(0)
            pe.wait_ge(cut_rest, len(cut_weights))
            with pe.Fori(0, GROUPS - 1) as g:
                group(g, False)
            group(GROUPS - 1, True)


def feed_forward(k, d):
    h, x = k.h, k.x
    half = SC * P * KC
    raw = [k.sb(f"ff_raw{i}", [P, 2 * half]) for i in range(2)]
    parts = [[k.sb(f"ff_part{i}{part}", [P, 2 * half], F32R) for part in ("", "_rest")] for i in range(2)]
    ln_g = k.sb("ln2_g", [P, KC])
    ln_b = k.sb("ln2_b", [P, KC])
    bfc = k.sb("bfc", [P, IC])
    bproj_rows = k.sb("bproj_rows", [P, D])
    norm, ahead = Norm(k, "norm2"), Norm(k, "ahead_m0")
    a = k.a
    aT = [k.sb(f"ff_aT{part}", [P, KC, TOKENS], F32R) for part in ("", "_rest")]
    gT = [[k.sb(f"gT{i}{part}", [P, SC, GN], F32R) for part in ("", "_rest")] for i in range(2)]
    bias = [k.sb(f"ff_bias{i}", [P, SC]) for i in range(2)]
    ps_a = [k.ps(f"ff_ps_a{c}", [P, GN]) for c in range(2)]
    ps_f = [[k.ps(f"ps_f{i}{c}", [P, GN]) for c in range(SC)] for i in range(2)]
    ps_p = [k.ps(f"ps_p{i}", [P, D]) for i in range(2)]

    consts_in, raw_in = k.sem("ff_consts_in"), [k.sem(f"ff_raw_in{i}") for i in range(2)]
    dve = k.sem("ff_dve")
    a_ready, t_ready = k.sem("ff_a_ready"), k.sem("ff_t_ready")
    aT_made, aT_cut, aT_rest = k.sem("ff_aT_made"), k.sem("ff_aT_cut"), k.sem("ff_aT_rest")
    cut, cut_rest, bias_ready = k.sem("ff_cut"), k.sem("ff_cut_rest"), k.sem("ff_bias_ready")
    fc_mm, gelu_done, hid_cut, hid_rest = k.sem("fc_mm"), k.sem("gelu_done"), k.sem("ff_hid_cut"), k.sem("ff_hid_rest")
    proj_mm, h_done = k.sem("proj_mm"), k.sem("ff_h_done")
    pool_own, summed = k.sem("ff_pool"), k.sem("ff_summed")
    CONSTS = 16 * 4
    WAVE = 2 * GROUPS
    CUT_AT = 1

    def fc_weights(q, w, i, c):
        first = i * SC * P + c * P
        return parts[q][w][:, first:first + P]

    def proj_weights(q, w, c):
        return parts[q][w][:, half + c * D:half + (c + 1) * D]

    def waves(engine, step):
        for m in range(CUT_AT + GROUPS):
            step(0, m, True)
        with engine.Fori(1, SLICES // 2) as i:
            for m in range(CUT_AT - GROUPS, CUT_AT + GROUPS):
                step(i, m, False)
        for m in range(CUT_AT - GROUPS, 0):
            step(SLICES // 2, m, False)

    def cuts(i, m):
        if m == CUT_AT:
            return 2 * i + 1, 1
        if m == CUT_AT - GROUPS and not isinstance(i, int):
            return 2 * i, 0
        return None

    def tile(buf, g, j):
        return buf[:, bass.ds(g * GT + j, 1), :].rearrange("p a n -> p (a n)")

    with k.nc.Block() as block:
        @block.sync
        def _(sp):
            for dst, src in ((ln_g, d["ln2_g"]), (ln_b, d["ln2_b"]), (bfc, d["bfc"]),
                             (bproj_rows, d["bproj"].to_broadcast([P, D]))):
                sp.dma_start(dst[:, :], src).then_inc(consts_in, 16)
            for i in range(2):
                sp.dma_start(raw[i][:, :], d["ff"][i, :, :]).then_inc(raw_in[i], 16)
            with sp.Fori(1, SLICES // 2) as i:
                for q in range(2):
                    sp.wait_ge(cut_rest, 4 * i - 2 + 2 * q)
                    sp.dma_start(raw[q][:, :], d["ff"][bass.ds(2 * i + q, 1), :, :].rearrange("a p n -> (a p) n"))\
                        .then_inc(raw_in[q], 16)

        @block.gpsimd
        def _(pool):
            steps = Steps(pool, pool_own)
            pool.wait_ge(consts_in, CONSTS)

            def residuals(g, passed):
                for j in range(GT):
                    steps.note(pool.tensor_tensor(tile(h, g, j), tile(h, g, j), tile(x, g, j), ALU.add))
                steps.settle(passed)
                for j in range(GT):
                    steps.note(pool.tensor_tensor(tile(h, g, j), tile(h, g, j), bproj_rows[:, :], ALU.add))
                steps.settle()
                pool.sem_inc(summed, 1)

            norm_gpsimd(pool, k, norm, 0)
            residuals(0, norm.passed)
            with steps.loop(GROUPS - 2, 2 * GT) as i:
                norm_gpsimd(pool, k, norm, i + 1)
                residuals(i + 1, norm.passed)
            residuals(GROUPS - 1, norm.passed)
            norm_gpsimd(pool, k, ahead, 0)

        @block.vector
        def _(v):
            steps = Steps(v, dve)

            def normalise(g):
                v.wait_ge(t_ready, g * KC)
                norm_vector(v, steps, norm, g - 1, lambda j: x[:, g * GT + j, :], lambda j: a[:, j, :])\
                    .then_inc(a_ready, 1)

            def rest_of_turned(g, some):
                for c in some:
                    v.wait_ge(aT_cut, g * KC + (c + 1))
                    v.tensor_tensor(aT[1][:, c, g * GN:(g + 1) * GN], ps_a[c % 2][:, :],
                                    aT[0][:, c, g * GN:(g + 1) * GN], ALU.subtract).then_inc(aT_rest, 1)

            def rest_of_weights(e, q):
                for s in range(2):
                    v.wait_ge(cut, 2 * e + (s + 1))
                    at = slice(s * half, (s + 1) * half)
                    v.tensor_tensor(parts[q][1][:, at], raw[q][:, at], parts[q][0][:, at], ALU.subtract)\
                        .then_inc(cut_rest, 1)

            def rest_of_hidden(n, m, c):
                v.wait_ge(hid_cut, n * SC + (c + 1))
                v.tensor_tensor(gT[m % 2][1][:, c, :], ps_f[m % 2][c][:, :], gT[m % 2][0][:, c, :],
                                ALU.subtract).then_inc(hid_rest, 1)

            def accumulate(n, m, tiles=range(GT)):
                for j in tiles:
                    v.wait_ge(proj_mm, n * GT + (j + 1))
                    t = h[:, (m % GROUPS) * GT + j, :]
                    v.tensor_tensor(t, ps_p[j % 2][:, :], t, ALU.add).then_inc(h_done, 1)

            def step(i, m, first):
                n = i * WAVE + m
                prepare = first and m < GROUPS - 1
                if prepare:
                    normalise(m + 1)
                rest_of_hidden(n, m, 0)
                if prepare or (first and m == 0):
                    rest_of_hidden(n, m, 1)
                    rest_of_turned(m + 1, (0, 1))
                if not first or m > 0:
                    if first and m <= GROUPS:
                        v.wait_ge(summed, m)
                    accumulate(n - 1, m - 1, range(1))
                    if not prepare:
                        rest_of_hidden(n, m, 1)
                    accumulate(n - 1, m - 1, range(1, GT))
                if prepare:
                    rest_of_turned(m + 1, (2, 3))
                if cuts(i, m):
                    rest_of_weights(*cuts(i, m))
                if not first and isinstance(i, int) and m == -2:
                    v.wait_ge(t_ready, GROUPS * KC)
                    v.wait_ge(h_done, ((SLICES - 1) * GROUPS + 1) * GT)
                    normalise_ahead(v, steps, ahead, k, h)

            v.sem_inc(a_ready, 1)
            rest_of_turned(0, range(KC))
            rest_of_weights(0, 0)
            waves(v, step)
            accumulate(SLICES * GROUPS - 1, -1)

        @block.scalar
        def _(act):
            def turned(g):
                for c in range(KC):
                    act.wait_ge(t_ready, g * KC + (c + 1))
                    act.activation(ps_a[c % 2][:, :], ps_a[c % 2][:, :], ACT.Identity, bias=ln_b[:, c:c + 1],
                                   scale=ln_g[:, c:c + 1]).then_inc(aT_made, 1)
                    act.wait_ge(aT_made, g * KC + (c + 1))
                    act.copy(aT[0][:, c, g * GN:(g + 1) * GN], ps_a[c % 2][:, :]).then_inc(aT_cut, 1)

            def cut_weights(e, q, i, first):
                act.wait_ge(raw_in[q], 16 * (i + 1))
                if not first:
                    act.wait_ge(proj_mm, (e - 1) * GROUPS * GT)
                for s in range(2):
                    at = slice(s * half, (s + 1) * half)
                    act.copy(parts[q][0][:, at], raw[q][:, at]).then_inc(cut, 1)
                act.copy(bias[q][:, :], bfc[:, bass.ds(e * SC, SC)]).then_inc(bias_ready, 1)

            def step(i, m, first):
                n = i * WAVE + m
                if m % GROUPS == 0:
                    act.wait_ge(bias_ready, 2 * i + m // GROUPS + 1)
                if not first or m >= 2:
                    act.wait_ge(proj_mm, (n - 1) * GT)
                for c in range(SC):
                    f = ps_f[m % 2][c][:, :]
                    act.wait_ge(fc_mm, n * SC + (c + 1))
                    act.activation(f, f, ACT.Gelu_apprx_tanh, bias=bias[m // GROUPS % 2][:, c:c + 1])\
                        .then_inc(gelu_done, 1)
                    act.wait_ge(gelu_done, n * SC + (c + 1))
                    act.copy(gT[m % 2][0][:, c, :], f).then_inc(hid_cut, 1)
                if first and m < GROUPS - 1:
                    turned(m + 1)
                if cuts(i, m):
                    cut_weights(*cuts(i, m), i, first)

            act.wait_ge(consts_in, CONSTS)
            turned(0)
            cut_weights(0, 0, 0, True)
            waves(act, step)

        @block.tensor
        def _(pe):
            def turn(g, some):
                for c in some:
                    if g * KC + c >= 2:
                        pe.wait_ge(aT_rest, g * KC + c - 1)
                    for j in range(GT):
                        last = pe.transpose(ps_a[c % 2][:, j * P:(j + 1) * P], a[:, j, c * P:(c + 1) * P],
                                            k.ident[:, :])
                    last.then_inc(t_ready, 1)

            def up(i, m, first):
                n, g, q = i * WAVE + m, m % GROUPS, m // GROUPS % 2
                if first and m < GROUPS:
                    pe.wait_ge(aT_rest, (m + 1) * KC)
                if g == 0:
                    pe.wait_ge(cut_rest, 2 * (2 * i + m // GROUPS) + 2)
                if not first or m >= 2:
                    pe.wait_ge(hid_rest, (n - 1) * SC)
                for c in range(SC):
                    for a_ in range(KC):
                        for p, (w, t) in enumerate(PASSES):
                            mm = pe.matmul(ps_f[m % 2][c][:, :], fc_weights(q, w, a_, c),
                                           aT[t][:, a_, g * GN:(g + 1) * GN], start=(a_ == 0 and p == 0),
                                           stop=(a_ == KC - 1 and p == len(PASSES) - 1))
                    mm.then_inc(fc_mm, 1)

            def down(n, m):
                q = m // GROUPS % 2
                pe.wait_ge(hid_rest, (n + 1) * SC)
                for j in range(GT):
                    if not isinstance(n, int) or n * GT + j - 1 > 0:
                        pe.wait_ge(h_done, n * GT + j - 1)
                    for c in range(SC):
                        for p, (t, w) in enumerate(PASSES):
                            mm = pe.matmul(ps_p[j % 2][:, :], gT[m % 2][t][:, c, j * P:(j + 1) * P],
                                           proj_weights(q, w, c), start=(c == 0 and p == 0),
                                           stop=(c == SC - 1 and p == len(PASSES) - 1))
                    mm.then_inc(proj_mm, 1)

            def step(i, m, first):
                up(i, m, first)
                prepare = first and m < GROUPS - 1
                if prepare:
                    pe.wait_ge(a_ready, m + 2)
                    turn(m + 1, (0, 1))
                if not first or m > 0:
                    down(i * WAVE + m - 1, m - 1)
                if prepare:
                    turn(m + 1, (2, 3))

            pe.wait_ge(a_ready, 1)
            turn(0, range(KC))
            waves(pe, step)
            down(SLICES * GROUPS - 1, -1)


BLOCK = 2 * P
E0, TOP0, SETS0, SET_TOP0 = 16, 4, 4, 2
MID0, SHARED = 352, 704
E1, TOP1, MID1 = 8, 2, 256


def chunks(n):
    return [(c, min(P, n - c)) for c in range(0, n, P)]


class Routing:

    def __init__(self, k, name, experts, top):
        self.name, self.experts, self.top = name, experts, top
        self.blocks = (TOKENS * top + experts * (BLOCK - 1)) // BLOCK
        self.slots = self.blocks * BLOCK
        self.best = k.sb(f"{name}_best", [P, TILES, 8])
        self.slot = k.sb(f"{name}_slot", [P, TILES, top], I32)
        self.token = k.sb(f"{name}_token", [P, 2 * self.blocks], I32)
        self.back = k.sb(f"{name}_back", [P, 2 * self.blocks], I32)
        self.expert = k.sb(f"{name}_expert", [P, self.blocks], I32)
        self.weight = self.best
        nc = k.nc
        self.rows = nc.dram_tensor(f"{name}_rows", (TOKENS, D), F32).ap()
        self.map = nc.dram_tensor(f"{name}_map", (self.slots, 1), I32).ap()
        self.result = nc.dram_tensor(f"{name}_result", (TOKENS * top + self.slots, D), F32).ap()


def carver(flat):
    used = [0]

    def take(name, shape):
        n = math.prod(shape[1:])
        part = flat[:, used[0]:used[0] + n]
        used[0] += n
        dims = dict(zip("abc", shape[1:]))
        names = " ".join(dims)
        return part.rearrange(f"p ({names}) -> p {names}", **dims)

    return take


class RoutingWork:

    def __init__(self, k, r, scatter, take=None, take_more=None):
        n, e = r.name, r.experts
        self.scatter = scatter
        take = take or (lambda name, shape: k.sb(f"{n}_{name}", shape))
        take_more = take_more or take
        self.scores = k.sb(f"{n}_scores", [P, TILES, e])
        self.index = k.sb(f"{n}_index", [P, TILES, 8], U32)
        self.chosen = take_more("chosen", [P, r.top, TILES, e])
        self.indexf = k.sb(f"{n}_indexf", [P, TILES, 8])
        self.any = take("any", [P, TILES, e])
        self.before = take("before", [P, TILES, e])
        self.count = k.sb(f"{n}_count", [P, e])
        self.counti = k.sb(f"{n}_counti", [P, e], I32)
        self.blocks = k.sb(f"{n}_nblocks", [P, e])
        self.end = k.sb(f"{n}_end", [P, e])
        self.first = k.sb(f"{n}_first", [P, 1, e])
        self.place = take("place", [P, TILES, e])
        self.product = take("product", [P, TILES, e])
        self.slotf = k.sb(f"{n}_slotf", [P, TILES, r.top])
        self.past = take("past", [P, r.blocks, e])
        self.expertf = k.sb(f"{n}_expertf", [P, r.blocks])
        self.iota_e = k.sb(f"{n}_iota_e", [P, 1, e])
        self.iota_b = k.sb(f"{n}_iota_b", [P, r.blocks, 1])
        if scatter:
            self.row_back = k.sb(f"{n}_row_back", [P, TILES, r.top], I32)
            self.unused = k.sb(f"{n}_unused", [2 * r.blocks, P], I32)
            self.map = k.sb(f"{n}_map_sb", [2 * r.blocks, P], I32)
            self.mapf = k.sb(f"{n}_mapf", [2 * r.blocks, P])
        else:
            self.tile_id = k.sb(f"{n}_tile_id", [P, TILES, 1])
            self.row_id = k.sb(f"{n}_row_id", [P, 1])
            self.iota_p = k.sb(f"{n}_iota_p", [P, 1, P])
            self.iota_c = k.sb(f"{n}_iota_c", [P, 1, 2 * r.blocks])
            self.high = k.sb(f"{n}_high", [P, TILES, r.top], I32)
            self.highf = k.sb(f"{n}_highf", [P, TILES, r.top])
            self.lowf = k.sb(f"{n}_lowf", [P, TILES, r.top])
            self.spot = k.sb(f"{n}_spot", [P, r.top, TILES, P], BF16)
            self.item = k.sb(f"{n}_item", [P, r.top, TILES, 3, 2 * r.blocks], BF16)
            self.tokenf = k.sb(f"{n}_tokenf", [P, 2 * r.blocks])
            self.choice = k.sb(f"{n}_choice", [P, 2 * r.blocks])
            self.free = k.sb(f"{n}_free", [P, 2 * r.blocks])
            self.unused = k.sb(f"{n}_unused", [P, 2 * r.blocks])
            self.item_ready = k.sem(f"{n}_item_ready")
        self.before_p = k.sb(f"{n}_before_p", [P, P])
        self.ones = k.sb(f"{n}_ones", [P, P])
        self.made, self.any_ready, self.ranked = k.sem(f"{n}_made"), k.sem(f"{n}_any_ready"), k.sem(f"{n}_ranked")
        self.slot_ready, self.scattered = k.sem(f"{n}_slot_ready"), k.sem(f"{n}_scattered")
        self.map_zeroed, self.map_in = k.sem(f"{n}_map_zeroed"), k.sem(f"{n}_map_in")
        self.map_ready, self.map_turned = k.sem(f"{n}_map_ready"), k.sem(f"{n}_map_turned")
        self.token_ready = k.sem(f"{n}_token_ready")


def routing_constants(pool, r, w):
    pool.memset(w.before_p[:, :], 0.0).then_inc(w.made, 1)
    pool.memset(w.ones[:, :], 1.0).then_inc(w.made, 1)
    small = {"base": 0, "channel_multiplier": 0, "allow_small_or_imprecise_dtypes": True}
    pool.iota(w.iota_e[:, :, :], [[1, r.experts]], **small).then_inc(w.made, 1)
    pool.iota(w.iota_b[:, :, :], [[1, r.blocks]], **small).then_inc(w.made, 1)
    if w.scatter:
        pool.iota(w.unused[:, :], [[1, P]], base=TOKENS * r.top, channel_multiplier=P).then_inc(w.made, 1)
        pool.iota(w.row_back[:, :, :], [[P * r.top, TILES], [1, r.top]], base=0, channel_multiplier=r.top)\
            .then_inc(w.made, 1)
        pool.wait_ge(w.made, 6)
    else:
        pool.iota(w.iota_p[:, :, :], [[1, P]], **small).then_inc(w.made, 1)
        pool.iota(w.iota_c[:, :, :], [[1, 2 * r.blocks]], **small).then_inc(w.made, 1)
        pool.iota(w.tile_id[:, :, :], [[1, TILES]], **small).then_inc(w.made, 1)
        pool.iota(w.row_id[:, :], [[1, 1]], base=0, channel_multiplier=1,
                  allow_small_or_imprecise_dtypes=True).then_inc(w.made, 1)
        pool.iota(w.unused[:, :], [[P, 2 * r.blocks]], base=TOKENS * r.top + 1, channel_multiplier=1,
                  allow_small_or_imprecise_dtypes=True).then_inc(w.made, 1)
        pool.wait_ge(w.made, 9)
    pool.affine_select(out=w.before_p[:, :], in_=w.before_p[:, :], compare_op=ALU.is_ge, fill=1.0, base=0,
                       pattern=[[-1, P]], channel_multiplier=1).then_inc(w.made, 1)
    if w.scatter:
        pool.dma_start(r.map.rearrange("(a b) n -> a (b n)", b=P), w.unused[:, :]).then_inc(w.map_zeroed, 16)


def routing_made(w):
    return 7 if w.scatter else 10


def routing_vector(v, steps, r, w, iota=True):
    e = r.experts
    steps.note(v.tensor_copy(w.indexf[:, :, :], w.index[:, :, :]))
    steps.settle()
    for c in range(r.top):
        steps.note(v.tensor_tensor(w.chosen[:, c, :, :], w.indexf[:, :, c:c + 1].to_broadcast([P, TILES, e]),
                                   w.iota_e[:, :, :].to_broadcast([P, TILES, e]), ALU.is_equal))
    steps.settle()
    steps.note(v.tensor_tensor(w.any[:, :, :], w.chosen[:, 0, :, :], w.chosen[:, 1, :, :], ALU.add))
    for c in range(2, r.top):
        steps.settle()
        steps.note(v.tensor_tensor(w.any[:, :, :], w.any[:, :, :], w.chosen[:, c, :, :], ALU.add))
    steps.settle()
    v.sem_inc(w.any_ready, 1)


def routing_tensor(pe, r, w, ps_rank, ps_sum):
    pe.wait_ge(w.any_ready, 1)
    pe.wait_ge(w.made, routing_made(w))
    pe.matmul(ps_rank, w.before_p[:, :], w.any[:, :, :].rearrange("p t e -> p (t e)"), start=True, stop=True)
    pe.matmul(ps_sum, w.ones[:, :], w.any[:, :, :].rearrange("p t e -> p (t e)"), start=True, stop=True)\
        .then_inc(w.ranked, 1)


def routing_slots(v, steps, r, w, ps_rank, ps_sum):
    e = r.experts
    rank = ps_rank.rearrange("p (t e) -> p t e", e=e)
    rows = ps_sum.rearrange("p (t e) -> p t e", e=e)
    steps.note(v.memset(w.before[:, 0, :], 0.0))
    steps.settle()
    v.wait_ge(w.ranked, 1)
    for t in range(TILES):
        out = w.before[:, t + 1, :] if t + 1 < TILES else w.count[:, :]
        steps.note(v.tensor_tensor(out, rows[:, t, :], w.before[:, t, :], ALU.add))
        steps.settle()
    steps.note(v.tensor_scalar(w.counti[:, :], w.count[:, :], float(BLOCK - 1), None, ALU.add))
    steps.settle()
    steps.note(v.tensor_scalar(w.counti[:, :], w.counti[:, :], BLOCK.bit_length() - 1, None,
                               ALU.logical_shift_right))
    steps.settle()
    steps.note(v.tensor_copy(w.blocks[:, :], w.counti[:, :]))
    steps.settle()
    steps.note(v.tensor_copy(w.end[:, 0:1], w.blocks[:, 0:1]))
    for i in range(1, e):
        steps.settle()
        steps.note(v.tensor_tensor(w.end[:, i:i + 1], w.end[:, i - 1:i], w.blocks[:, i:i + 1], ALU.add))
    steps.settle()
    steps.note(v.tensor_tensor(w.first[:, 0, :], w.end[:, :], w.blocks[:, :], ALU.subtract))
    steps.note(v.tensor_tensor(w.past[:, :, :], w.iota_b[:, :, :].to_broadcast([P, r.blocks, e]),
                               w.end[:, :].rearrange("p (a e) -> p a e", a=1).to_broadcast([P, r.blocks, e]),
                               ALU.is_ge))
    steps.note(v.tensor_tensor(w.place[:, :, :], rank, w.before[:, :, :], ALU.add))
    steps.settle()
    steps.note(v.tensor_scalar(w.first[:, 0, :], w.first[:, 0, :], float(BLOCK), None, ALU.mult))
    steps.note(v.tensor_reduce(w.expertf[:, :], w.past[:, :, :], AX.X, ALU.add))
    steps.settle()
    steps.note(v.tensor_tensor(w.place[:, :, :], w.place[:, :, :], w.first[:, :, :].to_broadcast([P, TILES, e]),
                               ALU.add))
    steps.note(v.tensor_scalar(r.expert[:, :], w.expertf[:, :], float(e - 1), None, ALU.min))
    for c in range(r.top):
        steps.settle()
        steps.note(v.tensor_tensor(w.product[:, :, :], w.place[:, :, :], w.chosen[:, c, :, :], ALU.mult))
        steps.settle()
        steps.note(v.tensor_reduce(w.slotf[:, :, c], w.product[:, :, :], AX.X, ALU.add))
    steps.settle()
    v.tensor_copy(r.slot[:, :, :], w.slotf[:, :, :]).then_inc(w.slot_ready, 1)


def routing_map_vector(v, steps, r, w, ps_map):
    slots = 2 * r.blocks
    v.wait_ge(w.slot_ready, 1)
    steps.note(v.tensor_scalar(w.high[:, :, :], r.slot[:, :, :], P.bit_length() - 1, None, ALU.logical_shift_right))
    steps.settle()
    steps.note(v.tensor_copy(w.highf[:, :, :], w.high[:, :, :]))
    steps.settle()
    steps.note(v.scalar_tensor_tensor(out=w.lowf[:, :, :], in0=w.highf[:, :, :], scalar=float(-P),
                                      in1=w.slotf[:, :, :], op0=ALU.mult, op1=ALU.add))
    steps.settle()
    for c in range(r.top):
        row, tile = w.item[:, c, :, 0, :], w.item[:, c, :, 1, :]
        steps.note(v.tensor_tensor(row, w.highf[:, :, c:c + 1].to_broadcast([P, TILES, slots]),
                                   w.iota_c[:, :, :].to_broadcast([P, TILES, slots]), ALU.is_equal))
        steps.note(v.tensor_tensor(w.spot[:, c, :, :], w.lowf[:, :, c:c + 1].to_broadcast([P, TILES, P]),
                                   w.iota_p[:, :, :].to_broadcast([P, TILES, P]), ALU.is_equal))
        steps.settle()
        steps.note(v.tensor_scalar(w.item[:, c, :, 2, :], row, float(c + 1), None, ALU.mult))
        steps.note(v.tensor_tensor(tile, row, w.tile_id[:, :, :].to_broadcast([P, TILES, slots]), ALU.mult))
        steps.settle()
        v.tensor_scalar(row, row, w.row_id[:, 0:1], None, ALU.mult).then_inc(w.item_ready, 1)
    v.wait_ge(w.map_turned, 1)
    steps.note(v.tensor_copy(w.tokenf[:, :], ps_map[:, 0:slots]))
    steps.note(v.tensor_copy(w.choice[:, :], ps_map[:, 2 * slots:3 * slots]))
    steps.settle()
    steps.note(v.scalar_tensor_tensor(out=w.tokenf[:, :], in0=ps_map[:, slots:2 * slots], scalar=float(P),
                                      in1=w.tokenf[:, :], op0=ALU.mult, op1=ALU.add))
    steps.note(v.tensor_scalar(w.free[:, :], w.choice[:, :], 0.0, None, ALU.is_equal))
    steps.settle()
    steps.note(v.tensor_copy(r.token[:, :], w.tokenf[:, :]))
    steps.note(v.tensor_tensor(w.free[:, :], w.free[:, :], w.unused[:, :], ALU.mult))
    steps.note(v.scalar_tensor_tensor(out=w.choice[:, :], in0=w.tokenf[:, :], scalar=float(r.top),
                                      in1=w.choice[:, :], op0=ALU.mult, op1=ALU.add))
    steps.settle()
    steps.note(v.tensor_tensor(w.choice[:, :], w.choice[:, :], w.free[:, :], ALU.add))
    steps.settle()
    v.tensor_scalar(r.back[:, :], w.choice[:, :], -1.0, None, ALU.add).then_inc(w.token_ready, 1)


def routing_map_tensor(pe, r, w, ps_map):
    for c in range(r.top):
        pe.wait_ge(w.item_ready, c + 1)
        for t in range(TILES):
            mm = pe.matmul(ps_map, w.spot[:, c, t, :], w.item[:, c, t, :, :].rearrange("p a n -> p (a n)"), start=(c == 0 and t == 0),
                           stop=(c == r.top - 1 and t == TILES - 1))
    mm.then_inc(w.map_turned, 1)


def routing_scatter(pool, r, w):
    pool.wait_ge(w.map_zeroed, 16)
    pool.wait_ge(w.slot_ready, 1)
    for t in range(TILES):
        for c in range(r.top):
            pool.indirect_dma_start(r.map, bass.IndirectOffsetOnAxis(ap=r.slot[:, t, c:c + 1].bitcast(U32), axis=0),
                                    w.row_back[:, t, c:c + 1], None).then_inc(w.scattered, 16)
    pool.wait_ge(w.scattered, 16 * TILES * r.top)
    pool.dma_start(w.map[:, :], r.map.rearrange("(a b) n -> a (b n)", b=P)).then_inc(w.map_in, 16)


def experts(k, d, r, mid, gated):
    n, nb, mids = r.name + "e", r.blocks, chunks(mid)
    nm = len(mids)
    width = 2 * mid if gated else mid
    parts = KC + nm
    turns = (nb - 1) // 2
    spare = k.x[:, :, :].rearrange("p t n -> p (t n)")
    up = [spare[:, i * KC * width:(i + 1) * KC * width].rearrange("p (c n) -> p c n", c=KC) for i in range(2)]
    down = [k.sb(f"{n}_down{i}", [P, nm, D]) for i in range(2)]
    two = lambda name, shape: [k.sb(f"{n}_{name}{part}", shape, F32R) for part in ("", "_rest")]
    up_parts = [two(f"up_part{i}", [P, KC, width]) for i in range(2)]
    down_parts = [two(f"down_part{i}", [P, nm, D]) for i in range(2)]
    if not gated:
        up_bias = [k.sb(f"{n}_up_bias{i}", [P, nm]) for i in range(2)]
        down_bias = [k.sb(f"{n}_down_bias{i}", [P, D]) for i in range(2)]
    pick, put = ([k.sb(f"{n}_{s}{i}", [P, 2], I32) for i in range(2)] for s in ("pick", "put"))
    rows = [k.sb(f"{n}_xrows{i}", [P, 2, D]) for i in range(2)]
    rowsT = two("rowsT", [P, KC, BLOCK])
    act_up = k.sb(f"{n}_act_up", [P, nm, BLOCK])
    hid = k.sb(f"{n}_hid", [P, nm, BLOCK])
    hidT = two("hidT", [P, nm, BLOCK])
    y = [k.sb(f"{n}_y{i}", [P, 2, D]) for i in range(2)]
    ps_t = [k.ps(f"{n}_ps_t{i}", [P, 2, BLOCK]) for i in range(2)]
    ps_u = [k.ps(f"{n}_ps_u{i}", [P, 2, BLOCK]) for i in range(3)]
    ps_d = [k.ps(f"{n}_ps_d{i}", [P, D]) for i in range(2)]
    pair = lambda s: [k.sem(f"{n}_{s}{i}") for i in range(2)]
    bias_in = pair("bias_in")
    up_in, rows_in, y_out = pair("up_in"), pair("rows_in"), pair("y_out")
    pick_ready, put_ready, y_left = pair("pick_ready"), pair("put_ready"), pair("y_left")
    cut, cut_rest = pair("cut"), pair("cut_rest")
    turned, down_mm, y_ready, y1_ready = pair("turned"), pair("down_mm"), pair("y_ready"), pair("y1_ready")
    rows_cut, rows_rest = k.sem(f"{n}_rows_cut"), k.sem(f"{n}_rows_rest")
    up_mm, act_done, hid_made = k.sem(f"{n}_up_mm"), k.sem(f"{n}_act_done"), k.sem(f"{n}_hid_made")
    hid_cut, hid_rest = k.sem(f"{n}_hid_cut"), k.sem(f"{n}_hid_rest")
    LOADS = 16 * 2

    def piece(q, s):
        if s < KC:
            return up[q][:, s, :], up_parts[q][0][:, s, :], up_parts[q][1][:, s, :]
        return (down[q][:, s - KC, :], down_parts[q][0][:, s - KC, :], down_parts[q][1][:, s - KC, :])

    def following(i, q):
        return (i, 1) if q == 0 else (i + 1, 0)

    def blocks(engine, block):
        with engine.Fori(0, turns) as i:
            block(i, 0, False)
            block(i, 1, False)
        for t in range(2 * turns, nb):
            block(turns, t % 2, t == nb - 1)

    with k.nc.Block() as block:
        @block.sync
        def _(sp):
            def expert_of(i, q):
                return sp.value_load(r.expert[0:1, bass.ds(2 * i + q, 1)], min_val=0, max_val=r.experts - 1)

            def load(i, q):
                e = expert_of(i, q)
                sp.wait_ge(cut_rest[q], FIRST + i * parts)
                sp.dma_start(up[q].rearrange("p c n -> p (c n)"),
                             d[f"{r.name}_up"][bass.ds(e, 1), :, :].rearrange("a p n -> (a p) n"))\
                    .then_inc(up_in[q], 16)
                sp.dma_start(down[q][:, :, :].rearrange("p c n -> p (c n)"),
                             d[f"{r.name}_down"][bass.ds(e, 1), :, :].rearrange("a p n -> (a p) n"))\
                    .then_inc(up_in[q], 16)

            def load_biases(i, q):
                if gated:
                    return
                e = expert_of(i, q)
                sp.wait_ge(y_ready[q], FIRST + i)
                sp.wait_ge(y1_ready[q], FIRST + i)
                sp.dma_start(up_bias[q][:, :], d[f"{r.name}_up_bias"][bass.ds(e, 1), :, :]
                             .rearrange("a p n -> (a p) n")).then_inc(bias_in[q], 16)
                sp.dma_start(down_bias[q][:, :], d[f"{r.name}_down_bias"][bass.ds(e, 1), :]
                             .to_broadcast([P, D])).then_inc(bias_in[q], 16)

            load(0, 0)
            load_biases(0, 0)
            sp.wait_ge(turned[0], FIRST + 1)
            load(0, 1)
            load_biases(0, 1)
            load(1, 0)
            with sp.Fori(0, turns - 1) as i:
                for q in range(2):
                    load(i + 1 + q, 1 - q)
                    load_biases(i + 1, q)
            for t in range(2 * (turns - 1), nb - 2):
                if t + 3 < nb:
                    load((t + 3) // 2, (t + 3) % 2)
                load_biases((t + 2) // 2, t % 2)

        @block.gpsimd
        def _(pool):
            for s in y_left:
                pool.sem_inc(s, FIRST)

            def gather(i, q):
                wait_alone(pool, turned[q], FIRST + i, k.passed_pool)
                pool.tensor_copy(pick[q][:, :], r.token[:, bass.ds(4 * i + 2 * q, 2)]).then_inc(pick_ready[q], 1)
                wait_alone(pool, pick_ready[q], i + 1, k.passed_pool)
                for j in range(2):
                    pool.indirect_dma_start(rows[q][:, j, :], None, r.rows, bass.IndirectOffsetOnAxis(
                        ap=pick[q][:, j:j + 1].bitcast(U32), axis=0)).then_inc(rows_in[q], 16)

            def send_back(i, q):
                pool.tensor_copy(put[q][:, :], r.back[:, bass.ds(4 * i + 2 * q, 2)]).then_inc(put_ready[q], 1)
                wait_alone(pool, put_ready[q], i + 1, k.passed_pool)
                wait_alone(pool, y_ready[q], FIRST + i + 1, k.passed_pool)
                wait_alone(pool, y1_ready[q], FIRST + i + 1, k.passed_pool)
                for j in range(2):
                    pool.indirect_dma_start(r.result, bass.IndirectOffsetOnAxis(
                        ap=put[q][:, j:j + 1].bitcast(U32), axis=0), y[q][:, j, :], None).then_inc(y_out[q], 16)

            def sent(i, q):
                wait_alone(pool, y_out[q], 32 * (i + 1), y_left[q])

            for t in range(3):
                gather(t // 2, t % 2)
            with pool.Fori(0, turns - 1) as i:
                for q in range(2):
                    send_back(i, q)
                    gather(i + 1 + q, 1 - q)
                    sent(i, q)
            for t in range(2 * (turns - 1), nb):
                send_back(t // 2, t % 2)
                if t + 3 < nb:
                    gather((t + 3) // 2, (t + 3) % 2)
                sent(t // 2, t % 2)

        @block.scalar
        def _(act):
            for s in y_ready if gated else [hid_made]:
                act.sem_inc(s, FIRST)

            def cut_weights(i, q, some):
                for s in some:
                    if s == 0:
                        act.wait_ge(up_in[q], LOADS * (i + 1))
                        act.wait_ge(down_mm[q], FIRST + i)
                    came, part, rest = piece(q, s)
                    act.copy(part, came).then_inc(cut[q], 1)

            def cut_rows(i, q):
                act.wait_ge(turned[q], FIRST + i + 1)
                for half in range(2):
                    act.copy(rowsT[0][:, 2 * half:2 * half + 2, :], ps_t[half][:, :, :]).then_inc(rows_cut, 1)

            def hidden(i, q, m):
                size = mids[m][1]
                act.wait_ge(up_mm, (2 * i + q) * nm + (m + 1))
                if gated:
                    act.activation(act_up[0:size, m, :], ps_u[m][0:size, 0, :], ACT.Silu).then_inc(act_done, 1)
                else:
                    act.wait_ge(bias_in[q], LOADS * (i + 1))
                    act.activation(hid[0:size, m, :], ps_u[m][0:size, 0, :], ACT.Silu,
                                   bias=up_bias[q][0:size, m:m + 1]).then_inc(hid_made, 1)

            def cut_hidden(i, q, m):
                size = mids[m][1]
                act.wait_ge(hid_made, FIRST + (2 * i + q) * nm + (m + 1))
                act.copy(hidT[0][0:size, m, :], hid[0:size, m, :]).then_inc(hid_cut, 1)

            def step(i, q, last):
                then = following(i, q)
                if not last:
                    cut_weights(*then, (0,))
                for m in range(nm):
                    hidden(i, q, m)
                    if not last and m < nm - 1:
                        cut_weights(*then, (m + 1,))
                    cut_hidden(i, q, m)
                if not last:
                    cut_rows(*then)
                    cut_weights(*then, range(nm, parts))
                if gated:
                    act.wait_ge(y_left[q], FIRST + i)
                    act.wait_ge(down_mm[q], FIRST + i + 1)
                    act.copy(y[q][:, 0, :], ps_d[0][:, :]).then_inc(y_ready[q], 1)

            act.activation(act_up[0:1, 0, 0:1], k.ident[0:1, 0:1], ACT.Silu)
            cut_weights(0, 0, range(parts))
            cut_rows(0, 0)
            blocks(act, step)

        @block.vector
        def _(v):
            for s in ([hid_made] if gated else y_ready) + y1_ready + cut_rest:
                v.sem_inc(s, FIRST)

            def rest_of_weights(i, q, some):
                for s in some:
                    came, part, rest = piece(q, s)
                    v.wait_ge(cut[q], i * parts + (s + 1))
                    v.tensor_tensor(rest, came, part, ALU.subtract).then_inc(cut_rest[q], 1)

            def rest_of_rows(i, q):
                for half in range(2):
                    two_chunks = slice(2 * half, 2 * half + 2)
                    v.wait_ge(rows_cut, 2 * (2 * i + q) + (half + 1))
                    v.tensor_tensor(rowsT[1][:, two_chunks, :], ps_t[half][:, :, :], rowsT[0][:, two_chunks, :],
                                    ALU.subtract).then_inc(rows_rest, 1)

            def gate(i, q, m):
                size = mids[m][1]
                v.wait_ge(act_done, (2 * i + q) * nm + (m + 1))
                v.tensor_tensor(hid[0:size, m, :], act_up[0:size, m, :], ps_u[m][0:size, 1, :], ALU.mult)\
                    .then_inc(hid_made, 1)

            def rest_of_hidden(i, q, m):
                size = mids[m][1]
                v.wait_ge(hid_cut, (2 * i + q) * nm + (m + 1))
                v.tensor_tensor(hidT[1][0:size, m, :], hid[0:size, m, :], hidT[0][0:size, m, :], ALU.subtract)\
                    .then_inc(hid_rest, 1)

            def step(i, q, last):
                then = following(i, q)
                if not last:
                    rest_of_weights(*then, (0,))
                for m in range(nm):
                    if gated:
                        gate(i, q, m)
                    if not last and m < nm - 1:
                        rest_of_weights(*then, (m + 1,))
                    rest_of_hidden(i, q, m)
                if not last:
                    rest_of_rows(*then)
                    rest_of_weights(*then, range(nm, parts))
                v.wait_ge(y_left[q], FIRST + i)
                v.wait_ge(down_mm[q], FIRST + i + 1)
                if gated:
                    v.tensor_copy(y[q][:, 1, :], ps_d[1][:, :]).then_inc(y1_ready[q], 1)
                else:
                    v.tensor_tensor(y[q][:, 0, :], ps_d[0][:, :], down_bias[q][:, :], ALU.add)\
                        .then_inc(y_ready[q], 1)
                    v.tensor_tensor(y[q][:, 1, :], ps_d[1][:, :], down_bias[q][:, :], ALU.add)\
                        .then_inc(y1_ready[q], 1)

            rest_of_weights(0, 0, range(parts))
            rest_of_rows(0, 0)
            blocks(v, step)

        @block.tensor
        def _(pe):
            for s in down_mm + turned:
                pe.sem_inc(s, FIRST)

            def turn(i, q):
                pe.wait_ge(rows_in[q], 32 * (i + 1))
                for c in range(KC):
                    for j in range(2):
                        last = pe.transpose(ps_t[c // 2][:, c % 2, j * P:(j + 1) * P],
                                            rows[q][:, j, c * P:(c + 1) * P], k.ident[:, :])
                last.then_inc(turned[q], 1)

            def step(i, q, last):
                pe.wait_ge(rows_rest, 2 * (2 * i + q) + 2)
                pe.wait_ge(cut_rest[q], FIRST + i * parts + KC)
                pe.wait_ge(hid_made, FIRST + (2 * i + q) * nm)
                for m, (c, size) in enumerate(mids):
                    for side in range(2 if gated else 1):
                        first = side * mid + c
                        for a in range(KC):
                            for p, (w, x) in enumerate(PASSES):
                                mm = pe.matmul(ps_u[m][0:size, side, :], up_parts[q][w][:, a, first:first + size],
                                               rowsT[x][:, a, :], start=(a == 0 and p == 0),
                                               stop=(a == KC - 1 and p == len(PASSES) - 1))
                    mm.then_inc(up_mm, 1)
                if not last:
                    turn(*following(i, q))
                pe.wait_ge(cut_rest[q], FIRST + (i + 1) * parts)
                if q == 0:
                    pe.wait_ge(y_ready[1], FIRST + i)
                    pe.wait_ge(y1_ready[1], FIRST + i)
                else:
                    pe.wait_ge(y_ready[0], FIRST + i + 1)
                    pe.wait_ge(y1_ready[0], FIRST + i + 1)
                for j in range(2):
                    for m, (c, size) in enumerate(mids):
                        if j == 0:
                            pe.wait_ge(hid_rest, (2 * i + q) * nm + (m + 1))
                        for p, (w, x) in enumerate(PASSES):
                            mm = pe.matmul(ps_d[j][:, :], hidT[x][0:size, m, j * P:(j + 1) * P],
                                           down_parts[q][w][0:size, m, :], start=(m == 0 and p == 0),
                                           stop=(m == nm - 1 and p == len(PASSES) - 1))
                mm.then_inc(down_mm[q], 1)

            turn(0, 0)
            blocks(pe, step)


class Combine:

    def __init__(self, k, r):
        self.r = r
        self.deep = TILES // r.top // GT
        self.y = k.x[:, :, :].rearrange("p (g t c) n -> p g t c n", t=GT, c=r.top)
        self.weight = k.sb(f"{r.name}_weight_group", [P, GT, r.top])
        self.back = [[k.sem(f"{r.name}_back{i}{j}") for j in range(GT)] for i in range(self.deep)]
        self.added = k.sem(f"{r.name}_combined")
        self.notes = 1 + GT * (r.top - 1)


def combine_load(sp, cb, g, tiles=range(GT)):
    top = cb.r.top
    if g >= cb.deep:
        sp.wait_ge(cb.added, (g - cb.deep + 1) * GT)
    for j in tiles:
        first = (g * GT + j) * P * top
        sp.dma_start(cb.y[:, g % cb.deep, j, :, :], cb.r.result[first:first + P * top, :]
                     .rearrange("(p c) n -> p c n", c=top)).then_inc(cb.back[g % cb.deep][j], 16)


def combine_vector(v, steps, cb, k, g, buffer, turn, passed):
    r = cb.r
    steps.note(v.tensor_copy(cb.weight[:, :, :], r.weight[:, bass.ds(g * GT, GT), 0:r.top]))
    steps.settle(passed)
    for j in range(GT):
        t = tile_of(k.h, g, j)
        wait_alone(v, cb.back[buffer][j], 16 * (turn + 1), passed)
        for c in range(r.top):
            ins = v.scalar_tensor_tensor(out=t, in0=cb.y[:, buffer, j, c, :], scalar=cb.weight[:, j, c:c + 1],
                                         in1=t, op0=ALU.mult, op1=ALU.add)
            if c < r.top - 1:
                steps.note(ins)
                steps.settle(passed)
        ins.then_inc(cb.added, 1)
    wait_alone(v, cb.added, (g + 1) * GT, passed)


def tile_of(buf, g, j):
    return buf[:, bass.ds(g * GT + j, 1), :].rearrange("p a n -> p (a n)")


def mixture_first_route(k, d):
    h, r = k.h, k.route0
    mids = chunks(SHARED)
    nm = len(mids)
    wg = k.sb("wg", [P, KC, E0])
    raw = [k.sb(f"m0_raw{i}", [P, 3 * D]) for i in range(2)]
    ups = [k.sb(f"m0_ups{part}", [P, 4, 2 * SHARED], F32R) for part in ("", "_rest")]
    downs = [k.sb(f"m0_downs{part}", [P, 2, 3 * D], F32R) for part in ("", "_rest")]
    PIECES = 6
    norm = Norm(k, "norm3")
    a = k.a
    aT = k.x[:, :, :].rearrange("p (c g) n -> p c (g n)", c=KC)
    scoresT = k.sb("m0_scoresT", [E0, GN])
    act_up = raw[0][:, 0:2 * GN].rearrange("p (a n) -> p a n", a=2)
    take_a = carver(a[:, :, :].rearrange("p t n -> p (t n)"))
    take_raw = carver(raw[1][:, :])
    rowsT = [k.sb(f"m0_rowsT{part}", [P, KC, GN], F32R) for part in ("", "_rest")]
    hidT = [k.sb(f"m0_hidT{part}", [P, nm, GN], F32R) for part in ("", "_rest")]
    w = RoutingWork(k, r, True, take_a, take_raw)
    smax = k.sb("m0_smax", [P, TILES, 1])
    ssum = k.sb("m0_ssum", [P, TILES, 1])
    sets = take_raw("sets", [P, TILES, 8])
    set_best = take_raw("set_best", [P, TILES, 8])
    set_index = k.sb("m0_set_index", [P, TILES, 8], U32)
    set_indexf = take_raw("set_indexf", [P, TILES, 8])
    open0 = k.sb("m0_open0", [P, TILES, SETS0])
    open1 = k.sb("m0_open1", [P, TILES, SETS0])
    allowed = take_a("allowed", [P, TILES, E0])
    ps_a = [k.ps(f"m0_ps_a{i}", [P, 2, GN]) for i in range(2)]
    ps_r = k.ps("m0_ps_r", [P, GN])
    ps_q = k.ps("m0_ps_q", [P, GN])
    ps_d = [k.ps(f"m0_ps_d{i}", [P, D]) for i in range(2)]

    weights_in, dve = k.sem("m0_weights_in"), k.sem("m0_dve")
    a_ready, rows_out = k.sem("m0_a_ready"), k.sem("m0_rows_out")
    t_ready, aT_ready = k.sem("m0_t_ready"), k.sem("m0_aT_ready")
    rt_mm, rt_out, r_mm, r_out = k.sem("m0_rt_mm"), k.sem("m0_rt_out"), k.sem("m0_r_mm"), k.sem("m0_r_out")
    top_ready, exp_ready = k.sem("m0_top_ready"), k.sem("m0_exp_ready")
    up_mm, act_done, hid_made = k.sem("m0_up_mm"), k.sem("m0_act_done"), k.sem("m0_hid_made")
    hid_cut, hid_rest = k.sem("m0_hid_cut"), k.sem("m0_hid_rest")
    raw_in, cut, cut_rest = [k.sem(f"m0_raw_in{i}") for i in range(2)], k.sem("m0_cut"), k.sem("m0_cut_rest")
    rows_cut, rows_rest = k.sem("m0_rows_cut"), k.sem("m0_rows_rest")
    down_mm, added = k.sem("m0_down_mm"), k.sem("m0_added")

    def piece(s):
        if s < 4:
            return raw[s % 2][:, 0:2 * SHARED], ups[0][:, s, :], ups[1][:, s, :]
        return raw[s % 2][:, :], downs[0][:, s - 4, :], downs[1][:, s - 4, :]

    def pieces_of(g):
        return range(PIECES * g // GROUPS, PIECES * (g + 1) // GROUPS)

    def up_weights(part, side, a_, c, size):
        first = (a_ % 2) * SHARED + c
        return ups[part][:, 2 * side + a_ // 2, first:first + size]

    def down_weights(part, m, size):
        return downs[part][0:size, m // 3, (m % 3) * D:(m % 3 + 1) * D]

    def groups(engine, group):
        with engine.Fori(1, GROUPS - 1) as g:
            group(g, False)
        group(GROUPS - 1, True)

    with k.nc.Block() as block:
        @block.sync
        def _(sp):
            def load(s):
                if s >= 2:
                    sp.wait_ge(cut_rest, s - 1)
                sp.dma_start(piece(s)[0], d["ws_up"][s, :, :] if s < 4 else d["ws_down"][s - 4, :, :])\
                    .then_inc(raw_in[s % 2], 16)

            sp.sem_inc(rows_out, FIRST)
            sp.dma_start(wg[:, :, :], row_chunks(d["wg"])).then_inc(weights_in, 16)
            load(0)
            load(1)
            for g in range(GROUPS):
                sp.wait_ge(a_ready, g + 1)
                sp.dma_start(r.rows[g * GN:(g + 1) * GN, :].rearrange("(j p) n -> p j n", p=P), a[:, :, :])\
                    .then_inc(rows_out, 16)
                load(2 + g)
            sp.wait_ge(rows_out, FIRST + 16 * GROUPS)

        @block.gpsimd
        def _(pool):
            for g in range(GROUPS):
                if g > 0:
                    norm_gpsimd(pool, k, norm, g - 1)
                for s in pieces_of(g):
                    came, part, rest = piece(s)
                    pool.wait_ge(cut, s + 1)
                    pool.tensor_tensor(rest, came, part, ALU.subtract).then_inc(cut_rest, 1)
            routing_constants(pool, r, w)
            routing_scatter(pool, r, w)

        @block.vector
        def _(v):
            v.sem_inc(hid_rest, FIRST)
            v.sem_inc(added, FIRST)
            steps = Steps(v, dve)
            v.sem_inc(a_ready, 1)
            with steps.loop(GROUPS - 1, 2 * GT) as i:
                wait_alone(v, t_ready, FIRST + (i + 1) * KC, norm.passed)
                wait_alone(v, rows_out, FIRST + 16 * (i + 1), norm.passed)
                norm_vector(v, steps, norm, i, lambda j: tile_of(h, i + 1, j), lambda j: a[:, j, :])\
                    .then_inc(a_ready, 1)
            def rest_of_rows(g):
                for half in range(2):
                    two = slice(2 * half, 2 * half + 2)
                    v.wait_ge(rows_cut, 2 * g + (half + 1))
                    v.tensor_tensor(rowsT[1][:, two, :], aT[:, two, bass.ds(g * GN, GN)], rowsT[0][:, two, :],
                                    ALU.subtract).then_inc(rows_rest, 1)

            def shared_up(g, m):
                size = mids[m][1]
                made = ps_a[m % 2][0:size, 0, :]
                v.wait_ge(act_done, g * nm + (m + 1))
                v.tensor_tensor(made, act_up[0:size, m % 2, :], ps_a[m % 2][0:size, 1, :], ALU.mult)\
                    .then_inc(hid_made, 1)
                v.wait_ge(hid_cut, g * nm + (m + 1))
                v.tensor_tensor(hidT[1][0:size, m, :], made, hidT[0][0:size, m, :], ALU.subtract)\
                    .then_inc(hid_rest, 1)

            def shared_down(g, last):
                if not last:
                    rest_of_rows(g + 1)
                for j in range(GT):
                    v.wait_ge(down_mm, g * GT + (j + 1))
                    t = tile_of(h, g, j)
                    v.tensor_tensor(t, ps_d[j % 2][:, :], t, ALU.add).then_inc(added, 1)

            rest_of_rows(0)
            v.wait_ge(r_out, FIRST + GROUPS)
            v.wait_ge(rows_out, FIRST + 16 * GROUPS)
            v.wait_ge(cut_rest, PIECES)
            steps.note(v.tensor_reduce(smax[:, :, 0], w.scores[:, :, :], AX.X, ALU.max))
            steps.settle()
            v.tensor_tensor(w.scores[:, :, :], w.scores[:, :, :], smax[:, :, :].to_broadcast([P, TILES, E0]),
                            ALU.subtract).then_inc(top_ready, 1)
            v.wait_ge(exp_ready, 1)
            steps.note(v.tensor_reduce(ssum[:, :, 0], w.scores[:, :, :], AX.X, ALU.add))
            steps.settle()
            steps.note(v.reciprocal(ssum[:, :, :], ssum[:, :, :]))
            steps.settle()
            steps.note(v.tensor_tensor(w.scores[:, :, :], w.scores[:, :, :],
                                       ssum[:, :, :].to_broadcast([P, TILES, E0]), ALU.mult))
            steps.note(v.memset(sets[:, :, SETS0:8], -1.0))
            steps.settle()
            steps.note(v.tensor_reduce(sets[:, :, 0:SETS0], w.scores[:, :, :].rearrange("p t (s e) -> p t s e", s=SETS0),
                                       AX.X, ALU.max))
            steps.settle()
            for t in range(TILES):
                steps.note(v.max(set_best[:, t, :], sets[:, t, :]))
            shared_up(0, 0)
            steps.settle()
            for t in range(TILES):
                steps.note(v.max_index(set_index[:, t, :], set_best[:, t, :], sets[:, t, :]))
            v.wait_ge(w.made, routing_made(w))
            steps.settle()
            steps.note(v.tensor_copy(set_indexf[:, :, :], set_index[:, :, :]))
            steps.settle()
            for c, o in ((0, open0), (1, open1)):
                steps.note(v.tensor_tensor(o[:, :, :], set_indexf[:, :, c:c + 1].to_broadcast([P, TILES, SETS0]),
                                           w.iota_e[:, :, 0:SETS0].to_broadcast([P, TILES, SETS0]), ALU.is_equal))
            steps.settle()
            steps.note(v.tensor_tensor(open0[:, :, :], open0[:, :, :], open1[:, :, :], ALU.add))
            steps.settle()
            steps.note(v.tensor_scalar(open0[:, :, :], open0[:, :, :], 2.0, -2.0, ALU.mult, ALU.add))
            steps.settle()
            shared_up(0, 1)
            each = E0 // SETS0
            steps.note(v.tensor_tensor(
                allowed[:, :, :].rearrange("p t (s e) -> p (t s) e", s=SETS0),
                w.scores[:, :, :].rearrange("p t (s e) -> p (t s) e", s=SETS0),
                open0[:, :, :].rearrange("p t (s e) -> p (t s) e", e=1).to_broadcast([P, TILES * SETS0, each]),
                ALU.add))
            steps.settle()
            for t in range(TILES):
                steps.note(v.max(r.best[:, t, :], allowed[:, t, :]))
            steps.settle()
            for t in range(TILES):
                steps.note(v.max_index(w.index[:, t, :], r.best[:, t, :], allowed[:, t, :]))
            shared_up(0, 2)
            steps.settle()
            routing_vector(v, steps, r, w)
            shared_up(0, 3)
            shared_up(0, 4)
            routing_slots(v, steps, r, w, ps_r[:, 0:TILES * E0], ps_q[:, 0:TILES * E0])
            shared_up(0, 5)
            shared_down(0, False)

            def shared_vector(g, last):
                for m in range(nm):
                    shared_up(g, m)
                shared_down(g, last)

            groups(v, shared_vector)
            v.wait_ge(w.map_in, 16)
            v.tensor_copy(w.mapf[:, :], w.map[:, :]).then_inc(w.map_ready, 1)
            v.wait_ge(w.map_turned, 1)
            v.tensor_copy(r.back[:, :], ps_r[:, 0:2 * r.blocks]).then_inc(w.token_ready, 1)
            v.wait_ge(w.token_ready, 1)
            steps.note(v.tensor_scalar(r.token[:, :], r.back[:, :], TOP0.bit_length() - 1, None,
                                       ALU.logical_shift_right))
            steps.settle()
            v.tensor_scalar(r.token[:, :], r.token[:, :], TOKENS - 1, None, ALU.min).then_inc(w.token_ready, 1)

        @block.scalar
        def _(act):
            act.sem_inc(aT_ready, FIRST)
            act.sem_inc(r_out, FIRST)

            def cut_rows(g):
                for half in range(2):
                    two = slice(2 * half, 2 * half + 2)
                    act.copy(rowsT[0][:, two, :], aT[:, two, bass.ds(g * GN, GN)]).then_inc(rows_cut, 1)

            for g in range(GROUPS):
                for half in range(2):
                    act.wait_ge(t_ready, FIRST + g * KC + (2 * half + 2))
                    act.copy(aT[:, 2 * half:2 * half + 2, g * GN:(g + 1) * GN], ps_a[half][:, :, :])\
                        .then_inc(aT_ready, 1)
                act.wait_ge(rt_mm, g + 1)
                act.copy(scoresT[:, :], ps_r[0:E0, :]).then_inc(rt_out, 1)
                act.wait_ge(r_mm, g + 1)
                act.copy(w.scores[:, g * GT:(g + 1) * GT, :],
                         ps_q[:, 0:GT * E0].rearrange("p (t e) -> p t e", t=GT)).then_inc(r_out, 1)
                if g == 0:
                    act.wait_ge(aT_ready, FIRST + 2)
                    cut_rows(0)
                for s in pieces_of(g):
                    came, part, rest = piece(s)
                    act.wait_ge(raw_in[s % 2], 16 * (s // 2 + 1))
                    act.copy(part, came).then_inc(cut, 1)

            def shared_scalar(g, last):
                for m, (c, size) in enumerate(mids):
                    act.wait_ge(up_mm, g * nm + (m + 1))
                    act.activation(act_up[0:size, m % 2, :], ps_a[m % 2][0:size, 0, :], ACT.Silu)\
                        .then_inc(act_done, 1)
                    act.wait_ge(hid_made, g * nm + (m + 1))
                    act.copy(hidT[0][0:size, m, :], ps_a[m % 2][0:size, 0, :]).then_inc(hid_cut, 1)
                if not last:
                    cut_rows(g + 1)

            act.wait_ge(top_ready, 1)
            act.activation(w.scores[:, :, :], w.scores[:, :, :], ACT.Exp).then_inc(exp_ready, 1)
            shared_scalar(0, False)
            groups(act, shared_scalar)

        @block.tensor
        def _(pe):
            pe.sem_inc(t_ready, FIRST)
            with pe.Fori(0, GROUPS) as g:
                pe.wait_ge(a_ready, g + 1)
                pe.wait_ge(aT_ready, FIRST + 2 * g)
                for c in range(KC):
                    for j in range(GT):
                        last = pe.transpose(ps_a[c // 2][:, c % 2, j * P:(j + 1) * P], a[:, j, c * P:(c + 1) * P],
                                            k.ident[:, :])
                    last.then_inc(t_ready, 1)
                wait_alone(pe, weights_in, 16, k.passed_pe)
                pe.wait_ge(aT_ready, FIRST + 2 * g + 2)
                for c in range(KC):
                    mm = pe.matmul(ps_r[0:E0, :], wg[:, c, :], aT[:, c, bass.ds(g * GN, GN)],
                                   start=(c == 0), stop=(c == KC - 1))
                mm.then_inc(rt_mm, 1)
                wait_alone(pe, rt_out, g + 1, k.passed_pe)
                wait_alone(pe, r_out, FIRST + g, k.passed_pe)
                for j in range(GT):
                    last = pe.transpose(ps_q[:, j * E0:(j + 1) * E0], scoresT[:, j * P:(j + 1) * P],
                                        k.ident[0:E0, 0:E0])
                last.then_inc(r_mm, 1)

            def shared(g, last):
                pe.wait_ge(rows_rest, 2 * g + 2)
                for m, (c, size) in enumerate(mids):
                    if isinstance(g, int) and g == 0 and m == nm - 1:
                        routing_tensor(pe, r, w, ps_r[:, 0:TILES * E0], ps_q[:, 0:TILES * E0])
                    wait_alone(pe, hid_rest, FIRST + g * nm + max(m - 1, 0), k.passed_pe)
                    for side in range(2):
                        for a_ in range(KC):
                            for p, (w_, t) in enumerate(PASSES):
                                mm = pe.matmul(ps_a[m % 2][0:size, side, :], up_weights(w_, side, a_, c, size),
                                               rowsT[t][:, a_, :], start=(a_ == 0 and p == 0),
                                               stop=(a_ == KC - 1 and p == len(PASSES) - 1))
                    mm.then_inc(up_mm, 1)
                for j in range(GT):
                    pe.wait_ge(added, FIRST + g * GT + max(j - 1, 0))
                    for m, (c, size) in enumerate(mids):
                        if j == 0:
                            pe.wait_ge(hid_rest, FIRST + g * nm + (m + 1))
                        for p, (t, w_) in enumerate(PASSES):
                            mm = pe.matmul(ps_d[j % 2][:, :], hidT[t][0:size, m, j * P:(j + 1) * P],
                                           down_weights(w_, m, size), start=(m == 0 and p == 0),
                                           stop=(m == nm - 1 and p == len(PASSES) - 1))
                    mm.then_inc(down_mm, 1)

            pe.wait_ge(aT_ready, FIRST + 2 * GROUPS)
            pe.wait_ge(r_out, FIRST + GROUPS)
            pe.wait_ge(cut_rest, PIECES)
            shared(0, False)
            groups(pe, shared)
            pe.wait_ge(w.map_ready, 1)
            pe.transpose(ps_r[:, 0:2 * r.blocks], w.mapf[:, :], k.ident[0:2 * r.blocks, 0:2 * r.blocks])\
                .then_inc(w.map_turned, 1)


def mixture_first_experts(k, d):
    experts(k, d, k.route0, MID0, True)


HEADS2, HC2 = 2, 2
ATT1_SCALE = (HC2 * P) ** -0.5


def attention_second(k, d):
    h = k.h
    cb = Combine(k, k.route0)
    raw = {n: k.sb(f"raw_{n}", [P, KC, D], BF16) for n in "qkvo"}
    wt = {n: k.sb(f"w2_{n}", [P, KC, D], F32R) for n in "qkvo"}
    bq16, bk16 = k.sb("bq16", [P, KC], BF16), k.sb("bk16", [P, KC], BF16)
    bv16, bo16 = k.sb("bv16", [P, D], BF16), k.sb("bo16", [P, D], BF16)
    bias_q, bias_k = k.sb("bias_q", [P, KC]), k.sb("bias_k", [P, KC])
    norm, ahead = Norm(k, "norm4"), Norm(k, "ahead_m1")
    a = k.a
    aT, aT_rest = k.sb("a2_aT", [P, KC, GN], F32R), k.sb("a2_aT_rest", [P, KC, GN], F32R)
    qT = k.sb("a2_qT", [P, KC, GN])
    kT = k.sb("a2_kT", [P, KC, GN])
    vals = k.sb("a2_vals", [P, GT, D])
    top = k.sb("a2_top", [P, 2, HEADS2, 1])
    prob = k.sb("a2_prob", [P, 2, HEADS2, P])
    probT = k.sb("a2_probT", [P, 2, HEADS2, P])
    rsum = k.sb("a2_rsum", [P, 2, HEADS2, 1])
    o = k.sb("a2_o", [P, 2, D])
    oT, oT_rest = k.sb("a2_oT", [P, 2, KC, P], F32R), k.sb("a2_oT_rest", [P, 2, KC, P], F32R)
    res = k.sb("a2_res", [P, 2, D])
    ps_a = [k.ps(f"a2_ps_a{i}", [P, GN]) for i in range(4)]
    ps_m = [k.ps(f"a2_ps_m{i}", [P, GN]) for i in range(4)]

    weights_in, cast = k.sem("a2_weights_in"), k.sem("a2_cast")
    dve = k.sem("a2_dve")
    a_ready, t_ready, aT_ready = k.sem("a2_a_ready"), k.sem("a2_t_ready"), k.sem("a2_aT_ready")
    qk_mm, qk_done = k.sem("a2_qk_mm"), k.sem("a2_qk_done")
    v_mm, v_added, v_done = k.sem("a2_v_mm"), k.sem("a2_v_added"), k.sem("a2_v_done")
    s_ready, shifted, exp_done = k.sem("a2_s_ready"), k.sem("a2_shifted"), k.sem("a2_exp_done")
    pt_ready, pt_done = k.sem("a2_pt_ready"), k.sem("a2_pt_done")
    pv_ready, o_done = k.sem("a2_pv_ready"), k.sem("a2_o_done")
    ot_ready, ot_done, ot_rest = k.sem("a2_ot_ready"), k.sem("a2_ot_done"), k.sem("a2_ot_rest")
    aT_rest_ready = k.sem("a2_aT_rest_ready")
    wo_ready, wo_read = k.sem("a2_wo_ready"), k.sem("a2_wo_read")
    QK = 2 * KC

    with k.nc.Block() as block:
        @block.sync
        def _(sp):
            combine_load(sp, cb, 0, (0, 1))
            for n in "qkvo":
                sp.dma_start(raw[n][:, :, :], row_chunks(d["w2" + n])).then_inc(weights_in, 16)
            combine_load(sp, cb, 0, (2, 3))
            for dst, src in ((bq16, d["b2q"]), (bk16, d["b2k"]), (bv16, d["b2v"].to_broadcast([P, D])),
                             (bo16, d["b2o"].to_broadcast([P, D]))):
                sp.dma_start(dst[:, :], src).then_inc(weights_in, 16)
            for g in range(1, GROUPS):
                combine_load(sp, cb, g)

        WEIGHTS = 16 * 8

        @block.gpsimd
        def _(pool):
            with pool.Fori(0, GROUPS) as g:
                norm_gpsimd(pool, k, norm, g)
            norm_gpsimd(pool, k, ahead, 0)

        @block.vector
        def _(v):
            v.sem_inc(o_done, FIRST)
            v.sem_inc(wo_read, FIRST)
            v.sem_inc(v_added, FIRST)
            v.sem_inc(shifted, FIRST)
            v.sem_inc(ot_rest, FIRST)
            steps = Steps(v, dve)

            def normalise(g, first):
                combine_vector(v, steps, cb, k, g, 0, g, norm.passed)
                if not first:
                    wait_alone(v, t_ready, g * KC, norm.passed)
                norm_vector(v, steps, norm, g, lambda j: tile_of(h, g, j), lambda j: a[:, j, :]).then_inc(a_ready, 1)

            def turn_rest(g):
                for c in range(KC):
                    v.wait_ge(aT_ready, g * KC + (c + 1))
                    v.tensor_tensor(aT_rest[:, c, :], ps_a[c][:, :], aT[:, c, :], ALU.subtract)\
                        .then_inc(aT_rest_ready, 1)

            def heads_rest(g, b):
                v.wait_ge(ot_done, FIRST + g * GT + (b + 1))
                v.tensor_tensor(oT_rest[:, b % 2, :, :], ps_m[1][:, :].rearrange("p (c n) -> p c n", c=KC),
                                oT[:, b % 2, :, :],
                                ALU.subtract).then_inc(ot_rest, 1)

            def shift(g, b):
                s = ps_a[b % 2][:, 0:HEADS2 * P].rearrange("p (h n) -> p h n", h=HEADS2)
                v.wait_ge(s_ready, g * GT + (b + 1))
                steps.note(v.tensor_reduce(top[:, b % 2, :, 0], s, AX.X, ALU.max))
                steps.settle()
                v.tensor_tensor(prob[:, b % 2, :, :], s, top[:, b % 2, :, :].to_broadcast([P, HEADS2, P]),
                                ALU.subtract).then_inc(shifted, 1)

            def weights_sum(g, b):
                v.wait_ge(exp_done, g * GT + (b + 1))
                steps.note(v.tensor_reduce(rsum[:, b % 2, :, 0], prob[:, b % 2, :, :], AX.X, ALU.add))
                steps.settle()
                steps.note(v.reciprocal(rsum[:, b % 2, :, :], rsum[:, b % 2, :, :]))
                steps.settle()

            def divide(g, b):
                v.wait_ge(pv_ready, g * GT + (b + 1))
                v.tensor_tensor(o[:, b % 2, :].rearrange("p (h n) -> p h n", h=HEADS2),
                                ps_m[0][:, :].rearrange("p (h n) -> p h n", h=HEADS2),
                                rsum[:, b % 2, :, :].to_broadcast([P, HEADS2, HC2 * P]), ALU.mult).then_inc(o_done, 1)

            def residual(g, b):
                v.wait_ge(wo_ready, g * GT + (b + 1))
                v.tensor_tensor(res[:, b % 2, :], ps_m[3][:, :], bo16[:, :], ALU.add).then_inc(wo_read, 1)
                v.wait_ge(wo_read, FIRST + g * GT + (b + 1))
                t = tile_of(h, g, b)
                steps.note(v.scalar_tensor_tensor(out=t, in0=res[:, b % 2, :], scalar=0.0, in1=t,
                                                  op0=ALU.max, op1=ALU.add))

            def group(g, last):
                if not last:
                    normalise(g + 1, False)
                else:
                    v.wait_ge(t_ready, GROUPS * KC)
                    steps.settle()
                    normalise_ahead(v, steps, ahead, k, h)
                for j in range(GT):
                    v.wait_ge(v_mm, g * GT + (j + 1))
                    v.tensor_tensor(vals[:, j, :], ps_m[j][:, :], bv16[:, :], ALU.add).then_inc(v_added, 1)
                shift(g, 0)
                shift(g, 1)
                for b in range(GT):
                    weights_sum(g, b)
                    if b + 2 < GT:
                        shift(g, b + 2)
                    if b >= 1:
                        heads_rest(g, b - 1)
                    divide(g, b)
                    if b >= 2:
                        residual(g, b - 2)
                heads_rest(g, GT - 1)
                residual(g, GT - 2)
                if not last:
                    turn_rest(g + 1)
                residual(g, GT - 1)

            normalise(0, True)
            v.wait_ge(weights_in, WEIGHTS)
            turn_rest(0)
            with steps.loop(GROUPS - 1, 6 * GT + cb.notes) as g:
                group(g, False)
            group(GROUPS - 1, True)

        @block.scalar
        def _(act):
            act.sem_inc(ot_done, FIRST)
            act.sem_inc(pt_done, FIRST)
            act.wait_ge(weights_in, WEIGHTS)
            for n in "qkvo":
                act.copy(wt[n][:, :, :], raw[n][:, :, :]).then_inc(cast, 1)
            act.copy(bias_q[:, :], bq16[:, :]).then_inc(cast, 1)
            act.copy(bias_k[:, :], bk16[:, :]).then_inc(cast, 1)
            act.wait_ge(cast, 6)

            def turn(g):
                for c in range(KC):
                    act.wait_ge(t_ready, g * KC + (c + 1))
                    act.copy(aT[:, c, :], ps_a[c][:, :]).then_inc(aT_ready, 1)

            def group(g, last):
                for c in range(QK):
                    act.wait_ge(qk_mm, g * QK + (c + 1))
                    out, bias = (qT, bias_q) if c < KC else (kT, bias_k)
                    act.activation(out[:, c % KC, :], ps_m[c % 4][:, :], ACT.Relu, bias=bias[:, c % KC:c % KC + 1])\
                        .then_inc(qk_done, 1)
                for j in range(GT):
                    act.wait_ge(v_added, FIRST + g * GT + (j + 1))
                    act.activation(vals[:, j, :], vals[:, j, :], ACT.Relu).then_inc(v_done, 1)

                def exponent(b):
                    act.wait_ge(shifted, FIRST + g * GT + (b + 1))
                    act.activation(prob[:, b % 2, :, :], prob[:, b % 2, :, :], ACT.Exp, scale=ATT1_SCALE)\
                        .then_inc(exp_done, 1)

                def turned_heads(b):
                    act.wait_ge(ot_ready, g * GT + (b + 1))
                    act.copy(oT[:, b % 2, :, :], ps_m[1][:, :].rearrange("p (c n) -> p c n", c=KC)).then_inc(ot_done, 1)

                exponent(0)
                exponent(1)
                for b in range(GT):
                    act.wait_ge(pt_ready, g * GT + (b + 1))
                    act.copy(probT[:, b % 2, :, :], ps_a[2 + b % 2][:, 0:HEADS2 * P]
                             .rearrange("p (h n) -> p h n", h=HEADS2)).then_inc(pt_done, 1)
                    if b >= 1:
                        turned_heads(b - 1)
                    if b + 2 < GT:
                        exponent(b + 2)
                turned_heads(GT - 1)
                if not last:
                    turn(g + 1)

            turn(0)
            with act.Fori(0, GROUPS - 1) as g:
                group(g, False)
            group(GROUPS - 1, True)

        @block.tensor
        def _(pe):
            def turn(g, first):
                pe.wait_ge(a_ready, g + 1)
                if not first:
                    pe.wait_ge(shifted, FIRST + g * GT)
                    pe.wait_ge(pt_done, FIRST + g * GT)
                for c in range(KC):
                    for j in range(GT):
                        last = pe.transpose(ps_a[c][:, j * P:(j + 1) * P], a[:, j, c * P:(c + 1) * P], k.ident[:, :])
                    last.then_inc(t_ready, 1)

            def project(g):
                pe.wait_ge(aT_rest_ready, (g + 1) * KC)
                pe.wait_ge(ot_rest, FIRST + g * GT)
                pe.wait_ge(o_done, FIRST + g * GT)
                pe.wait_ge(ot_done, FIRST + g * GT)
                pe.wait_ge(v_added, FIRST + g * GT)
                for c in range(QK):
                    if c == 3:
                        pe.wait_ge(wo_read, FIRST + g * GT)
                    if c >= 4:
                        pe.wait_ge(qk_done, g * QK + (c - 3))
                    w = wt["q"] if c < KC else wt["k"]
                    for i in range(KC):
                        for part in (aT, aT_rest):
                            mm = pe.matmul(ps_m[c % 4][:, :], w[:, i, (c % KC) * P:(c % KC + 1) * P], part[:, i, :],
                                           start=(i == 0 and part is aT), stop=(i == KC - 1 and part is aT_rest))
                    mm.then_inc(qk_mm, 1)
                for j in range(GT):
                    pe.wait_ge(qk_done, g * QK + (KC + 1 + j))
                    for i in range(KC):
                        for part in (aT, aT_rest):
                            mm = pe.matmul(ps_m[j][:, :], part[:, i, j * P:(j + 1) * P], wt["v"][:, i, :],
                                           start=(i == 0 and part is aT), stop=(i == KC - 1 and part is aT_rest))
                    mm.then_inc(v_mm, 1)

            def scores(g, b):
                if b >= 2:
                    pe.wait_ge(shifted, FIRST + g * GT + (b - 1))
                for hh in range(HEADS2):
                    for c in range(HC2):
                        mm = pe.matmul(ps_a[b % 2][:, hh * P:(hh + 1) * P], qT[:, HC2 * hh + c, b * P:(b + 1) * P],
                                       kT[:, HC2 * hh + c, b * P:(b + 1) * P], start=(c == 0), stop=(c == HC2 - 1))
                mm.then_inc(s_ready, 1)

            def turn_probs(g, b):
                pe.wait_ge(exp_done, g * GT + (b + 1))
                for hh in range(HEADS2):
                    last = pe.transpose(ps_a[2 + b % 2][:, hh * P:(hh + 1) * P], prob[:, b % 2, hh, :], k.ident[:, :])
                last.then_inc(pt_ready, 1)

            def turn_heads(g, b):
                pe.wait_ge(o_done, FIRST + g * GT + (b + 1))
                for c in range(KC):
                    last = pe.transpose(ps_m[1][:, c * P:(c + 1) * P], o[:, b % 2, c * P:(c + 1) * P], k.ident[:, :])
                last.then_inc(ot_ready, 1)

            def weigh(g, b):
                pe.wait_ge(pt_done, FIRST + g * GT + (b + 1))
                if b == 0:
                    pe.wait_ge(v_done, (g + 1) * GT)
                for hh in range(HEADS2):
                    mm = pe.matmul(ps_m[0][:, hh * HC2 * P:(hh + 1) * HC2 * P], probT[:, b % 2, hh, :],
                                   vals[:, b, hh * HC2 * P:(hh + 1) * HC2 * P], start=True, stop=True)
                mm.then_inc(pv_ready, 1)

            def output(g, b):
                pe.wait_ge(ot_rest, FIRST + g * GT + (b + 1))
                if b >= 1:
                    pe.wait_ge(wo_read, FIRST + g * GT + b)
                for part in (oT, oT_rest):
                    for c in range(KC):
                        mm = pe.matmul(ps_m[3][:, :], part[:, b % 2, c, :], wt["o"][:, c, :],
                                       start=(c == 0 and part is oT), stop=(c == KC - 1 and part is oT_rest))
                mm.then_inc(wo_ready, 1)

            def group(g, last):
                project(g)
                pe.wait_ge(qk_done, (g + 1) * QK)
                scores(g, 0)
                scores(g, 1)
                for b in range(GT):
                    turn_probs(g, b)
                    if b + 2 < GT:
                        scores(g, b + 2)
                    if b >= 1:
                        turn_heads(g, b - 1)
                    weigh(g, b)
                    if b >= 2:
                        output(g, b - 2)
                turn_heads(g, GT - 1)
                output(g, GT - 2)
                if not last:
                    turn(g + 1, False)
                output(g, GT - 1)

            turn(0, True)
            pe.wait_ge(cast, 6)
            with pe.Fori(0, GROUPS - 1) as g:
                group(g, False)
            group(GROUPS - 1, True)


def mixture_second_route(k, d):
    h, r = k.h, k.route1
    r.weight = k.route1_weight
    wg1 = k.sb("wg1", [P, KC, E1])
    wg2 = k.sb("wg2", [E1, E1])
    norm = Norm(k, "norm5")
    a = k.a
    aT = k.sb("m1_aT", [P, KC, GN])
    tanhT = k.sb("m1_tanhT", [E1, GN])
    w = RoutingWork(k, r, False)
    gap = k.sb("m1_gap", [P, TILES, 1])
    ps_a = [k.ps(f"m1_ps_a{i}", [P, GN]) for i in range(4)]
    ps_r = k.ps("m1_ps_r", [P, GN])
    ps_q = k.ps("m1_ps_q", [P, GN])
    weights_in, dve = k.sem("m1_weights_in"), k.sem("m1_dve")
    a_ready, rows_out = k.sem("m1_a_ready"), k.sem("m1_rows_out")
    t_ready, aT_ready = k.sem("m1_t_ready"), k.sem("m1_aT_ready")
    rt_mm, rt_out, r_mm, r_out = k.sem("m1_rt_mm"), k.sem("m1_rt_out"), k.sem("m1_r_mm"), k.sem("m1_r_out")
    gap_ready, exp_ready = k.sem("m1_gap_ready"), k.sem("m1_exp_ready")

    with k.nc.Block() as block:
        @block.sync
        def _(sp):
            sp.sem_inc(rows_out, FIRST)
            sp.dma_start(wg1[:, :, :], row_chunks(d["wg1"])).then_inc(weights_in, 16)
            sp.dma_start(wg2[:, :], d["wg2"]).then_inc(weights_in, 16)
            with sp.Fori(0, GROUPS) as g:
                sp.wait_ge(a_ready, g + 1)
                sp.dma_start(r.rows[bass.ds(g * GN, GN), :].rearrange("(j p) n -> p j n", p=P), a[:, :, :])\
                    .then_inc(rows_out, 16)
            sp.wait_ge(rows_out, FIRST + 16 * GROUPS)

        @block.gpsimd
        def _(pool):
            with pool.Fori(0, GROUPS - 1) as i:
                norm_gpsimd(pool, k, norm, i)
            routing_constants(pool, r, w)

        @block.vector
        def _(v):
            steps = Steps(v, dve)
            v.sem_inc(a_ready, 1)
            with steps.loop(GROUPS - 1, 2 * GT) as i:
                wait_alone(v, t_ready, FIRST + (i + 1) * KC, norm.passed)
                wait_alone(v, rows_out, FIRST + 16 * (i + 1), norm.passed)
                norm_vector(v, steps, norm, i, lambda j: tile_of(h, i + 1, j), lambda j: a[:, j, :])\
                    .then_inc(a_ready, 1)
            v.wait_ge(r_out, FIRST + GROUPS)
            for t in range(TILES):
                steps.note(v.max(r.best[:, t, :], w.scores[:, t, :]))
            steps.settle()
            for t in range(TILES):
                steps.note(v.max_index(w.index[:, t, :], r.best[:, t, :], w.scores[:, t, :]))
            v.tensor_tensor(gap[:, :, :], r.best[:, :, 1:2], r.best[:, :, 0:1], ALU.subtract).then_inc(gap_ready, 1)
            v.wait_ge(w.made, routing_made(w))
            steps.settle()
            routing_vector(v, steps, r, w)
            v.wait_ge(exp_ready, 1)
            steps.note(v.tensor_scalar(r.weight[:, :, 1:2], gap[:, :, :], 1.0, None, ALU.add))
            steps.settle()
            steps.note(v.reciprocal(r.weight[:, :, 0:1], r.weight[:, :, 1:2]))
            steps.settle()
            steps.note(v.tensor_tensor(r.weight[:, :, 1:2], gap[:, :, :], r.weight[:, :, 0:1], ALU.mult))
            routing_slots(v, steps, r, w, ps_r[:, 0:TILES * E1], ps_q[:, 0:TILES * E1])
            routing_map_vector(v, steps, r, w, ps_r[:, 0:6 * r.blocks])

        @block.scalar
        def _(act):
            act.sem_inc(aT_ready, FIRST)
            act.sem_inc(r_out, FIRST)
            with act.Fori(0, GROUPS) as g:
                for c in range(KC):
                    act.wait_ge(t_ready, FIRST + g * KC + (c + 1))
                    act.copy(aT[:, c, :], ps_a[c][:, :]).then_inc(aT_ready, 1)
                act.wait_ge(rt_mm, g + 1)
                act.activation(tanhT[:, :], ps_r[0:E1, :], ACT.Tanh).then_inc(rt_out, 1)
                act.wait_ge(r_mm, g + 1)
                act.copy(w.scores[:, bass.ds(g * GT, GT), :],
                         ps_q[:, 0:GT * E1].rearrange("p (t e) -> p t e", t=GT)).then_inc(r_out, 1)
            act.wait_ge(gap_ready, 1)
            act.activation(gap[:, :, :], gap[:, :, :], ACT.Exp).then_inc(exp_ready, 1)

        @block.tensor
        def _(pe):
            pe.sem_inc(t_ready, FIRST)
            with pe.Fori(0, GROUPS) as g:
                pe.wait_ge(a_ready, g + 1)
                pe.wait_ge(aT_ready, FIRST + g * KC)
                for c in range(KC):
                    for j in range(GT):
                        last = pe.transpose(ps_a[c][:, j * P:(j + 1) * P], a[:, j, c * P:(c + 1) * P], k.ident[:, :])
                    last.then_inc(t_ready, 1)
                wait_alone(pe, weights_in, 32, k.passed_pe)
                wait_alone(pe, aT_ready, FIRST + (g + 1) * KC, k.passed_pe)
                for c in range(KC):
                    mm = pe.matmul(ps_r[0:E1, :], wg1[:, c, :], aT[:, c, :], start=(c == 0), stop=(c == KC - 1))
                mm.then_inc(rt_mm, 1)
                wait_alone(pe, rt_out, g + 1, k.passed_pe)
                wait_alone(pe, r_out, FIRST + g, k.passed_pe)
                for j in range(GT):
                    mm = pe.matmul(ps_q[:, j * E1:(j + 1) * E1], tanhT[:, j * P:(j + 1) * P], wg2[:, :],
                                   start=True, stop=True)
                mm.then_inc(r_mm, 1)
            pe.wait_ge(r_out, FIRST + GROUPS)
            routing_tensor(pe, r, w, ps_r[:, 0:TILES * E1], ps_q[:, 0:TILES * E1])
            routing_map_tensor(pe, r, w, ps_r[:, 0:6 * r.blocks])


def mixture_second_experts(k, d):
    experts(k, d, k.route1, MID1, False)


def mixture_second_combine(k, d):
    cb = Combine(k, k.route1)
    own, passed, out_sent = k.sem("m1_combine_dve"), k.sem("m1_combine_passed"), k.sem("out_sent")
    with k.nc.Block() as block:
        @block.sync
        def _(sp):
            for g in range(GROUPS):
                combine_load(sp, cb, g)

        @block.scalar
        def _(act):
            for g in range(GROUPS):
                act.wait_ge(cb.added, (g + 1) * GT)
                tiles = slice(g * GT, (g + 1) * GT)
                act.dma_start(d["out"][tiles, :, :].rearrange("t p n -> p t n"), k.h[:, tiles, :])\
                    .then_inc(out_sent, 16)
            act.wait_ge(out_sent, 16 * GROUPS)

        @block.vector
        def _(v):
            steps = Steps(v, own)
            for g in range(GROUPS):
                combine_vector(v, steps, cb, k, g, g % cb.deep, g // cb.deep, passed)




def program(nc, d):
    with ExitStack() as whole:
        k = Core(nc, whole)
        k.h = k.sb("h", [P, TILES, D])
        k.x = k.sb("x", [P, TILES, D])
        k.a = k.sb("a", [P, GT, D])
        k.passed_pool, k.passed_pe = k.sem("passed_pool"), k.sem("passed_pe")
        constants(k)
        k.route0 = Routing(k, "m0", E0, TOP0)
        k.route1 = Routing(k, "m1", E1, TOP1)
        k.route1_weight = k.sb("m1_weight", [P, TILES, TOP1])
        for stage in STAGES:
            with k.stage():
                stage(k, d)


STAGES = [attention_first, feed_forward, mixture_first_route, mixture_first_experts,
          attention_second, mixture_second_route, mixture_second_experts, mixture_second_combine]


def columns(a):
    import numpy as np
    return np.ascontiguousarray(np.reshape(a, (-1, P)).T)


def layouts(inputs):
    import numpy as np
    i = {n: np.asarray(a) for n, a in inputs.items()}
    wkv, bkv = i["L0_attn_wkv"], i["L0_attn_bkv"]
    a = {
        "ids": columns(i["x"].reshape(-1)), "tok": i["L0_tok_weight"], "extra": i["L0_tok_extra"],
        "wq": i["L0_attn_wq"], "wk4": np.tile(wkv[:, :HD], (1, QUADS)), "wv4": np.tile(wkv[:, HD:], (1, QUADS)),
        "wo": i["L0_attn_wo"],
        "ln1_g": columns(i["L0_attn_ln1_g"]), "ln1_b": columns(i["L0_attn_ln1_b"]),
        "ln2_g": columns(i["L0_attn_ln2_g"]), "ln2_b": columns(i["L0_attn_ln2_b"]),
        "bq": columns(i["L0_attn_bq"]), "bk4": np.tile(bkv[:HD], QUADS).reshape(P, 1),
        "bv": np.tile(bkv[HD:], QUADS).reshape(1, -1), "bo": i["L0_attn_bo"].reshape(1, D),
        "ff": np.concatenate([i["L0_attn_wfc"].reshape(KC, P, SLICES, SC * P).transpose(2, 1, 0, 3)
                              .reshape(SLICES, P, -1),
                              i["L0_attn_wproj"].reshape(SLICES, SC, P, D).transpose(0, 2, 1, 3)
                              .reshape(SLICES, P, -1)], 2),
        "bfc": columns(i["L0_attn_bfc"]),
        "bproj": i["L0_attn_bproj"].reshape(1, D),
    }
    def ups(w):
        e, m, _ = w.shape
        return w.transpose(0, 2, 1).reshape(e, KC, P, m).transpose(0, 2, 1, 3)

    def downs(w):
        e, o, m = w.shape
        pad = -m % P
        w = np.concatenate([w.transpose(0, 2, 1), np.zeros((e, pad, o), w.dtype)], 1)
        return w.reshape(e, -1, P, o).transpose(0, 2, 1, 3).reshape(e, P, -1)

    a |= {
        "wg": i["L0_ffn_Wg"].T,
        "ws_up": np.stack([i["L0_ffn_Ws1"].T, i["L0_ffn_Ws3"].T]).reshape(4, 2, P, SHARED).transpose(0, 2, 1, 3)
        .reshape(4, P, -1),
        "ws_down": downs(i["L0_ffn_Ws2"][None]).reshape(P, 2, -1).transpose(1, 0, 2),
        "m0_up": np.concatenate([ups(i["L0_ffn_W1"]), ups(i["L0_ffn_W3"])], 3).reshape(E0, P, -1),
        "m0_down": downs(i["L0_ffn_W2"]),
    }
    for n in "qkvo":
        a["w2" + n] = i["L1_attn_W" + n].T
    a |= {
        "b2q": columns(i["L1_attn_bq"]), "b2k": columns(i["L1_attn_bk"]),
        "b2v": i["L1_attn_bv"].reshape(1, D), "b2o": i["L1_attn_bo"].reshape(1, D),
        "wg1": i["L1_ffn_Wg1"].T, "wg2": i["L1_ffn_Wg2"].T,
        "m1_up": ups(i["L1_ffn_Wup"]).reshape(E1, P, -1), "m1_down": downs(i["L1_ffn_Wdown"]),
        "m1_up_bias": i["L1_ffn_bup"].reshape(E1, -1, P).transpose(0, 2, 1), "m1_down_bias": i["L1_ffn_bdown"],
    }
    return {n: np.ascontiguousarray(b) for n, b in a.items()}


def kernel(**inputs):
    import concourse.bacc as bacc
    from concourse.bass_utils import run_bass_kernel_spmd

    nc = bacc.Bacc("TRN2", target_bir_lowering=False, num_devices=1)
    arrays = layouts(inputs)
    d = {n: nc.dram_tensor("in_" + n, a.shape, mybir.dt.from_np(a.dtype), kind="ExternalInput").ap()
         for n, a in arrays.items()}
    d["out"] = nc.dram_tensor("out", (TILES, P, D), F32, kind="ExternalOutput").ap()
    program(nc, d)
    result = run_bass_kernel_spmd(nc, [{"in_" + n: a for n, a in arrays.items()}], core_ids=[0])
    return result.results[0]["out"]
```
